# Optimizing a Trainium2 kernel written in Bass

```python
import numpy as np
import jax
import jax.numpy as jnp

def _softmax(x, axis=-1):
    return jax.nn.softmax(x, axis=axis)

def _gelu(x):
    return jax.nn.gelu(x, approximate=True)

def _silu(x):
    return jax.nn.silu(x)

def _sigmoid(x):
    return jax.nn.sigmoid(x)

def _layernorm(x, axis=-1, eps=1e-05):
    m = jnp.mean(x, axis=axis, keepdims=True)
    v = jnp.var(x, axis=axis, keepdims=True)
    return (x - m) / jnp.sqrt(v + eps)

def _scatter_add(tgt, idx, src, axis=0):
    return tgt.at[idx].add(src)

def _segment_sum(src, seg, n):
    return jax.ops.segment_sum(src, seg, n)
kernel_name = 'mk_gnn_resnorm_d2_gnn_r8_eb3721'

def setup_inputs(seed: int=0):
    np.random.seed(seed)
    _w = jnp.asarray

    def _rec_inputs():
        import jax
        import jax.numpy as jnp
        _gk = jax.random.key(seed)
        x = -0.0005889 + 1 * jax.random.normal(jax.random.fold_in(_gk, 1), (12500, 128), jnp.float32)
        src = jax.random.randint(jax.random.fold_in(_gk, 2), (200000,), 0, 12500, jnp.int32)
        dst = jnp.minimum((12500 * jax.random.uniform(jax.random.fold_in(_gk, 3), (200000,)) ** 2.0).astype(jnp.int32), 99999)
        _o = jnp.argsort(dst, stable=True)
        src = src[_o]
        dst = dst[_o]
        edge_attr_64 = -6.8511e-05 + 1.00004 * jax.random.normal(jax.random.fold_in(_gk, 12), (200000, 64), jnp.float32)
        edge_weight1 = 0.000452788 + 0.999756 * jax.random.normal(jax.random.fold_in(_gk, 14), (200000, 1), jnp.float32)
        return (x, src, dst, edge_attr_64, edge_weight1)
    x, src, dst, edge_attr_64, edge_weight1 = _rec_inputs()

    def _L0_gnn_setup():
        import jax, jax.numpy as jnp
        import numpy as np
        N, E = (6250, 200000)
        F_X, F_E, F_U, H = (128, 64, 32, 128)
        B = 8
        key = jax.random.key(seed)
        ks = jax.random.split(key, 16)

        def lin(k, fan_in, fan_out):
            k1, k2 = jax.random.split(k)
            bound = 1.0 / np.sqrt(fan_in)
            W = jax.random.uniform(k1, (fan_in, fan_out), minval=-bound, maxval=bound, dtype=jnp.float32)
            b = jax.random.uniform(k2, (fan_out,), minval=-bound, maxval=bound, dtype=jnp.float32)
            return (W, b)
        W1a, b1a = lin(ks[0], F_X + F_E, H)
        W1b, b1b = lin(ks[1], H, H)
        W2a, b2a = lin(ks[2], H + F_X, H)
        W2b, b2b = lin(ks[3], H, F_X)
        return {'x': jax.random.normal(ks[4], (N, F_X), dtype=jnp.float32), 'edge_index': jax.random.randint(ks[5], (2, E), 0, N, dtype=jnp.int64), 'edge_attr': jax.random.normal(ks[6], (E, F_E), dtype=jnp.float32), 'u': jax.random.normal(ks[7], (B, F_U), dtype=jnp.float32), 'batch': jax.random.randint(ks[8], (N,), 0, B, dtype=jnp.int64), 'W1a': W1a, 'b1a': b1a, 'W1b': W1b, 'b1b': b1b, 'W2a': W2a, 'b2a': b2a, 'W2b': W2b, 'b2b': b2b}
    _L0_gnn_all = _L0_gnn_setup()
    _L0_gnn_in = {k: v for k, v in _L0_gnn_all.items() if k in ('u', 'W1a', 'b1a', 'W1b', 'b1b', 'W2a', 'b2a', 'W2b', 'b2b')}
    del _L0_gnn_all

    def _L1_gnn_setup():
        import jax, jax.numpy as jnp
        import numpy as np
        N, E, IN_C, HID, OUT_C, L = (12500, 200000, 128, 128, 128, 3)
        BN_EPS = 1e-05
        key = jax.random.key(seed)
        ks = jax.random.split(key, 16)
        inp = {'x': jax.random.normal(ks[0], (N, IN_C), dtype=jnp.float32), 'edge_index': jax.random.randint(ks[1], (2, E), 0, N, dtype=jnp.int64), 'edge_attr': jax.random.normal(ks[2], (E, 1), dtype=jnp.float32), 'lin0_w': jax.random.normal(ks[3], (IN_C, HID), dtype=jnp.float32) / np.sqrt(IN_C), 'lin0_b': jnp.zeros((HID,), dtype=jnp.float32), 'lin1_w': jax.random.normal(ks[4], (HID, OUT_C), dtype=jnp.float32) / np.sqrt(HID), 'lin1_b': jnp.zeros((OUT_C,), dtype=jnp.float32), 'conv_w': jax.random.normal(ks[5], (L, HID, HID), dtype=jnp.float32) / np.sqrt(HID), 'conv_b': jnp.zeros((L, HID), dtype=jnp.float32), 'bn_gamma': jnp.ones((L, HID), dtype=jnp.float32), 'bn_beta': jnp.zeros((L, HID), dtype=jnp.float32), 'bn_mean': 0.1 * jax.random.normal(ks[6], (L, HID), dtype=jnp.float32), 'bn_var': jax.random.uniform(ks[7], (L, HID), minval=0.5, maxval=1.5, dtype=jnp.float32)}
        return inp
    _L1_gnn_all = _L1_gnn_setup()
    _L1_gnn_in = {k: v for k, v in _L1_gnn_all.items() if k in ('lin0_w', 'lin0_b', 'lin1_w', 'lin1_b', 'conv_w', 'conv_b', 'bn_gamma', 'bn_beta', 'bn_mean', 'bn_var')}
    del _L1_gnn_all
    return {'x': x, 'src': src, 'dst': dst, 'edge_attr_64': edge_attr_64, 'edge_weight1': edge_weight1, 'L0_gnn_u': _L0_gnn_in['u'], 'L0_gnn_W1a': _L0_gnn_in['W1a'], 'L0_gnn_b1a': _L0_gnn_in['b1a'], 'L0_gnn_W1b': _L0_gnn_in['W1b'], 'L0_gnn_b1b': _L0_gnn_in['b1b'], 'L0_gnn_W2a': _L0_gnn_in['W2a'], 'L0_gnn_b2a': _L0_gnn_in['b2a'], 'L0_gnn_W2b': _L0_gnn_in['W2b'], 'L0_gnn_b2b': _L0_gnn_in['b2b'], 'L1_gnn_lin0_w': _L1_gnn_in['lin0_w'], 'L1_gnn_lin0_b': _L1_gnn_in['lin0_b'], 'L1_gnn_lin1_w': _L1_gnn_in['lin1_w'], 'L1_gnn_lin1_b': _L1_gnn_in['lin1_b'], 'L1_gnn_conv_w': _L1_gnn_in['conv_w'], 'L1_gnn_conv_b': _L1_gnn_in['conv_b'], 'L1_gnn_bn_gamma': _L1_gnn_in['bn_gamma'], 'L1_gnn_bn_beta': _L1_gnn_in['bn_beta'], 'L1_gnn_bn_mean': _L1_gnn_in['bn_mean'], 'L1_gnn_bn_var': _L1_gnn_in['bn_var']}

def reference(x, src, dst, edge_attr_64, edge_weight1, L0_gnn_u, L0_gnn_W1a, L0_gnn_b1a, L0_gnn_W1b, L0_gnn_b1b, L0_gnn_W2a, L0_gnn_b2a, L0_gnn_W2b, L0_gnn_b2b, L1_gnn_lin0_w, L1_gnn_lin0_b, L1_gnn_lin1_w, L1_gnn_lin1_b, L1_gnn_conv_w, L1_gnn_conv_b, L1_gnn_bn_gamma, L1_gnn_bn_beta, L1_gnn_bn_mean, L1_gnn_bn_var):
    import jax
    import jax.numpy as jnp

    def _L0_gnn_ref(x, edge_index, edge_attr, u, batch, W1a, b1a, W1b, b1b, W2a, b2a, W2b, b2b):
        import jax, jax.numpy as jnp
        import numpy as np
        N, E = (6250, 200000)
        F_X, F_E, F_U, H = (128, 64, 32, 128)
        B = 8
        row, col = (edge_index[0], edge_index[1])
        h = jnp.concatenate([x[col], edge_attr], axis=1)
        h = jax.nn.relu(h @ W1a + b1a) @ W1b + b1b
        sums = jax.ops.segment_sum(h, row, num_segments=x.shape[0])
        cnt = jax.ops.segment_sum(jnp.ones((h.shape[0],), dtype=h.dtype), row, num_segments=x.shape[0])
        agg = sums / jnp.maximum(cnt, 1.0)[:, None]
        z = jnp.concatenate([x, agg], axis=1)
        return jax.nn.relu(z @ W2a + b2a) @ W2b + b2b

    def _L1_gnn_ref(x, edge_index, edge_attr, lin0_w, lin0_b, lin1_w, lin1_b, conv_w, conv_b, bn_gamma, bn_beta, bn_mean, bn_var):
        import jax, jax.numpy as jnp
        import numpy as np
        N, E, IN_C, HID, OUT_C, L = (12500, 200000, 128, 128, 128, 3)
        BN_EPS = 1e-05
        n = x.shape[0]
        loops = jnp.arange(n, dtype=edge_index.dtype)
        src = jnp.concatenate([edge_index[0], loops])
        dst = jnp.concatenate([edge_index[1], loops])
        deg = jax.ops.segment_sum(jnp.ones_like(src, dtype=x.dtype), dst, num_segments=n)
        dinv = jnp.where(deg > 0, deg ** (-0.5), 0.0)
        norm = dinv[src] * dinv[dst]
        h = jax.nn.relu(x @ lin0_w + lin0_b)
        for l in range(L):
            hw = h @ conv_w[l]
            msg = hw[src] * norm[:, None]
            agg = jax.ops.segment_sum(msg, dst, num_segments=n) + conv_b[l]
            h = (agg - bn_mean[l]) * jax.lax.rsqrt(bn_var[l] + BN_EPS) * bn_gamma[l] + bn_beta[l]
            h = jax.nn.relu(h)
        out = h @ lin1_w + lin1_b
        return out
    edge_index = jnp.stack([src, dst])
    batch0 = jnp.zeros((12500,), jnp.int32)
    x = _layernorm(x + _L0_gnn_ref(x, edge_index, edge_attr_64, L0_gnn_u, batch0, L0_gnn_W1a, L0_gnn_b1a, L0_gnn_W1b, L0_gnn_b1b, L0_gnn_W2a, L0_gnn_b2a, L0_gnn_W2b, L0_gnn_b2b), axis=-1)
    x = _layernorm(x + _L1_gnn_ref(x, edge_index, edge_weight1, L1_gnn_lin0_w, L1_gnn_lin0_b, L1_gnn_lin1_w, L1_gnn_lin1_b, L1_gnn_conv_w, L1_gnn_conv_b, L1_gnn_bn_gamma, L1_gnn_bn_beta, L1_gnn_bn_mean, L1_gnn_bn_var), axis=-1)
    return x

_drawn_inputs = setup_inputs


def setup_inputs(seed=0):
    import zlib

    import numpy as np

    out = dict(_drawn_inputs(seed))
    spreads = {'L1_gnn_lin0_b': (0.0, 0.328),
     'L1_gnn_lin1_b': (0.0, 0.1),
     'L1_gnn_conv_b': (0.0, 0.1),
     'L1_gnn_bn_gamma': (1.0, 0.2),
     'L1_gnn_bn_beta': (0.0, 0.1)}
    factors = {'edge_attr_64': 8.0,
     'L0_gnn_W1a': 7.101,
     'L0_gnn_b1a': 45.145,
     'L0_gnn_b1b': 7.397,
     'L0_gnn_b2a': 3.922}
    for name, (base, spread) in spreads.items():
        noise = np.random.default_rng([zlib.crc32(name.encode()), seed]).standard_normal(out[name].shape)
        drawn = base * np.exp(spread * noise) if base else spread * noise
        out[name] = jnp.asarray(drawn.astype(out[name].dtype))
    for name, factor in factors.items():
        out[name] = (out[name] * factor).astype(out[name].dtype)
    return out
```

```python
from contextlib import ExitStack

import numpy as np

import concourse.bass as bass
from concourse import mybir

ALU = mybir.AluOpType
ACT = mybir.ActivationFunctionType
AXX = mybir.AxisListType.X
F32 = mybir.dt.float32
I32 = mybir.dt.int32

P = 128
FEATURES = 128
EDGE_FEATURES = 64
TILES = 8
EDGES = TILES * P
HALF = TILES // 2
CHUNK = 512
QUARTERS = CHUNK // P
WINDOW = 2 * P
TABLES = 4
LATER = 1024.0
EPS = 1e-5
LAYERS = 3
RING = 4


def sizes(nodes, edges):
    chunks = -(-(nodes + 1 + WINDOW) // CHUNK)
    supers = -(-edges // EDGES)
    return (chunks + chunks % 2) * CHUNK, supers + -supers % RING


def build(nc, nodes, edges, ins, out):
    NP, SUPERS = sizes(nodes, edges)
    NCHUNK = NP // CHUNK
    ROWW = FEATURES + 1
    TROWS = NP + P
    p_table = nc.dram_tensor("p_table", [NP, FEATURES], F32, kind="Internal").ap()
    g_table = nc.dram_tensor("g_table", [NP, FEATURES], F32, kind="Internal").ap()
    x1_rows = nc.dram_tensor("x1_rows", [NP, FEATURES], F32, kind="Internal").ap()
    sums = [nc.dram_tensor(f"sums{k}", [TROWS, ROWW], F32, kind="Internal").ap() for k in range(TABLES)]

    whole = ExitStack()
    with whole:
        def sb(name, shape, dt=F32, ctx=whole):
            return ctx.enter_context(nc.sbuf_tensor(name, shape, dt))

        acc = sb("acc", [P, NP])
        dinv = sb("dinv", [P, NP])
        ident = sb("ident", [P, P])
        ones = sb("ones", [P, P])
        later = sb("later", [P, P])
        iota_w = sb("iota_w", [P, WINDOW])
        part2 = sb("part2", [P, 2])
        spare = sb("spare", [P, 1])
        eps = sb("eps", [P, 1])
        w1x = sb("w1x", [P, FEATURES])
        w1e = sb("w1e", [EDGE_FEATURES, FEATURES])
        w1b = sb("w1b", [P, FEATURES])
        w2x = sb("w2x", [P, FEATURES])
        w2g = sb("w2g", [P, FEATURES])
        w2b = sb("w2b", [P, FEATURES])
        lin0 = sb("lin0", [P, FEATURES])
        lin1 = sb("lin1", [P, FEATURES])
        conv = sb("conv", [P, LAYERS, FEATURES])
        b1a_r = sb("b1a_r", [P, FEATURES])
        b1b_r = sb("b1b_r", [P, FEATURES])
        b2b_r = sb("b2b_r", [P, FEATURES])
        lin1b_r = sb("lin1b_r", [P, FEATURES])
        cols = sb("cols", [P, 2 + 5 * LAYERS])
        bn_s = sb("bn_s", [P, LAYERS])
        bn_b = sb("bn_b", [P, LAYERS])
        bn_t = sb("bn_t", [P, LAYERS])
        bn_d = sb("bn_d", [P, LAYERS])
        first_i = sb("first_i", [1, SUPERS], I32)
        first = sb("first", [P, SUPERS], I32)
        starts = sb("starts", [P, NP // WINDOW])
        wide = sb("wide", [P, 1], I32)

        setup(nc, locals(), ins, p_table, sums, NP, NCHUNK, TROWS)
        find_wide(nc, locals(), ins, SUPERS)
        message_pass(nc, locals(), ins, p_table, sums, SUPERS)
        degree_roots(nc, dinv)
        update_nodes(nc, locals(), ins, sums, x1_rows, g_table, NCHUNK)
        sem = lambda name: whole.enter_context(nc.semaphore(name))
        convolve_sems, project_sems = convolve_semaphores(sem), project_semaphores(sem)
        for layer in range(LAYERS):
            convolve(nc, locals(), ins, g_table, SUPERS, layer, convolve_sems)
            if layer + 1 < LAYERS:
                project(nc, locals(), g_table, NCHUNK, layer, project_sems)
        finish(nc, locals(), x1_rows, out, nodes, NCHUNK)


def setup(nc, t, ins, p_table, sums, NP, NCHUNK, TROWS):
    acc, dinv, ident, ones, later = t["acc"], t["dinv"], t["ident"], t["ones"], t["later"]
    w1x, b1a_r = t["w1x"], t["b1a_r"]
    rows = [(t["b1b_r"], "b1b"), (t["b2b_r"], "b2b"), (t["lin1b_r"], "lin1_b")]
    squares = [(t["w1e"], ins["W1a"][FEATURES:, :]), (t["w1b"], ins["W1b"]),
               (t["w2x"], ins["W2a"][0:FEATURES, :]), (t["w2g"], ins["W2a"][FEATURES:, :]),
               (t["w2b"], ins["W2b"]), (t["lin0"], ins["lin0_w"]), (t["lin1"], ins["lin1_w"])]
    flat = TROWS * (FEATURES + 1) // P
    with ExitStack() as ctx:
        xc = ctx.enter_context(nc.sbuf_tensor("xc", [P, 2, CHUNK], F32))
        pr = ctx.enter_context(nc.sbuf_tensor("pr", [P, 2, QUARTERS, FEATURES], F32))
        ps = [ctx.enter_context(nc.psum_tensor(f"ps{b}", [P, QUARTERS, FEATURES], F32)) for b in range(2)]
        sem = lambda name: ctx.enter_context(nc.semaphore(name))
        weights_in, rest_in = sem("weights_in"), sem("rest_in")
        x_in = [sem(f"x_in{b}") for b in range(2)]
        stored = [sem(f"p_stored{b}") for b in range(2)]
        zeroed, cleared = sem("zeroed"), sem("cleared")
        made, multiplied, biased = sem("made"), sem("multiplied"), sem("biased")
        bn = sem("bn")
        block = ctx.enter_context(nc.Block())

        @block.sync
        def _(sp):
            sp.dma_start(w1x[:, :], ins["W1a"][0:FEATURES, :]).then_inc(weights_in, 16)
            sp.dma_start(b1a_r[:, :], ins["b1a"].rearrange("(a n) -> a n", a=1).to_broadcast([P, FEATURES])).then_inc(weights_in, 16)
            sp.sem_inc(stored[0], 16)
            sp.sem_inc(stored[1], 16)
            with sp.Fori(0, NCHUNK // 2) as i:
                for b in range(2):
                    c = i * 2 + b
                    sp.wait_ge(multiplied, c + 1)
                    sp.dma_start(xc[:, b, :], ins["xT"][:, bass.ds(c * CHUNK, CHUNK)]).then_inc(x_in[b], 16)
            for tile, source in squares:
                sp.dma_start(tile[:, :], source).then_inc(rest_in, 16)
            for tile, name in rows:
                sp.dma_start(tile[:, :], ins[name].rearrange("(a n) -> a n", a=1).to_broadcast([P, FEATURES])).then_inc(rest_in, 16)
            sp.dma_start(t["conv"][:, :, :], ins["conv_w"].rearrange("l k n -> k l n")).then_inc(rest_in, 16)
            sp.dma_start(t["cols"][:, :], ins["cols"]).then_inc(rest_in, 16)
            sp.dma_start(t["first_i"][:, :], ins["first"]).then_inc(rest_in, 16)
            sp.dma_start(t["first"][:, :], ins["first"].to_broadcast([P, ins["first"].shape[1]])).then_inc(rest_in, 16)
            sp.wait_ge(rest_in, 16 * (len(squares) + len(rows) + 4))

        @block.gpsimd
        def _(pool):
            nc.gpsimd.memset(ident[:, :], 0.0).then_inc(made, 1)
            nc.gpsimd.memset(later[:, :], 1.0).then_inc(made, 1)
            nc.gpsimd.memset(ones[:, :], 1.0)
            nc.gpsimd.memset(t["eps"][:, :], EPS)
            pool.wait_ge(made, 2)
            nc.gpsimd.affine_select(out=ident[:, :], in_=ident[:, :], compare_op=ALU.not_equal, fill=1.0, base=0,
                                    pattern=[[-1, P]], channel_multiplier=1).then_inc(made, 1)
            nc.gpsimd.affine_select(out=later[:, :], in_=later[:, :], compare_op=ALU.is_ge, fill=1.0 + LATER, base=0,
                                    pattern=[[1, P]], channel_multiplier=-1).then_inc(made, 1)
            nc.gpsimd.iota(t["iota_w"][:, :], pattern=[[1, WINDOW]], base=0, channel_multiplier=0,
                           allow_small_or_imprecise_dtypes=True).then_inc(made, 1)
            nc.gpsimd.iota(t["part2"][:, :], pattern=[[P, 2]], base=0, channel_multiplier=1,
                           allow_small_or_imprecise_dtypes=True).then_inc(made, 1)
            nc.gpsimd.iota(t["starts"][:, :], pattern=[[WINDOW, NP // WINDOW]], base=0, channel_multiplier=0,
                           allow_small_or_imprecise_dtypes=True).then_inc(made, 1)
            nc.gpsimd.iota(t["spare"][:, :], pattern=[[0, 1]], base=NP, channel_multiplier=1,
                           allow_small_or_imprecise_dtypes=True).then_inc(made, 1)
            pool.wait_ge(cleared, 1)
            for table in sums:
                whole = table.rearrange("(p a) c -> p (a c)", p=P)
                pool.dma_start(whole[:, 0:NP], acc[:, :]).then_inc(zeroed, 16)
                pool.dma_start(whole[:, NP:flat], acc[:, 0:flat - NP]).then_inc(zeroed, 16)
            pool.wait_ge(zeroed, 32 * len(sums))

        @block.tensor
        def _(pe):
            pe.sem_inc(multiplied, 2)
            pe.wait_ge(weights_in, 32)
            with pe.Fori(0, NCHUNK // 2) as i:
                for b in range(2):
                    c = i * 2 + b
                    pe.wait_ge(x_in[b], (i + 1) * 16)
                    pe.wait_ge(biased, c + 1)
                    for q in range(QUARTERS):
                        last = nc.tensor.matmul(ps[b][:, q, :], xc[:, b, q * P:(q + 1) * P], w1x[:, :], start=True, stop=True)
                    last.then_inc(multiplied, 1)

        @block.vector
        def _(dve):
            nc.vector.memset(acc[:, :], 0.0).then_inc(cleared, 1)
            nc.vector.memset(dinv[:, :], 0.0)
            dve.sem_inc(biased, 2)
            dve.wait_ge(weights_in, 32)
            with dve.Fori(0, NCHUNK // 2) as i:
                for b in range(2):
                    c = i * 2 + b
                    dve.wait_ge(multiplied, c + 3)
                    dve.wait_ge(stored[b], (i + 1) * 16)
                    nc.vector.tensor_tensor(pr[:, b, :, :], ps[b][:, :, :],
                                            b1a_r[:, :].unsqueeze(1).to_broadcast([P, QUARTERS, FEATURES]),
                                            ALU.add).then_inc(biased, 1)
            conv_b, gamma, beta, mean, var = (t["cols"][:, 2 + LAYERS * j:2 + LAYERS * (j + 1)] for j in range(5))
            dve.wait_ge(bn, 1)
            nc.vector.reciprocal(t["bn_d"][:, :], t["bn_t"][:, :]).then_inc(bn, 1)
            dve.wait_ge(bn, 2)
            nc.vector.tensor_tensor(t["bn_s"][:, :], t["bn_d"][:, :], gamma, ALU.mult).then_inc(bn, 1)
            nc.vector.tensor_tensor(t["bn_t"][:, :], conv_b, mean, ALU.subtract).then_inc(bn, 1)
            dve.wait_ge(bn, 4)
            nc.vector.tensor_tensor(t["bn_d"][:, :], t["bn_t"][:, :], t["bn_s"][:, :], ALU.mult).then_inc(bn, 1)
            dve.wait_ge(bn, 5)
            nc.vector.tensor_tensor(t["bn_b"][:, :], t["bn_d"][:, :], beta, ALU.add)

        @block.scalar
        def _(act):
            with act.Fori(0, NCHUNK // 2) as i:
                for b in range(2):
                    c = i * 2 + b
                    act.wait_ge(biased, c + 3)
                    act.dma_start(p_table[bass.ds(c * CHUNK, CHUNK), :].rearrange("(q p) n -> p q n", p=P),
                                  pr[:, b, :, :]).then_inc(stored[b], 16)
            act.wait_ge(rest_in, 16 * (len(squares) + len(rows) + 4))
            act.wait_ge(made, 8)
            nc.scalar.activation(t["bn_t"][:, :], t["cols"][:, 2 + 4 * LAYERS:2 + 5 * LAYERS], ACT.Sqrt,
                                 bias=t["eps"][:, 0:1]).then_inc(bn, 1)
            for b in range(2):
                act.wait_ge(stored[b], 16 * (NCHUNK // 2 + 1))


def find_wide(nc, t, ins, SUPERS):
    with ExitStack() as ctx:
        def sb(name, shape, dt=F32):
            return ctx.enter_context(nc.sbuf_tensor(name, shape, dt))

        dst_c = sb("dst_all", [P, SUPERS, TILES], I32)
        place = sb("place_all", [P, SUPERS, TILES])
        ends = sb("ends", [P, 4])
        beyond, most = sb("beyond", [P, 1]), sb("most", [P, 1])
        dst_in, steps, reduced = (ctx.enter_context(nc.semaphore(x)) for x in ("dst_all_in", "wide_steps", "wide_reduced"))
        block = ctx.enter_context(nc.Block())

        @block.sync
        def _(sp):
            sp.dma_start(dst_c[:, :, :].rearrange("p n t -> p (n t)"), ins["dst_cols"]).then_inc(dst_in, 16)

        @block.vector
        def _(dve):
            dve.wait_ge(dst_in, 16)
            nc.vector.tensor_tensor(place[:, :, :], dst_c[:, :, :], t["first"][:, :].unsqueeze(2).to_broadcast([P, SUPERS, TILES]),
                                    ALU.subtract).then_inc(steps, 1)
            dve.wait_ge(steps, 1)
            flat = place[:, :, :].rearrange("p n t -> p (n t)")
            nc.vector.tensor_reduce(ends[:, 0:1], flat, AXX, ALU.min).then_inc(steps, 1)
            nc.vector.tensor_reduce(ends[:, 1:2], flat, AXX, ALU.max).then_inc(steps, 1)
            dve.wait_ge(steps, 3)
            nc.vector.tensor_scalar(ends[:, 2:3], ends[:, 0:1], -1.0, None, ALU.mult).then_inc(steps, 1)
            nc.vector.tensor_scalar(ends[:, 3:4], ends[:, 1:2], float(WINDOW - 1), None, ALU.subtract).then_inc(steps, 1)
            dve.wait_ge(steps, 5)
            nc.vector.tensor_tensor(beyond[:, :], ends[:, 2:3], ends[:, 3:4], ALU.max).then_inc(steps, 1)
            dve.wait_ge(reduced, 1)
            nc.vector.tensor_scalar(t["wide"][:, :], most[:, :], 0.0, None, ALU.is_gt)

        @block.gpsimd
        def _(pool):
            pool.wait_ge(steps, 6)
            nc.gpsimd.partition_all_reduce(most[:, :], beyond[:, :], P, bass.bass_isa.ReduceOp.max).then_inc(reduced, 1)


def each_way(eng, t, program):
    flag = eng.value_load(t["wide"][0:1, 0:1], min_val=0, max_val=1)
    with eng.If(flag):
        program(True)
    with eng.Else():
        program(False)


def visits(eng, wide, n, slot, windows, carrier):
    if not wide:
        yield n, slot, None
        return
    eng.sem_inc(carrier, 1)
    with eng.Fori(0, windows // 2) as v:
        for s in range(2):
            yield n * windows + v * 2 + s, s, v * 2 + s


def message_pass(nc, t, ins, p_table, sums, SUPERS):
    dinv, ident, ones, w1e = t["dinv"], t["ident"], t["ones"], t["w1e"]
    NP = dinv.shape[1]
    WINDOWS = NP // WINDOW
    with ExitStack() as ctx:
        def sb(name, shape, dt=F32):
            return ctx.enter_context(nc.sbuf_tensor(name, shape, dt))

        src_b = sb("src_b", [P, 2, TILES, P], I32)
        dst_b = sb("dst_b", [P, 2, EDGES], I32)
        src_c = sb("src_c", [P, 2, TILES], I32)
        attr = sb("attr", [EDGE_FEATURES, 2, EDGES])
        window = sb("window", [P, 2, 2, FEATURES])
        nodes_w = sb("nodes_w", [P, 2, 2])
        pick = sb("pick", [P, 2, 2, EDGES])
        degree_c = sb("degree_c", [P, 2, 2])
        degree_d = sb("degree_d", [P, 2, 2, P])
        same = sb("same", [P, 2, TILES, P])
        marked = sb("marked", [P, TILES, P])
        offset = sb("offset", [P, TILES])
        moved = sb("moved", [P, TILES])
        rows = sb("rows", [P, 2, TILES, FEATURES])
        total = sb("total", [P, 2, TILES, FEATURES + 1])
        target = sb("target", [P, 2, TILES], I32)
        ps_rows = [ctx.enter_context(nc.psum_tensor(f"ps_rows{h}", [P, HALF, FEATURES], F32)) for h in range(2)]
        ps_total = [ctx.enter_context(nc.psum_tensor(f"ps_total{h}", [P, HALF, FEATURES], F32)) for h in range(2)]
        ps_degree = ctx.enter_context(nc.psum_tensor("ps_degree", [P, WINDOW], F32))
        sem = lambda name: ctx.enter_context(nc.semaphore(name))
        index_in = [sem(f"index_in{b}") for b in range(2)]
        attr_in = [sem(f"attr_in{b}") for b in range(2)]
        window_in = [sem(f"window_in{b}") for b in range(2)]
        index_free, attr_free, visited = sem("index_free"), sem("attr_free"), sem("visited")
        nodes_ready, picks_ready, degree_ready = sem("nodes_ready"), sem("picks_ready"), sem("degree_ready")
        degree_summed, degree_added = sem("degree_summed"), sem("degree_added")
        same_ready, marked_ready, steps = sem("same_ready"), sem("marked_ready"), sem("steps")
        target_ready = sem("target_ready")
        rows_ready, total_done, total_ready = (sem(x) for x in ("rows_ready", "total_done", "total_ready"))
        total_free, issued, carrier = sem("total_free"), sem("issued"), sem("carrier")
        added = [sem(f"added{k}") for k in range(TABLES)]
        CREDIT = 4
        block = ctx.enter_context(nc.Block())

        @block.sync
        def _(sp):
            def program(wide):
                with sp.Fori(0, SUPERS // 2) as i:
                    for b in range(2):
                        n = i * 2 + b
                        sp.wait_ge(index_free, n + 1)
                        sp.dma_start(dst_b[:, b, :], ins["dst_flat"][:, bass.ds(n * EDGES, EDGES)].to_broadcast([P, EDGES])).then_inc(index_in[b], 16)
                        sp.dma_start(src_b[:, b, :, :].rearrange("p t e -> p (t e)"),
                                     ins["src_flat"][:, bass.ds(n * EDGES, EDGES)].to_broadcast([P, EDGES])).then_inc(index_in[b], 16)
                        sp.dma_start(src_c[:, b, :], ins["src_cols"][:, bass.ds(n * TILES, TILES)]).then_inc(index_in[b], 16)
                        sp.wait_ge(attr_free, n + 1)
                        sp.dma_start(attr[:, b, :], ins["attrT"][:, bass.ds(n * EDGES, EDGES)]).then_inc(attr_in[b], 16)
                        for m, s, w in visits(sp, wide, n, b, WINDOWS, carrier):
                            base = w * WINDOW if wide else sp.value_load(t["first_i"][0:1, bass.ds(n, 1)], min_val=0, max_val=NP - WINDOW)
                            sp.wait_ge(visited, m * 2 + 2)
                            sp.dma_start(window[:, s, :, :], p_table[bass.ds(base, WINDOW), :].rearrange("(w p) n -> p w n", p=P)).then_inc(window_in[s], 16)

            each_way(sp, t, program)

        @block.vector
        def _(dve):
            def pick_out(wide, n, m, s, b, w):
                start = t["starts"][:, bass.ds(w, 1)] if wide else t["first"][:, bass.ds(n, 1)]
                nc.vector.tensor_scalar(nodes_w[:, s, :], t["part2"][:, :], start, None, ALU.add).then_inc(nodes_ready, 1)
                dve.wait_ge(nodes_ready, m + 1)
                dve.wait_ge(visited, m * 2 + 2)
                for half in range(2):
                    nc.vector.tensor_scalar(pick[:, s, half, :], dst_b[:, b, :], nodes_w[:, s, half:half + 1], 0.0, ALU.is_equal, ALU.add,
                                            accum_out=degree_c[:, s, half:half + 1]).then_inc(picks_ready, 1)

            def spread_degrees(m, s):
                dve.wait_ge(picks_ready, (m + 1) * 2)
                nc.vector.tensor_tensor(degree_d[:, s, :, :], ident[:, :].unsqueeze(1).to_broadcast([P, 2, P]),
                                        degree_c[:, s, :].unsqueeze(2).to_broadcast([P, 2, P]), ALU.mult).then_inc(degree_ready, 1)

            def find_targets(n, b):
                dve.wait_ge(same_ready, n + 1)
                nc.vector.tensor_tensor(marked[:, :, :], same[:, b, :, :],
                                        t["later"][:, :].unsqueeze(1).to_broadcast([P, TILES, P]), ALU.mult).then_inc(marked_ready, 1)
                nc.vector.tensor_scalar(offset[:, :], src_c[:, b, :], -1.0, t["spare"][:, 0:1], ALU.mult, ALU.add).then_inc(steps, 1)
                dve.wait_ge(marked_ready, n + 1)
                dve.wait_ge(total_free, n + 1)
                nc.vector.tensor_reduce(total[:, b, :, FEATURES], marked[:, :, :], AXX, ALU.add).then_inc(steps, 1)
                dve.wait_ge(steps, n * 3 + 2)
                nc.vector.scalar_tensor_tensor(out=moved[:, :], in0=total[:, b, :, FEATURES], scalar=LATER, in1=offset[:, :],
                                               op0=ALU.is_ge, op1=ALU.mult).then_inc(steps, 1)
                dve.wait_ge(steps, n * 3 + 3)
                nc.vector.tensor_tensor(target[:, b, :], moved[:, :], src_c[:, b, :], ALU.add).then_inc(target_ready, 1)

            def add_degrees(m, base):
                dve.wait_ge(degree_summed, m + 1)
                dve.wait_ge(degree_added, m + 1)
                nc.vector.tensor_tensor(dinv[:, bass.ds(base, WINDOW)], dinv[:, bass.ds(base, WINDOW)], ps_degree[:, :], ALU.add).then_inc(degree_added, 1)

            def program(wide):
                with dve.Fori(0, SUPERS // 2) as i:
                    for b in range(2):
                        n = i * 2 + b
                        dve.wait_ge(index_in[b], (i + 1) * 48)
                        if not wide:
                            pick_out(wide, n, n, b, b, None)
                        else:
                            dve.wait_ge(attr_free, n + 1)
                        nc.vector.tensor_tensor(same[:, b, :, :], src_b[:, b, :, :],
                                                src_c[:, b, :].unsqueeze(2).to_broadcast([P, TILES, P]), ALU.is_equal).then_inc(same_ready, 1)
                        if not wide:
                            spread_degrees(n, b)
                        find_targets(n, b)
                        for m, s, w in visits(dve, wide, n, b, WINDOWS, carrier):
                            if wide:
                                pick_out(wide, n, m, s, b, w)
                                spread_degrees(m, s)
                                add_degrees(m, w * WINDOW)
                        dve.wait_ge(target_ready, n + 1)
                        dve.sem_inc(index_free, 1)
                        if not wide:
                            add_degrees(n, dve.value_load(t["first_i"][0:1, bass.ds(n, 1)], min_val=0, max_val=NP - WINDOW))

            dve.sem_inc(index_free, 2)
            dve.sem_inc(degree_added, 1)
            each_way(dve, t, program)

        @block.tensor
        def _(pe):
            def from_attributes(h, b):
                for q in range(HALF):
                    e = slice((h * HALF + q) * P, (h * HALF + q + 1) * P)
                    nc.tensor.matmul(ps_rows[h][:, q, :], attr[:, b, e], w1e[:, :], start=(q == 0), stop=False, skip_group_check=True)

            def from_window(h, s):
                for q in range(HALF):
                    e = slice((h * HALF + q) * P, (h * HALF + q + 1) * P)
                    for half in range(2):
                        last = nc.tensor.matmul(ps_rows[h][:, q, :], pick[:, s, half, e], window[:, s, half, :],
                                                start=False, stop=(half == 1), skip_group_check=True)
                last.then_inc(visited, 1)

            def sum_degrees(m, s):
                pe.wait_ge(degree_ready, m + 1)
                pe.wait_ge(degree_added, m + 1)
                for half in range(2):
                    last = nc.tensor.matmul(ps_degree[:, half * P:(half + 1) * P], ones[:, :], degree_d[:, s, half, :], start=True, stop=True)
                last.then_inc(degree_summed, 1)

            def program(wide):
                with pe.Fori(0, SUPERS // 2) as i:
                    for b in range(2):
                        n = i * 2 + b
                        pe.wait_ge(attr_in[b], (i + 1) * 16)
                        if wide:
                            for h in range(2):
                                pe.wait_ge(rows_ready, n * 2 + h + 1)
                                from_attributes(h, b)
                        for m, s, w in visits(pe, wide, n, b, WINDOWS, carrier):
                            pe.wait_ge(window_in[s], ((m - s) // 2 if not wide else n * (WINDOWS // 2) + (w - s) // 2) * 16 + 16)
                            pe.wait_ge(picks_ready, (m + 1) * 2)
                            for h in range(2):
                                if not wide:
                                    pe.wait_ge(rows_ready, n * 2 + h + 1)
                                    from_attributes(h, b)
                                from_window(h, s)
                            sum_degrees(m, s)
                        pe.wait_ge(same_ready, n + 1)
                        for h in range(2):
                            pe.wait_ge(rows_ready, n * 2 + h + 3)
                            pe.wait_ge(total_ready, n * 2 + h + 1)
                            for q in range(HALF):
                                last = nc.tensor.matmul(ps_total[h][:, q, :], same[:, b, h * HALF + q, :], rows[:, b, h * HALF + q, :], start=True, stop=True)
                            last.then_inc(total_done, 1)
                        pe.wait_ge(total_done, n * 2 + 2)
                        pe.sem_inc(attr_free, 1)

            pe.sem_inc(attr_free, 2)
            pe.sem_inc(visited, CREDIT)
            each_way(pe, t, program)

        @block.scalar
        def _(act):
            def program(wide):
                with act.Fori(0, SUPERS // 2) as i:
                    for b in range(2):
                        n = i * 2 + b
                        for h in range(2):
                            last = (n + 1) * WINDOWS - 1 if wide else n
                            act.wait_ge(visited, last * 2 + CREDIT + h + 1)
                            nc.scalar.activation(rows[:, b, h * HALF:(h + 1) * HALF, :], ps_rows[h][:, :, :], ACT.Relu).then_inc(rows_ready, 1)
                        act.wait_ge(total_free, n + 1)
                        for h in range(2):
                            act.wait_ge(total_done, n * 2 + h + 1)
                            nc.scalar.activation(total[:, b, h * HALF:(h + 1) * HALF, 0:FEATURES], ps_total[h][:, :, :], ACT.Copy).then_inc(total_ready, 1)

            act.sem_inc(rows_ready, 2)
            act.sem_inc(total_ready, 2)
            each_way(act, t, program)

        @block.gpsimd
        def _(pool):
            pool.sem_inc(total_free, 1)
            for k in range(TABLES):
                pool.dma_start(sums[k][NP + P - 1:, 0:1], ones[0:1, 0:1]).then_inc(added[k], 16)
            with pool.Fori(0, SUPERS // 2) as i:
                for b in range(2):
                    n = i * 2 + b
                    for k in range(TABLES):
                        pool.wait_ge(added[k], n * (16 * TILES // TABLES) + 16)
                    pool.sem_inc(total_free, 1)
                    pool.wait_ge(target_ready, n + 1)
                    pool.wait_ge(total_ready, n * 2 + 4)
                    pool.sem_inc(issued, 1)
                    for q in range(TILES):
                        k = q % TABLES
                        if q >= TABLES:
                            pool.wait_ge(added[k], (n * (TILES // TABLES) + q // TABLES) * 16 + 16)
                            pool.sem_inc(issued, 1)
                        pool.indirect_dma_start(sums[k], bass.IndirectOffsetOnAxis(ap=target[:, b, q:q + 1], axis=0),
                                                total[:, b, q, :], None, compute_op=ALU.add).then_inc(added[k], 16)
            for k in range(TABLES):
                pool.wait_ge(added[k], SUPERS * (16 * TILES // TABLES) + 16)


def degree_roots(nc, dinv):
    with ExitStack() as ctx:
        rooted = ctx.enter_context(nc.semaphore("rooted"))
        block = ctx.enter_context(nc.Block())

        @block.scalar
        def _(act):
            nc.scalar.activation(dinv[:, :], dinv[:, :], ACT.Sqrt, bias=1.0).then_inc(rooted, 1)

        @block.vector
        def _(dve):
            dve.wait_ge(rooted, 1)
            nc.vector.reciprocal(dinv[:, :], dinv[:, :])


def update_nodes(nc, t, ins, sums, x1_rows, g_table, NCHUNK):
    ident, dinv, acc = t["ident"], t["dinv"], t["acc"]
    b2a, lin0_b = t["cols"][:, 0:1], t["cols"][:, 1:2]
    spread = [P, QUARTERS, FEATURES]
    with ExitStack() as ctx:
        def sb(name, shape, dt=F32):
            return ctx.enter_context(nc.sbuf_tensor(name, shape, dt))

        part = sb("part", [P, 2, TABLES, QUARTERS, FEATURES + 1])
        x_cols, x_rows = sb("x_cols", [P, 2, CHUNK]), sb("x_rows", [P, 2] + spread[1:])
        total01, total23, total = (sb(x, [P, QUARTERS, FEATURES + 1]) for x in ("total01", "total23", "total_n"))
        x_bias = sb("x_bias", spread)
        count = sb("count", [P, 3, QUARTERS])
        scale_d, some_d = sb("scale_d", spread), sb("some_d", spread)
        mean_c, agg_c, mid_c, x1_c, h_c, hs_c = (sb(x, [P, CHUNK]) for x in ("mean_c", "agg_c", "mid_c", "x1_c", "h_c", "hs_c"))
        res, x1 = sb("res", spread), sb("x1", spread)
        g_rows = sb("g_rows", spread)
        stats, moments, dev, inv = norm_tiles(sb)
        pa = ctx.enter_context(nc.psum_tensor("pa", spread, F32))
        pb = ctx.enter_context(nc.psum_tensor("pb", spread, F32))
        pc = ctx.enter_context(nc.psum_tensor("pc", spread, F32))
        flat = lambda ps: ps[:, :, :].rearrange("p q n -> p (q n)")
        sem = lambda name: ctx.enter_context(nc.semaphore(name))
        in_ = [sem(f"node_in{b}") for b in range(2)]
        (slots_free, pair01, pair23, biased, summed, clipped, inverted, diagonals, meaned, mean_ready, agged, agg_ready,
         mixed, mid_ready, outed, res_ready, stat, stat_seen, mom, dev_ready, inv_ready, x1_ready, turned, x1c_ready, lined, h_ready,
         hs_ready, projected, g_ready, acc_ready) = (sem(x) for x in (
            "slots_free pair01 pair23 biased summed clipped inverted diagonals meaned mean_ready agged agg_ready mixed "
            "mid_ready outed res_ready stat stat_seen mom dev_ready inv_ready x1_ready turned x1c_ready lined h_ready hs_ready "
            "projected g_ready acc_ready").split())
        x1_stored, g_stored = sem("x1_stored"), sem("g_stored")
        block = ctx.enter_context(nc.Block())

        @block.sync
        def _(sp):
            with sp.Fori(0, NCHUNK // 2) as i:
                for b in range(2):
                    c = i * 2 + b
                    at = bass.ds(c * CHUNK, CHUNK)
                    sp.wait_ge(slots_free, c + 1)
                    for k in range(TABLES):
                        sp.dma_start(part[:, b, k, :, :], sums[k][at, :].rearrange("(q p) n -> p q n", p=P)).then_inc(in_[b], 16)
                    sp.dma_start(x_cols[:, b, :], ins["xT"][:, at]).then_inc(in_[b], 16)
                    sp.dma_start(x_rows[:, b, :, :], ins["x"][at, :].rearrange("(q p) n -> p q n", p=P)).then_inc(in_[b], 16)

        @block.gpsimd
        def _(pool):
            with pool.Fori(0, NCHUNK // 2) as i:
                for b in range(2):
                    c = i * 2 + b
                    pool.wait_ge(in_[b], (i + 1) * 96)
                    pool.wait_ge(slots_free, c + 2)
                    nc.gpsimd.tensor_tensor(total23[:, :, :], part[:, b, 2, :, :], part[:, b, 3, :, :], ALU.add).then_inc(pair23, 1)
                    nc.gpsimd.tensor_tensor(x_bias[:, :, :], x_rows[:, b, :, :], t["b2b_r"][:, :].unsqueeze(1).to_broadcast(spread),
                                            ALU.add).then_inc(biased, 1)

        @block.vector
        def _(dve):
            dve.sem_inc(slots_free, 2)
            with dve.Fori(0, NCHUNK // 2) as i:
                for b in range(2):
                    c = i * 2 + b
                    dve.wait_ge(in_[b], (i + 1) * 96)
                    nc.vector.tensor_tensor(total01[:, :, :], part[:, b, 0, :, :], part[:, b, 1, :, :], ALU.add).then_inc(pair01, 1)
                    dve.wait_ge(pair01, c + 1)
                    dve.wait_ge(pair23, c + 1)
                    nc.vector.tensor_tensor(total[:, :, :], total01[:, :, :], total23[:, :, :], ALU.add).then_inc(summed, 1)
                    dve.wait_ge(summed, c + 1)
                    nc.vector.tensor_scalar(count[:, 0, :], total[:, :, FEATURES], 1.0, None, ALU.max).then_inc(clipped, 1)
                    nc.vector.tensor_scalar(count[:, 2, :], total[:, :, FEATURES], 1.0, None, ALU.min).then_inc(clipped, 1)
                    dve.wait_ge(clipped, c * 2 + 2)
                    nc.vector.reciprocal(count[:, 1, :], count[:, 0, :]).then_inc(inverted, 1)
                    dve.wait_ge(inverted, c + 1)
                    for tile, j in ((scale_d, 1), (some_d, 2)):
                        nc.vector.tensor_tensor(tile[:, :, :], ident[:, :].unsqueeze(1).to_broadcast(spread),
                                                count[:, j, :].unsqueeze(2).to_broadcast(spread), ALU.mult).then_inc(diagonals, 1)
                    dve.wait_ge(outed, c + 1)
                    dve.wait_ge(biased, c + 1)
                    nc.vector.tensor_tensor(res[:, :, :], pb[:, :, :], x_bias[:, :, :], ALU.add).then_inc(res_ready, 1)
                    dve.wait_ge(res_ready, c + 1)
                    norm_moments(nc, dve, c, res, stats, moments, stat, stat_seen, mom)
                    dve.wait_ge(dev_ready, c + 1)
                    nc.vector.reciprocal(inv[:, :], dev[:, :]).then_inc(inv_ready, 1)
                    dve.wait_ge(inv_ready, c + 1)
                    dve.wait_ge(x1_stored, c * 16 + 16)
                    for q in range(QUARTERS):
                        nc.vector.tensor_scalar(x1[:, q, :], res[:, q, :], moments[:, q, 0:1], inv[:, q:q + 1],
                                                ALU.subtract, ALU.mult).then_inc(x1_ready, 1)
                    dve.wait_ge(h_ready, c + 1)
                    nc.vector.tensor_tensor(hs_c[:, :], h_c[:, :], dinv[:, bass.ds(c * CHUNK, CHUNK)], ALU.mult).then_inc(hs_ready, 1)
                    dve.wait_ge(projected, c + 1)
                    nc.vector.tensor_scalar(acc[:, bass.ds(c * CHUNK, CHUNK)], flat(pb), 0.0, None, ALU.add).then_inc(acc_ready, 1)
                    dve.wait_ge(acc_ready, c + 1)
                    dve.sem_inc(slots_free, 1)

        @block.tensor
        def _(pe):
            with pe.Fori(0, NCHUNK // 2) as i:
                for b in range(2):
                    c = i * 2 + b
                    pe.wait_ge(diagonals, c * 2 + 2)
                    for q in range(QUARTERS):
                        last = nc.tensor.matmul(pa[:, q, :], total[:, q, 0:FEATURES], scale_d[:, q, :], start=True, stop=True)
                    last.then_inc(meaned, 1)
                    pe.wait_ge(mean_ready, c + 1)
                    pe.wait_ge(slots_free, c + 2)
                    for q in range(QUARTERS):
                        nc.tensor.matmul(pb[:, q, :], t["w1b"][:, :], mean_c[:, q * P:(q + 1) * P], start=True, stop=False)
                        last = nc.tensor.matmul(pb[:, q, :], t["b1b_r"][:, :], some_d[:, q, :], start=False, stop=True)
                    last.then_inc(agged, 1)
                    pe.wait_ge(agg_ready, c + 1)
                    nc.tensor.matmul(flat(pa), t["w2x"][:, :], x_cols[:, b, :], start=True, stop=False)
                    nc.tensor.matmul(flat(pa), t["w2g"][:, :], agg_c[:, :], start=False, stop=True).then_inc(mixed, 1)
                    pe.wait_ge(mid_ready, c + 1)
                    for q in range(QUARTERS):
                        last = nc.tensor.matmul(pb[:, q, :], mid_c[:, q * P:(q + 1) * P], t["w2b"][:, :], start=True, stop=True)
                    last.then_inc(outed, 1)
                    pe.wait_ge(x1_ready, c * QUARTERS + QUARTERS)
                    for q in range(QUARTERS):
                        last = nc.tensor.transpose(pa[:, q, :], x1[:, q, :], ident[:, :])
                    last.then_inc(turned, 1)
                    pe.wait_ge(x1c_ready, c + 1)
                    nc.tensor.matmul(flat(pb), t["lin0"][:, :], x1_c[:, :], start=True, stop=True).then_inc(lined, 1)
                    pe.wait_ge(hs_ready, c + 1)
                    project_chunk(nc, t["conv"][:, 0, :], hs_c, pc, flat(pb)).then_inc(projected, 1)

        @block.scalar
        def _(act):
            act.sem_inc(x1_stored, 16)
            act.sem_inc(g_stored, 16)
            with act.Fori(0, NCHUNK // 2) as i:
                for b in range(2):
                    c = i * 2 + b
                    at = bass.ds(c * CHUNK, CHUNK)
                    act.wait_ge(meaned, c + 1)
                    nc.scalar.activation(mean_c[:, :], flat(pa), ACT.Copy).then_inc(mean_ready, 1)
                    act.wait_ge(agged, c + 1)
                    nc.scalar.activation(agg_c[:, :], flat(pb), ACT.Copy).then_inc(agg_ready, 1)
                    act.wait_ge(mixed, c + 1)
                    nc.scalar.activation(mid_c[:, :], flat(pa), ACT.Relu, bias=b2a).then_inc(mid_ready, 1)
                    act.wait_ge(mom, c * QUARTERS + QUARTERS)
                    nc.scalar.activation(dev[:, :], moments[:, :, 1], ACT.Sqrt, bias=t["eps"][:, 0:1]).then_inc(dev_ready, 1)
                    act.wait_ge(x1_ready, c * QUARTERS + QUARTERS)
                    act.dma_start(x1_rows[at, :].rearrange("(q p) n -> p q n", p=P), x1[:, :, :]).then_inc(x1_stored, 16)
                    act.wait_ge(turned, c + 1)
                    nc.scalar.activation(x1_c[:, :], flat(pa), ACT.Copy).then_inc(x1c_ready, 1)
                    act.wait_ge(lined, c + 1)
                    nc.scalar.activation(h_c[:, :], flat(pb), ACT.Relu, bias=lin0_b).then_inc(h_ready, 1)
                    act.wait_ge(projected, c + 1)
                    act.wait_ge(g_stored, c * 16 + 16)
                    nc.scalar.activation(g_rows[:, :, :], pc[:, :, :], ACT.Copy).then_inc(g_ready, 1)
                    act.wait_ge(g_ready, c + 1)
                    act.dma_start(g_table[at, :].rearrange("(q p) n -> p q n", p=P), g_rows[:, :, :]).then_inc(g_stored, 16)
            act.wait_ge(x1_stored, NCHUNK * 16 + 16)
            act.wait_ge(g_stored, NCHUNK * 16 + 16)


def norm_tiles(sb):
    return (sb("stats", [P, QUARTERS, 6]), sb("moments", [P, QUARTERS, 2]), sb("dev", [P, QUARTERS]), sb("inv", [P, QUARTERS]))


def norm_moments(nc, dve, c, res, stats, moments, stat, stat_seen, mom):
    for q in range(QUARTERS):
        nc.vector.bn_stats(stats[:, q, :], res[:, q, :]).then_inc(stat, 1)
    dve.wait_ge(stat, c * QUARTERS + QUARTERS)
    dve.sem_inc(stat_seen, 1)
    for q in range(QUARTERS):
        nc.vector.bn_aggr(moments[:, q, :], stats[:, q, :]).then_inc(mom, 1)
    dve.wait_ge(mom, c * QUARTERS + QUARTERS)


def project_chunk(nc, weights, hs_c, ps_rows, ps_cols):
    for q in range(QUARTERS):
        nc.tensor.matmul(ps_rows[:, q, :], hs_c[:, q * P:(q + 1) * P], weights, start=True, stop=True)
    return nc.tensor.matmul(ps_cols, weights, hs_c[:, :], start=True, stop=True)


def convolve_semaphores(sem):
    one = "dst_free rows_used placed picked acc_added summed gathers_issued"
    return {**{x: sem(x) for x in one.split()}, "src_in": [sem(f"src_in{r}") for r in range(RING)],
            "dst_in": [sem(f"dst_in{b}") for b in range(2)], "rows_in": [sem(f"rows_in{r}") for r in range(RING)]}


def convolve(nc, t, ins, g_table, SUPERS, layer, sems):
    acc = t["acc"]
    NP = acc.shape[1]
    WINDOWS = NP // WINDOW
    with ExitStack() as ctx:
        def sb(name, shape, dt=F32):
            return ctx.enter_context(nc.sbuf_tensor(f"{name}{layer}", shape, dt))

        src_c, dst_c = sb("gsrc", [P, RING, TILES], I32), sb("gdst", [P, 2, TILES], I32)
        place = sb("place", [P, 2, TILES])
        pick = sb("gpick", [P, 2, TILES, WINDOW])
        rows = sb("grows", [P, RING, TILES, FEATURES])
        ps = [ctx.enter_context(nc.psum_tensor(f"gps{layer}_{b}", [P, WINDOW], F32)) for b in range(2)]
        src_in, dst_in, rows_in = sems["src_in"], sems["dst_in"], sems["rows_in"]
        dst_free, rows_used, placed, picked, added, summed, issued = (
            sems[x] for x in "dst_free rows_used placed picked acc_added summed gathers_issued".split())
        carrier = issued
        done = layer * SUPERS
        block = ctx.enter_context(nc.Block())

        @block.sync
        def _(sp):
            with sp.Fori(0, SUPERS // RING) as i:
                for r in range(RING):
                    n = i * RING + r + done
                    at = bass.ds((i * RING + r) * TILES, TILES)
                    sp.wait_ge(rows_used, n + 1)
                    sp.dma_start(src_c[:, r, :], ins["src_cols"][:, at]).then_inc(src_in[r], 16)
                    sp.wait_ge(dst_free, n + 1)
                    sp.dma_start(dst_c[:, r % 2, :], ins["dst_cols"][:, at]).then_inc(dst_in[r % 2], 16)

        @block.gpsimd
        def _(pool):
            with pool.Fori(0, SUPERS // RING) as i:
                for r in range(RING):
                    pool.wait_ge(src_in[r], (i + done // RING + 1) * 16)
                    pool.sem_inc(issued, 1)
                    for q in range(TILES):
                        pool.indirect_dma_start(rows[:, r, q, :], None, g_table,
                                                bass.IndirectOffsetOnAxis(ap=src_c[:, r, q:q + 1], axis=0)).then_inc(rows_in[r], 16)

        @block.vector
        def _(dve):
            def pick_out(local, m, s, b, w):
                dve.wait_ge(summed, m + 1)
                start = t["first"][:, bass.ds(local, 1)] if w is None else t["starts"][:, bass.ds(w, 1)]
                nc.vector.tensor_tensor(place[:, s, :], dst_c[:, b, :], start.to_broadcast([P, TILES]), ALU.subtract).then_inc(placed, 1)
                dve.wait_ge(placed, m + 1)
                for q in range(TILES):
                    last = nc.vector.tensor_scalar(pick[:, s, q, :], t["iota_w"][:, :], place[:, s, q:q + 1], None, ALU.is_equal)
                last.then_inc(picked, 1)

            def add_sums(m, s, base):
                dve.wait_ge(summed, m + 3)
                dve.wait_ge(added, m + 2)
                nc.vector.tensor_tensor(acc[:, bass.ds(base, WINDOW)], acc[:, bass.ds(base, WINDOW)], ps[s][:, :], ALU.add).then_inc(added, 1)

            def program(wide):
                with dve.Fori(0, SUPERS // RING) as i:
                    for r in range(RING):
                        local, b = i * RING + r, r % 2
                        n = local + done
                        dve.wait_ge(dst_in[b], (i * (RING // 2) + done // 2 + r // 2 + 1) * 16)
                        for m, s, w in visits(dve, wide, n, b, WINDOWS, carrier):
                            pick_out(local, m, s, b, w)
                            if wide:
                                add_sums(m, s, w * WINDOW)
                        dve.sem_inc(dst_free, 1)
                        if not wide:
                            add_sums(n, b, dve.value_load(t["first_i"][0:1, bass.ds(local, 1)], min_val=0, max_val=NP - WINDOW))

            if layer == 0:
                dve.sem_inc(dst_free, 2)
            each_way(dve, t, program)

        @block.tensor
        def _(pe):
            def program(wide):
                with pe.Fori(0, SUPERS // RING) as i:
                    for r in range(RING):
                        local, b = i * RING + r, r % 2
                        n = local + done
                        pe.wait_ge(rows_in[r], (i + done // RING + 1) * 16 * TILES)
                        for m, s, w in visits(pe, wide, n, b, WINDOWS, carrier):
                            pe.wait_ge(picked, m + 1)
                            pe.wait_ge(added, m + 1)
                            for q in range(TILES):
                                last = nc.tensor.matmul(ps[s][:, :], rows[:, r, q, :], pick[:, s, q, :], start=(q == 0), stop=(q == TILES - 1))
                            last.then_inc(summed, 1)
                        last_visit = (n + 1) * WINDOWS - 1 if wide else n
                        pe.wait_ge(summed, last_visit + 3)
                        pe.sem_inc(rows_used, 1)

            if layer == 0:
                pe.sem_inc(summed, 2)
                pe.sem_inc(rows_used, RING)
                pe.sem_inc(added, 2)
            each_way(pe, t, program)


def project_semaphores(sem):
    return {**{x: sem(x + "_p") for x in "scaled h_ready hs_ready projected g_ready acc_ready".split()},
            "g_stored": [sem(f"g_stored_p{b}") for b in range(2)]}


def project(nc, t, g_table, NCHUNK, layer, sems):
    acc, dinv = t["acc"], t["dinv"]
    spread = [P, QUARTERS, FEATURES]
    with ExitStack() as ctx:
        def sb(name, shape, dt=F32):
            return ctx.enter_context(nc.sbuf_tensor(f"{name}_p{layer}", shape, dt))

        t_c, h_c, hs_c, g_rows = sb("t_c", [P, 2, CHUNK]), sb("h_c", [P, 2, CHUNK]), sb("hs_c", [P, 2, CHUNK]), sb("g_rows", [P, 2] + spread[1:])
        pr = [ctx.enter_context(nc.psum_tensor(f"pr{layer}_{b}", spread, F32)) for b in range(2)]
        pc = [ctx.enter_context(nc.psum_tensor(f"pc{layer}_{b}", [P, CHUNK], F32)) for b in range(2)]
        scaled, h_ready, hs_ready, projected, g_ready, acc_ready, g_stored = (
            sems[x] for x in "scaled h_ready hs_ready projected g_ready acc_ready g_stored".split())
        done = layer * NCHUNK
        block = ctx.enter_context(nc.Block())

        @block.vector
        def _(dve):
            if layer == 0:
                dve.sem_inc(acc_ready, 2)
            with dve.Fori(0, NCHUNK // 2) as i:
                for b in range(2):
                    c = i * 2 + b + done
                    at = bass.ds((i * 2 + b) * CHUNK, CHUNK)
                    dve.wait_ge(hs_ready, c + 1)
                    nc.vector.tensor_tensor(t_c[:, b, :], acc[:, at], dinv[:, at], ALU.mult).then_inc(scaled, 1)
                    dve.wait_ge(h_ready, c + 1)
                    nc.vector.tensor_tensor(hs_c[:, b, :], h_c[:, b, :], dinv[:, at], ALU.mult).then_inc(hs_ready, 1)
                    dve.wait_ge(projected, c + 1)
                    nc.vector.tensor_scalar(acc[:, at], pc[b][:, :], 0.0, None, ALU.add).then_inc(acc_ready, 1)

        @block.scalar
        def _(act):
            if layer == 0:
                act.sem_inc(hs_ready, 1)
                act.sem_inc(g_stored[0], 16)
                act.sem_inc(g_stored[1], 16)
            with act.Fori(0, NCHUNK // 2) as i:
                for b in range(2):
                    c = i * 2 + b + done
                    act.wait_ge(scaled, c + 1)
                    nc.scalar.activation(h_c[:, b, :], t_c[:, b, :], ACT.Relu, bias=t["bn_b"][:, layer:layer + 1],
                                         scale=t["bn_s"][:, layer:layer + 1]).then_inc(h_ready, 1)
                    act.wait_ge(projected, c + 1)
                    act.wait_ge(g_stored[b], (i + done // 2 + 1) * 16)
                    nc.scalar.activation(g_rows[:, b, :, :], pr[b][:, :, :], ACT.Copy).then_inc(g_ready, 1)

        @block.tensor
        def _(pe):
            with pe.Fori(0, NCHUNK // 2) as i:
                for b in range(2):
                    c = i * 2 + b + done
                    pe.wait_ge(hs_ready, c + 2)
                    pe.wait_ge(acc_ready, c + 1)
                    for q in range(QUARTERS):
                        nc.tensor.matmul(pr[b][:, q, :], hs_c[:, b, q * P:(q + 1) * P], t["conv"][:, layer + 1, :], start=True, stop=True)
                    nc.tensor.matmul(pc[b][:, :], t["conv"][:, layer + 1, :], hs_c[:, b, :], start=True, stop=True).then_inc(projected, 1)

        @block.sync
        def _(sp):
            with sp.Fori(0, NCHUNK // 2) as i:
                for b in range(2):
                    c = i * 2 + b + done
                    sp.wait_ge(g_ready, c + 1)
                    sp.dma_start(g_table[bass.ds((i * 2 + b) * CHUNK, CHUNK), :].rearrange("(q p) n -> p q n", p=P), g_rows[:, b, :, :]).then_inc(g_stored[b], 16)
            for b in range(2):
                sp.wait_ge(g_stored[b], (done + NCHUNK) // 2 * 16 + 16)


def finish(nc, t, x1_rows, out, nodes, NCHUNK):
    acc, dinv = t["acc"], t["dinv"]
    spread = [P, QUARTERS, FEATURES]
    layer = LAYERS - 1
    with ExitStack() as ctx:
        def sb(name, shape, dt=F32):
            return ctx.enter_context(nc.sbuf_tensor(f"{name}_f", shape, dt))

        t_c, h_c = sb("t_c", [P, CHUNK]), sb("h_c", [P, CHUNK])
        x1, x1_bias = sb("x1", [P, 2] + spread[1:]), sb("x1_bias", spread)
        res, y = sb("res", spread), sb("y", [P, 2] + spread[1:])
        stats, moments, dev, inv = norm_tiles(sb)
        ps = ctx.enter_context(nc.psum_tensor("ps_f", spread, F32))
        sem = lambda name: ctx.enter_context(nc.semaphore(f"{name}_f"))
        x1_in = [sem(f"x1_in{b}") for b in range(2)]
        stored = [sem(f"stored{b}") for b in range(2)]
        scaled, h_ready, biased, lined, res_ready, stat, stat_seen, mom, dev_ready, inv_ready, y_ready = (
            sem(x) for x in "scaled h_ready biased lined res_ready stat stat_seen mom dev_ready inv_ready y_ready".split())
        block = ctx.enter_context(nc.Block())

        @block.sync
        def _(sp):
            with sp.Fori(0, NCHUNK // 2) as i:
                for b in range(2):
                    c = i * 2 + b
                    sp.wait_ge(biased, c + 1)
                    sp.dma_start(x1[:, b, :, :], x1_rows[bass.ds(c * CHUNK, CHUNK), :].rearrange("(q p) n -> p q n", p=P)).then_inc(x1_in[b], 16)

        @block.gpsimd
        def _(pool):
            pool.sem_inc(biased, 2)
            pool.sem_inc(res_ready, 1)
            with pool.Fori(0, NCHUNK // 2) as i:
                for b in range(2):
                    c = i * 2 + b
                    pool.wait_ge(x1_in[b], (i + 1) * 16)
                    pool.wait_ge(res_ready, c + 1)
                    nc.gpsimd.tensor_tensor(x1_bias[:, :, :], x1[:, b, :, :], t["lin1b_r"][:, :].unsqueeze(1).to_broadcast(spread),
                                            ALU.add).then_inc(biased, 1)

        @block.vector
        def _(dve):
            with dve.Fori(0, NCHUNK // 2) as i:
                for b in range(2):
                    c = i * 2 + b
                    at = bass.ds(c * CHUNK, CHUNK)
                    nc.vector.tensor_tensor(t_c[:, :], acc[:, at], dinv[:, at], ALU.mult).then_inc(scaled, 1)
                    dve.wait_ge(lined, c + 1)
                    dve.wait_ge(biased, c + 3)
                    nc.vector.tensor_tensor(res[:, :, :], ps[:, :, :], x1_bias[:, :, :], ALU.add).then_inc(res_ready, 1)
                    dve.wait_ge(res_ready, c + 2)
                    norm_moments(nc, dve, c, res, stats, moments, stat, stat_seen, mom)
                    dve.wait_ge(dev_ready, c + 1)
                    nc.vector.reciprocal(inv[:, :], dev[:, :]).then_inc(inv_ready, 1)
                    dve.wait_ge(inv_ready, c + 1)
                    dve.wait_ge(stored[b], (i + 1) * 16)
                    for q in range(QUARTERS):
                        nc.vector.tensor_scalar(y[:, b, q, :], res[:, q, :], moments[:, q, 0:1], inv[:, q:q + 1],
                                                ALU.subtract, ALU.mult).then_inc(y_ready, 1)

        @block.tensor
        def _(pe):
            with pe.Fori(0, NCHUNK) as c:
                pe.wait_ge(h_ready, c + 1)
                pe.wait_ge(res_ready, c + 1)
                for q in range(QUARTERS):
                    last = nc.tensor.matmul(ps[:, q, :], h_c[:, q * P:(q + 1) * P], t["lin1"][:, :], start=True, stop=True)
                last.then_inc(lined, 1)

        @block.scalar
        def _(act):
            act.sem_inc(stored[0], 16)
            act.sem_inc(stored[1], 16)
            full = nodes // CHUNK
            with act.Fori(0, NCHUNK // 2) as i:
                for b in range(2):
                    c = i * 2 + b
                    act.wait_ge(scaled, c + 1)
                    nc.scalar.activation(h_c[:, :], t_c[:, :], ACT.Relu, bias=t["bn_b"][:, layer:layer + 1],
                                         scale=t["bn_s"][:, layer:layer + 1]).then_inc(h_ready, 1)
                    act.wait_ge(mom, c * QUARTERS + QUARTERS)
                    nc.scalar.activation(dev[:, :], moments[:, :, 1], ACT.Sqrt, bias=t["eps"][:, 0:1]).then_inc(dev_ready, 1)
                    act.wait_ge(y_ready, c * QUARTERS + QUARTERS)
                    act.dma_start(out[bass.ds(c * CHUNK, CHUNK), :].rearrange("(q p) n -> p q n", p=P), y[:, b, :, :]).then_inc(stored[b], 16)
            for b in range(2):
                act.wait_ge(stored[b], NCHUNK // 2 * 16 + 16)


_L0, _L1 = "L0_gnn_", "L1_gnn_"


def kernel(**inputs):
    import concourse.bacc as bacc
    from concourse.bass_utils import run_bass_kernel_spmd

    a = {k: np.asarray(v) for k, v in inputs.items()}
    nodes, edges = a["x"].shape[0], a["src"].shape[0]
    NP, SUPERS = sizes(nodes, edges)
    EP = SUPERS * EDGES

    def padded(v, rows, fill=0):
        return np.concatenate([v, np.full((rows - v.shape[0],) + v.shape[1:], fill, v.dtype)])

    x, src, dst = padded(a["x"], NP), padded(a["src"], EP, nodes), padded(a["dst"], EP, nodes)
    per_layer = [a[_L1 + k] for k in ("conv_b", "bn_gamma", "bn_beta", "bn_mean", "bn_var")]
    arrays = {
        "x": x, "xT": np.ascontiguousarray(x.T), "attrT": np.ascontiguousarray(padded(a["edge_attr_64"], EP).T),
        "src_flat": src.reshape(1, EP), "dst_flat": dst.reshape(1, EP),
        "src_cols": np.ascontiguousarray(src.reshape(-1, P).T), "dst_cols": np.ascontiguousarray(dst.reshape(-1, P).T),
        "first": np.ascontiguousarray(dst.reshape(SUPERS, EDGES)[:, 0]).reshape(1, SUPERS),
        "cols": np.ascontiguousarray(np.concatenate([a[_L0 + "b2a"][None], a[_L1 + "lin0_b"][None], *per_layer]).T),
        "lin0_w": a[_L1 + "lin0_w"], "lin1_w": a[_L1 + "lin1_w"], "lin1_b": a[_L1 + "lin1_b"], "conv_w": a[_L1 + "conv_w"],
        **{k: a[_L0 + k] for k in ("W1a", "b1a", "W1b", "b1b", "W2a", "W2b", "b2b")},
    }
    arrays = {f"in_{k}": v for k, v in arrays.items()}
    nc = bacc.Bacc("TRN2", target_bir_lowering=False, num_devices=1)
    ins = {k[3:]: nc.dram_tensor(k, v.shape, mybir.dt.from_np(v.dtype), kind="ExternalInput").ap() for k, v in arrays.items()}
    out = nc.dram_tensor("out", (NP, FEATURES), F32, kind="ExternalOutput").ap()
    build(nc, nodes, edges, ins, out)
    r = run_bass_kernel_spmd(nc, [arrays], core_ids=[0])
    return r.results[0]["out"][:nodes]
```

```python
from contextlib import ExitStack

import numpy as np

import concourse.bass as bass
from concourse import mybir

ALU = mybir.AluOpType
ACT = mybir.ActivationFunctionType
AXX = mybir.AxisListType.X
F32 = mybir.dt.float32
I32 = mybir.dt.int32

P = 128
FEATURES = 128
EDGE_FEATURES = 64
TILES = 8
EDGES = TILES * P
HALF = TILES // 2
CHUNK = 512
QUARTERS = CHUNK // P
LEAD = P - EDGE_FEATURES
WINDOW = LEAD + P
STEP = P
TABLES = 4
LATER = 1024.0
EPS = 1e-5
LAYERS = 3
RING = 4


def sizes(nodes, edges):
    chunks = -(-(nodes + 1 + WINDOW) // CHUNK)
    supers = -(-edges // EDGES)
    return (chunks + chunks % 2) * CHUNK, supers + -supers % RING


def build(nc, nodes, edges, ins, out):
    NP, SUPERS = sizes(nodes, edges)
    NCHUNK = NP // CHUNK
    ROWW = FEATURES + 1
    TROWS = NP + P
    p_table = nc.dram_tensor("p_table", [NP, FEATURES], F32, kind="Internal").ap()
    g_table = nc.dram_tensor("g_table", [NP, FEATURES], F32, kind="Internal").ap()
    x1_rows = nc.dram_tensor("x1_rows", [NP, FEATURES], F32, kind="Internal").ap()
    sums = [nc.dram_tensor(f"sums{k}", [TROWS, ROWW], F32, kind="Internal").ap() for k in range(TABLES)]

    whole = ExitStack()
    with whole:
        def sb(name, shape, dt=F32):
            return whole.enter_context(nc.sbuf_tensor(name, shape, dt))

        sem = lambda name: whole.enter_context(nc.semaphore(name))
        carrier = sem("carrier")

        acc = sb("acc", [P, NP])
        dinv = sb("dinv", [P, NP])
        ident = sb("ident", [P, P])
        ones = sb("ones", [P, P])
        later = sb("later", [P, P])
        iota_w = sb("iota_w", [P, WINDOW])
        part_node = sb("part_node", [P, 3])
        spare = sb("spare", [P, 1])
        eps = sb("eps", [P, 1])
        w1x = sb("w1x", [P, FEATURES])
        w1b = sb("w1b", [P, FEATURES])
        w2x = sb("w2x", [P, FEATURES])
        w2g = sb("w2g", [P, FEATURES])
        w2b = sb("w2b", [P, FEATURES])
        lin0 = sb("lin0", [P, FEATURES])
        lin1 = sb("lin1", [P, FEATURES])
        conv = sb("conv", [P, LAYERS, FEATURES])
        b1a_r = sb("b1a_r", [P, FEATURES])
        b1b_r = sb("b1b_r", [P, FEATURES])
        b2b_r = sb("b2b_r", [P, FEATURES])
        lin1b_r = sb("lin1b_r", [P, FEATURES])
        cols = sb("cols", [P, 2 + 5 * LAYERS])
        bn_s = sb("bn_s", [P, LAYERS])
        bn_b = sb("bn_b", [P, LAYERS])
        bn_t = sb("bn_t", [P, LAYERS])
        bn_d = sb("bn_d", [P, LAYERS])
        first_i = sb("first_i", [1, SUPERS], I32)
        first = sb("first", [P, SUPERS], I32)
        starts = sb("starts", [P, NP // STEP])
        wide = sb("wide", [P, 1], I32)

        setup(nc, locals(), ins, p_table, sums, NP, NCHUNK, TROWS)
        find_wide(nc, locals(), ins, SUPERS)
        message_pass(nc, locals(), ins, p_table, sums, SUPERS)
        degree_roots(nc, dinv)
        update_nodes(nc, locals(), ins, sums, x1_rows, g_table, NCHUNK)
        convolve_sems, project_sems = convolve_semaphores(sem), project_semaphores(sem)
        for layer in range(LAYERS):
            convolve(nc, locals(), ins, g_table, SUPERS, layer, convolve_sems)
            if layer + 1 < LAYERS:
                project(nc, locals(), g_table, NCHUNK, layer, project_sems)
        finish(nc, locals(), x1_rows, out, NCHUNK)


def setup(nc, t, ins, p_table, sums, NP, NCHUNK, TROWS):
    acc, dinv, ident, ones, later = t["acc"], t["dinv"], t["ident"], t["ones"], t["later"]
    w1x, b1a_r = t["w1x"], t["b1a_r"]
    rows = [(t["b1b_r"], "b1b"), (t["b2b_r"], "b2b"), (t["lin1b_r"], "lin1_b")]
    squares = [(t["w1b"], ins["W1b"]),
               (t["w2x"], ins["W2a"][0:FEATURES, :]), (t["w2g"], ins["W2a"][FEATURES:, :]),
               (t["w2b"], ins["W2b"]), (t["lin0"], ins["lin0_w"]), (t["lin1"], ins["lin1_w"])]
    flat = TROWS * (FEATURES + 1) // P
    with ExitStack() as ctx:
        xc = ctx.enter_context(nc.sbuf_tensor("xc", [P, 2, CHUNK], F32))
        pr = ctx.enter_context(nc.sbuf_tensor("pr", [P, 2, QUARTERS, FEATURES], F32))
        ps = [ctx.enter_context(nc.psum_tensor(f"ps{b}", [P, QUARTERS, FEATURES], F32)) for b in range(2)]
        sem = lambda name: ctx.enter_context(nc.semaphore(name))
        weights_in, rest_in = sem("weights_in"), sem("rest_in")
        x_in = [sem(f"x_in{b}") for b in range(2)]
        stored = [sem(f"p_stored{b}") for b in range(2)]
        zeroed, cleared = sem("zeroed"), sem("cleared")
        made, multiplied, biased = sem("made"), sem("multiplied"), sem("biased")
        bn = sem("bn")
        block = ctx.enter_context(nc.Block())

        @block.sync
        def _(sp):
            sp.dma_start(w1x[:, :], ins["W1a"][0:FEATURES, :]).then_inc(weights_in, 16)
            sp.dma_start(b1a_r[:, :], ins["b1a"].rearrange("(a n) -> a n", a=1).to_broadcast([P, FEATURES])).then_inc(weights_in, 16)
            sp.sem_inc(stored[0], 16)
            sp.sem_inc(stored[1], 16)
            with sp.Fori(0, NCHUNK // 2) as i:
                for b in range(2):
                    c = i * 2 + b
                    sp.wait_ge(multiplied, c + 1)
                    sp.dma_start(xc[:, b, :], ins["xT"][:, bass.ds(c * CHUNK, CHUNK)]).then_inc(x_in[b], 16)
            for tile, source in squares:
                sp.dma_start(tile[:, :], source).then_inc(rest_in, 16)
            for tile, name in rows:
                sp.dma_start(tile[:, :], ins[name].rearrange("(a n) -> a n", a=1).to_broadcast([P, FEATURES])).then_inc(rest_in, 16)
            sp.dma_start(t["conv"][:, :, :], ins["conv_w"].rearrange("l k n -> k l n")).then_inc(rest_in, 16)
            sp.dma_start(t["cols"][:, :], ins["cols"]).then_inc(rest_in, 16)
            sp.dma_start(t["first_i"][:, :], ins["first"]).then_inc(rest_in, 16)
            sp.dma_start(t["first"][:, :], ins["first"].to_broadcast([P, ins["first"].shape[1]])).then_inc(rest_in, 16)
            sp.wait_ge(rest_in, 16 * (len(squares) + len(rows) + 4))

        @block.gpsimd
        def _(pool):
            nc.gpsimd.memset(ident[:, :], 0.0).then_inc(made, 1)
            nc.gpsimd.memset(later[:, :], 1.0).then_inc(made, 1)
            nc.gpsimd.memset(ones[:, :], 1.0)
            nc.gpsimd.memset(t["eps"][:, :], EPS)
            pool.wait_ge(made, 2)
            nc.gpsimd.affine_select(out=ident[:, :], in_=ident[:, :], compare_op=ALU.not_equal, fill=1.0, base=0,
                                    pattern=[[-1, P]], channel_multiplier=1).then_inc(made, 1)
            nc.gpsimd.affine_select(out=later[:, :], in_=later[:, :], compare_op=ALU.is_ge, fill=1.0 + LATER, base=0,
                                    pattern=[[1, P]], channel_multiplier=-1).then_inc(made, 1)
            nc.gpsimd.iota(t["iota_w"][:, :], pattern=[[1, WINDOW]], base=0, channel_multiplier=0,
                           allow_small_or_imprecise_dtypes=True).then_inc(made, 1)
            for j, offset in enumerate((-EDGE_FEATURES, LEAD, 0)):
                nc.gpsimd.iota(t["part_node"][:, j:j + 1], pattern=[[0, 1]], base=offset, channel_multiplier=1,
                               allow_small_or_imprecise_dtypes=True).then_inc(made, 1)
            nc.gpsimd.iota(t["starts"][:, :], pattern=[[STEP, NP // STEP]], base=0, channel_multiplier=0,
                           allow_small_or_imprecise_dtypes=True).then_inc(made, 1)
            nc.gpsimd.iota(t["spare"][:, :], pattern=[[0, 1]], base=NP, channel_multiplier=1,
                           allow_small_or_imprecise_dtypes=True).then_inc(made, 1)
            pool.wait_ge(cleared, 1)
            for table in sums:
                whole = table.rearrange("(p a) c -> p (a c)", p=P)
                pool.dma_start(whole[:, 0:NP], acc[:, :]).then_inc(zeroed, 16)
                pool.dma_start(whole[:, NP:flat], acc[:, 0:flat - NP]).then_inc(zeroed, 16)
            pool.wait_ge(zeroed, 32 * len(sums))

        @block.tensor
        def _(pe):
            pe.sem_inc(multiplied, 2)
            pe.wait_ge(weights_in, 32)
            with pe.Fori(0, NCHUNK // 2) as i:
                for b in range(2):
                    c = i * 2 + b
                    pe.wait_ge(x_in[b], (i + 1) * 16)
                    pe.wait_ge(biased, c + 1)
                    for q in range(QUARTERS):
                        last = nc.tensor.matmul(ps[b][:, q, :], xc[:, b, q * P:(q + 1) * P], w1x[:, :], start=True, stop=True)
                    last.then_inc(multiplied, 1)

        @block.vector
        def _(dve):
            nc.vector.memset(acc[:, :], 0.0).then_inc(cleared, 1)
            nc.vector.memset(dinv[:, :], 0.0)
            dve.sem_inc(biased, 2)
            dve.wait_ge(weights_in, 32)
            with dve.Fori(0, NCHUNK // 2) as i:
                for b in range(2):
                    c = i * 2 + b
                    dve.wait_ge(multiplied, c + 3)
                    dve.wait_ge(stored[b], (i + 1) * 16)
                    nc.vector.tensor_tensor(pr[:, b, :, :], ps[b][:, :, :],
                                            b1a_r[:, :].unsqueeze(1).to_broadcast([P, QUARTERS, FEATURES]),
                                            ALU.add).then_inc(biased, 1)
            conv_b, gamma, beta, mean, var = (t["cols"][:, 2 + LAYERS * j:2 + LAYERS * (j + 1)] for j in range(5))
            dve.wait_ge(bn, 1)
            nc.vector.reciprocal(t["bn_d"][:, :], t["bn_t"][:, :]).then_inc(bn, 1)
            dve.wait_ge(bn, 2)
            nc.vector.tensor_tensor(t["bn_s"][:, :], t["bn_d"][:, :], gamma, ALU.mult).then_inc(bn, 1)
            nc.vector.tensor_tensor(t["bn_t"][:, :], conv_b, mean, ALU.subtract).then_inc(bn, 1)
            dve.wait_ge(bn, 4)
            nc.vector.tensor_tensor(t["bn_d"][:, :], t["bn_t"][:, :], t["bn_s"][:, :], ALU.mult).then_inc(bn, 1)
            dve.wait_ge(bn, 5)
            nc.vector.tensor_tensor(t["bn_b"][:, :], t["bn_d"][:, :], beta, ALU.add)

        @block.scalar
        def _(act):
            with act.Fori(0, NCHUNK // 2) as i:
                for b in range(2):
                    c = i * 2 + b
                    act.wait_ge(biased, c + 3)
                    act.dma_start(p_table[bass.ds(c * CHUNK, CHUNK), :].rearrange("(q p) n -> p q n", p=P),
                                  pr[:, b, :, :]).then_inc(stored[b], 16)
            act.wait_ge(rest_in, 16 * (len(squares) + len(rows) + 4))
            act.wait_ge(made, 10)
            nc.scalar.activation(t["bn_t"][:, :], t["cols"][:, 2 + 4 * LAYERS:2 + 5 * LAYERS], ACT.Sqrt,
                                 bias=t["eps"][:, 0:1]).then_inc(bn, 1)
            for b in range(2):
                act.wait_ge(stored[b], 16 * (NCHUNK // 2 + 1))


def find_wide(nc, t, ins, SUPERS):
    with ExitStack() as ctx:
        def sb(name, shape, dt=F32):
            return ctx.enter_context(nc.sbuf_tensor(name, shape, dt))

        dst_c = sb("dst_all", [P, SUPERS, TILES], I32)
        place = sb("place_all", [P, SUPERS, TILES])
        ends = sb("ends", [P, 4])
        beyond, most = sb("beyond", [P, 1]), sb("most", [P, 1])
        dst_in, steps, reduced = (ctx.enter_context(nc.semaphore(x)) for x in ("dst_all_in", "wide_steps", "wide_reduced"))
        block = ctx.enter_context(nc.Block())

        @block.sync
        def _(sp):
            sp.dma_start(dst_c[:, :, :].rearrange("p n t -> p (n t)"), ins["dst_cols"]).then_inc(dst_in, 16)

        @block.vector
        def _(dve):
            dve.wait_ge(dst_in, 16)
            nc.vector.tensor_tensor(place[:, :, :], dst_c[:, :, :], t["first"][:, :].unsqueeze(2).to_broadcast([P, SUPERS, TILES]),
                                    ALU.subtract).then_inc(steps, 1)
            dve.wait_ge(steps, 1)
            flat = place[:, :, :].rearrange("p n t -> p (n t)")
            nc.vector.tensor_reduce(ends[:, 0:1], flat, AXX, ALU.min).then_inc(steps, 1)
            nc.vector.tensor_reduce(ends[:, 1:2], flat, AXX, ALU.max).then_inc(steps, 1)
            dve.wait_ge(steps, 3)
            nc.vector.tensor_scalar(ends[:, 2:3], ends[:, 0:1], -1.0, None, ALU.mult).then_inc(steps, 1)
            nc.vector.tensor_scalar(ends[:, 3:4], ends[:, 1:2], float(WINDOW - 1), None, ALU.subtract).then_inc(steps, 1)
            dve.wait_ge(steps, 5)
            nc.vector.tensor_tensor(beyond[:, :], ends[:, 2:3], ends[:, 3:4], ALU.max).then_inc(steps, 1)
            dve.wait_ge(reduced, 1)
            nc.vector.tensor_scalar(t["wide"][:, :], most[:, :], 0.0, None, ALU.is_gt)

        @block.gpsimd
        def _(pool):
            pool.wait_ge(steps, 6)
            nc.gpsimd.partition_all_reduce(most[:, :], beyond[:, :], P, bass.bass_isa.ReduceOp.max).then_inc(reduced, 1)


def each_way(eng, t, program):
    flag = eng.value_load(t["wide"][0:1, 0:1], min_val=0, max_val=1)
    with eng.If(flag):
        program(True)
    with eng.Else():
        program(False)


def visits(eng, wide, n, slot, windows, carrier):
    if not wide:
        yield n, slot, None
        return
    eng.sem_inc(carrier, 1)
    with eng.Fori(0, windows // 2) as v:
        for s in range(2):
            yield n * windows + v * 2 + s, s, v * 2 + s


def message_pass(nc, t, ins, p_table, sums, SUPERS):
    dinv, ident, ones = t["dinv"], t["ident"], t["ones"]
    NP = dinv.shape[1]
    WINDOWS = NP // STEP
    carrier = t["carrier"]
    with ExitStack() as ctx:
        def sb(name, shape, dt=F32):
            return ctx.enter_context(nc.sbuf_tensor(name, shape, dt))

        src_b = sb("src_b", [P, 2, TILES, P], I32)
        dst_b = sb("dst_b", [P, 2, EDGES], I32)
        src_c = sb("src_c", [P, 2, TILES], I32)
        mixed = sb("mixed", [P, 2, EDGES])
        mixed_w = sb("mixed_w", [P, 2, FEATURES])
        pick = sb("pick", [P, 2, EDGES])
        window = sb("window", [P, 2, FEATURES])
        nodes_w = sb("nodes_w", [P, 2, 2])
        degree_c = sb("degree_c", [P, 2, 2])
        degree_lead = sb("degree_lead", [P, 2, LEAD])
        degree_main = sb("degree_main", [P, 2, P])
        lead = slice(EDGE_FEATURES, P)
        same = sb("same", [P, 2, TILES, P])
        marked = sb("marked", [P, TILES, P])
        offset = sb("offset", [P, TILES])
        moved = sb("moved", [P, TILES])
        rows = sb("rows", [P, 2, TILES, FEATURES])
        total = sb("total", [P, 2, TILES, FEATURES + 1])
        target = sb("target", [P, 2, TILES], I32)
        ps_rows = [ctx.enter_context(nc.psum_tensor(f"ps_rows{h}", [P, HALF, FEATURES], F32)) for h in range(2)]
        ps_total = [ctx.enter_context(nc.psum_tensor(f"ps_total{h}", [P, HALF, FEATURES], F32)) for h in range(2)]
        ps_degree = ctx.enter_context(nc.psum_tensor("ps_degree", [P, WINDOW], F32))
        sem = lambda name: ctx.enter_context(nc.semaphore(name))
        index_in = [sem(f"index_in{b}") for b in range(2)]
        attr_in = [sem(f"attr_in{b}") for b in range(2)]
        window_in = [sem(f"window_in{b}") for b in range(2)]
        index_free, attr_free, visited, weights_in = (sem(x) for x in ("index_free", "attr_free", "visited", "edge_weights_in"))
        nodes_ready, picks_ready, degree_ready = sem("nodes_ready"), sem("picks_ready"), sem("degree_ready")
        degree_summed, degree_added = sem("degree_summed"), sem("degree_added")
        same_ready, marked_ready, steps = sem("same_ready"), sem("marked_ready"), sem("steps")
        target_ready = sem("target_ready")
        rows_ready, total_done, total_ready = (sem(x) for x in ("rows_ready", "total_done", "total_ready"))
        total_free, issued = sem("total_free"), sem("issued")
        added = [sem(f"added{k}") for k in range(TABLES)]
        CREDIT = 4
        block = ctx.enter_context(nc.Block())

        @block.sync
        def _(sp):
            def program(wide):
                with sp.Fori(0, SUPERS // 2) as i:
                    for b in range(2):
                        n = i * 2 + b
                        sp.wait_ge(index_free, n + 1)
                        sp.dma_start(dst_b[:, b, :], ins["dst_flat"][:, bass.ds(n * EDGES, EDGES)].to_broadcast([P, EDGES])).then_inc(index_in[b], 16)
                        sp.dma_start(src_b[:, b, :, :].rearrange("p t e -> p (t e)"),
                                     ins["src_flat"][:, bass.ds(n * EDGES, EDGES)].to_broadcast([P, EDGES])).then_inc(index_in[b], 16)
                        sp.dma_start(src_c[:, b, :], ins["src_cols"][:, bass.ds(n * TILES, TILES)]).then_inc(index_in[b], 16)
                        sp.wait_ge(attr_free, n + 1)
                        sp.dma_start(mixed[0:EDGE_FEATURES, b, :], ins["attrT"][:, bass.ds(n * EDGES, EDGES)]).then_inc(attr_in[b], 16)
                        for m, s, w in visits(sp, wide, n, b, WINDOWS, carrier):
                            base = w * STEP if wide else sp.value_load(t["first_i"][0:1, bass.ds(n, 1)], min_val=0, max_val=NP - WINDOW)
                            sp.wait_ge(visited, m * 2 + 2)
                            if not wide:
                                sp.dma_start(mixed_w[lead, s, :], p_table[bass.ds(base, LEAD), :]).then_inc(window_in[s], 16)
                            sp.dma_start(window[:, s, :], p_table[bass.ds(base if wide else base + LEAD, P), :]).then_inc(window_in[s], 16)

            for b in range(2):
                sp.dma_start(mixed_w[0:EDGE_FEATURES, b, :], ins["W1a"][FEATURES:, :]).then_inc(weights_in, 16)
            each_way(sp, t, program)

        @block.vector
        def _(dve):
            def pick_out(wide, n, m, s, b, w):
                if wide:
                    nc.vector.tensor_scalar(nodes_w[:, s, 1:2], t["part_node"][:, 2:3], t["starts"][:, bass.ds(w, 1)], None, ALU.add).then_inc(nodes_ready, 1)
                else:
                    nc.vector.tensor_scalar(nodes_w[:, s, :], t["part_node"][:, 0:2], t["first"][:, bass.ds(n, 1)], None, ALU.add).then_inc(nodes_ready, 1)
                dve.wait_ge(nodes_ready, m + 1)
                dve.wait_ge(visited, m * 2 + 2)
                if not wide:
                    nc.vector.tensor_scalar(mixed[lead, s, :], dst_b[lead, b, :], nodes_w[lead, s, 0:1], 0.0, ALU.is_equal, ALU.add,
                                            accum_out=degree_c[lead, s, 0:1]).then_inc(picks_ready, 1)
                nc.vector.tensor_scalar(pick[:, s, :], dst_b[:, b, :], nodes_w[:, s, 1:2], 0.0, ALU.is_equal, ALU.add,
                                        accum_out=degree_c[:, s, 1:2]).then_inc(picks_ready, 1)

            def spread_degrees(wide, m, s):
                dve.wait_ge(picks_ready, m + 1 if wide else m * 2 + 2)
                if not wide:
                    nc.vector.tensor_scalar(degree_lead[lead, s, :], ident[lead, lead], degree_c[lead, s, 0:1], None, ALU.mult).then_inc(degree_ready, 1)
                nc.vector.tensor_scalar(degree_main[:, s, :], ident[:, :], degree_c[:, s, 1:2], None, ALU.mult).then_inc(degree_ready, 1)

            def find_targets(n, b):
                dve.wait_ge(same_ready, n + 1)
                nc.vector.tensor_tensor(marked[:, :, :], same[:, b, :, :],
                                        t["later"][:, :].unsqueeze(1).to_broadcast([P, TILES, P]), ALU.mult).then_inc(marked_ready, 1)
                nc.vector.tensor_scalar(offset[:, :], src_c[:, b, :], -1.0, t["spare"][:, 0:1], ALU.mult, ALU.add).then_inc(steps, 1)
                dve.wait_ge(marked_ready, n + 1)
                dve.wait_ge(total_free, n + 1)
                nc.vector.tensor_reduce(total[:, b, :, FEATURES], marked[:, :, :], AXX, ALU.add).then_inc(steps, 1)
                dve.wait_ge(steps, n * 3 + 2)
                nc.vector.scalar_tensor_tensor(out=moved[:, :], in0=total[:, b, :, FEATURES], scalar=LATER, in1=offset[:, :],
                                               op0=ALU.is_ge, op1=ALU.mult).then_inc(steps, 1)
                dve.wait_ge(steps, n * 3 + 3)
                nc.vector.tensor_tensor(target[:, b, :], moved[:, :], src_c[:, b, :], ALU.add).then_inc(target_ready, 1)

            def add_degrees(wide, m, base):
                dve.wait_ge(degree_summed, m + 1)
                dve.wait_ge(degree_added, m + 1)
                at, new = (bass.ds(base, STEP), ps_degree[:, LEAD:]) if wide else (bass.ds(base, WINDOW), ps_degree[:, :])
                nc.vector.tensor_tensor(dinv[:, at], dinv[:, at], new, ALU.add).then_inc(degree_added, 1)

            def program(wide):
                with dve.Fori(0, SUPERS // 2) as i:
                    for b in range(2):
                        n = i * 2 + b
                        dve.wait_ge(index_in[b], (i + 1) * 48)
                        if not wide:
                            pick_out(wide, n, n, b, b, None)
                            spread_degrees(wide, n, b)
                        else:
                            dve.wait_ge(attr_free, n + 1)
                        nc.vector.tensor_tensor(same[:, b, :, :], src_b[:, b, :, :],
                                                src_c[:, b, :].unsqueeze(2).to_broadcast([P, TILES, P]), ALU.is_equal).then_inc(same_ready, 1)
                        find_targets(n, b)
                        for m, s, w in visits(dve, wide, n, b, WINDOWS, carrier):
                            if wide:
                                pick_out(wide, n, m, s, b, w)
                                spread_degrees(wide, m, s)
                                add_degrees(wide, m, w * STEP)
                        dve.wait_ge(target_ready, n + 1)
                        dve.sem_inc(index_free, 1)
                        if not wide:
                            add_degrees(wide, n, dve.value_load(t["first_i"][0:1, bass.ds(n, 1)], min_val=0, max_val=NP - WINDOW))

            dve.sem_inc(index_free, 2)
            dve.sem_inc(degree_added, 1)
            each_way(dve, t, program)

        @block.tensor
        def _(pe):
            def edges_of(h, q):
                return slice((h * HALF + q) * P, (h * HALF + q + 1) * P)

            def from_both(h, b):
                for q in range(HALF):
                    e = edges_of(h, q)
                    nc.tensor.matmul(ps_rows[h][:, q, :], mixed[:, b, e], mixed_w[:, b, :], start=True, stop=False)
                    last = nc.tensor.matmul(ps_rows[h][:, q, :], pick[:, b, e], window[:, b, :], start=False, stop=True)
                last.then_inc(visited, 1)

            def from_attributes(h, b):
                for q in range(HALF):
                    nc.tensor.matmul(ps_rows[h][:, q, :], mixed[0:EDGE_FEATURES, b, edges_of(h, q)], mixed_w[0:EDGE_FEATURES, b, :],
                                     start=(q == 0), stop=False, skip_group_check=True)

            def from_window(h, s):
                for q in range(HALF):
                    last = nc.tensor.matmul(ps_rows[h][:, q, :], pick[:, s, edges_of(h, q)], window[:, s, :],
                                            start=False, stop=True, skip_group_check=True)
                last.then_inc(visited, 1)

            def sum_degrees(wide, m, s):
                pe.wait_ge(degree_ready, m + 1 if wide else m * 2 + 2)
                pe.wait_ge(degree_added, m + 1)
                if not wide:
                    nc.tensor.matmul(ps_degree[:, 0:LEAD], ones[lead, :], degree_lead[lead, s, :], start=True, stop=True)
                nc.tensor.matmul(ps_degree[:, LEAD:], ones[:, :], degree_main[:, s, :], start=True, stop=True).then_inc(degree_summed, 1)

            def program(wide):
                with pe.Fori(0, SUPERS // 2) as i:
                    for b in range(2):
                        n = i * 2 + b
                        pe.wait_ge(attr_in[b], (i + 1) * 16)
                        if wide:
                            for h in range(2):
                                pe.wait_ge(rows_ready, n * 2 + h + 1)
                                from_attributes(h, b)
                        for m, s, w in visits(pe, wide, n, b, WINDOWS, carrier):
                            pe.wait_ge(window_in[s], (n * (WINDOWS // 2) + (w - s) // 2) * 16 + 16 if wide else i * 32 + 32)
                            pe.wait_ge(picks_ready, m + 1 if wide else m * 2 + 2)
                            for h in range(2):
                                if wide:
                                    from_window(h, s)
                                else:
                                    pe.wait_ge(rows_ready, n * 2 + h + 1)
                                    from_both(h, b)
                                if h == 0:
                                    sum_degrees(wide, m, s)
                        pe.wait_ge(same_ready, n + 1)
                        for h in range(2):
                            pe.wait_ge(rows_ready, n * 2 + h + 3)
                            pe.wait_ge(total_ready, n * 2 + h + 1)
                            for q in range(HALF):
                                last = nc.tensor.matmul(ps_total[h][:, q, :], same[:, b, h * HALF + q, :], rows[:, b, h * HALF + q, :], start=True, stop=True)
                            last.then_inc(total_done, 1)
                        pe.wait_ge(total_done, n * 2 + 2)
                        pe.sem_inc(attr_free, 1)

            pe.sem_inc(attr_free, 2)
            pe.sem_inc(visited, CREDIT)
            pe.wait_ge(weights_in, 32)
            each_way(pe, t, program)

        @block.scalar
        def _(act):
            def program(wide):
                with act.Fori(0, SUPERS // 2) as i:
                    for b in range(2):
                        n = i * 2 + b
                        for h in range(2):
                            last = (n + 1) * WINDOWS - 1 if wide else n
                            act.wait_ge(visited, last * 2 + CREDIT + h + 1)
                            nc.scalar.activation(rows[:, b, h * HALF:(h + 1) * HALF, :], ps_rows[h][:, :, :], ACT.Relu).then_inc(rows_ready, 1)
                        act.wait_ge(total_free, n + 1)
                        for h in range(2):
                            act.wait_ge(total_done, n * 2 + h + 1)
                            nc.scalar.activation(total[:, b, h * HALF:(h + 1) * HALF, 0:FEATURES], ps_total[h][:, :, :], ACT.Copy).then_inc(total_ready, 1)

            act.sem_inc(rows_ready, 2)
            act.sem_inc(total_ready, 2)
            each_way(act, t, program)

        @block.gpsimd
        def _(pool):
            pool.sem_inc(total_free, 1)
            for k in range(TABLES):
                pool.dma_start(sums[k][NP + P - 1:, 0:1], ones[0:1, 0:1]).then_inc(added[k], 16)
            with pool.Fori(0, SUPERS // 2) as i:
                for b in range(2):
                    n = i * 2 + b
                    pool.wait_ge(target_ready, n + 1)
                    for q in range(TILES):
                        k = q % TABLES
                        if q % HALF == 0:
                            pool.wait_ge(total_ready, n * 2 + q // HALF + 3)
                        pool.wait_ge(added[k], (n * (TILES // TABLES) + q // TABLES) * 16 + 16)
                        pool.sem_inc(total_free if q == TABLES - 1 else issued, 1)
                        pool.indirect_dma_start(sums[k], bass.IndirectOffsetOnAxis(ap=target[:, b, q:q + 1], axis=0),
                                                total[:, b, q, :], None, compute_op=ALU.add).then_inc(added[k], 16)
            for k in range(TABLES):
                pool.wait_ge(added[k], SUPERS * (16 * TILES // TABLES) + 16)


def degree_roots(nc, dinv):
    with ExitStack() as ctx:
        rooted = ctx.enter_context(nc.semaphore("rooted"))
        block = ctx.enter_context(nc.Block())

        @block.scalar
        def _(act):
            nc.scalar.activation(dinv[:, :], dinv[:, :], ACT.Sqrt, bias=1.0).then_inc(rooted, 1)

        @block.vector
        def _(dve):
            dve.wait_ge(rooted, 1)
            nc.vector.reciprocal(dinv[:, :], dinv[:, :])


def pipeline(eng, chunks, depth, step):
    def at(k, slot, first, end):
        def live(d):
            if (first and k < d) or (end and k - d >= chunks):
                return None
            return k - d, (slot - d) % 2, (k - d - (slot - d) % 2) // 2
        return live

    for k in range(depth):
        step(k, at(k, k % 2, True, False))
    if chunks > depth:
        with eng.Fori(0, (chunks - depth) // 2) as i:
            for slot in range(2):
                k = i * 2 + slot + depth
                step(k, at(k, slot, False, False))
    for k in range(chunks, chunks + depth):
        step(k, at(k, k % 2, False, True))


def update_nodes(nc, t, ins, sums, x1_rows, g_table, NCHUNK):
    ident, dinv, acc = t["ident"], t["dinv"], t["acc"]
    b2a, lin0_b = t["cols"][:, 0:1], t["cols"][:, 1:2]
    spread = [P, QUARTERS, FEATURES]
    carrier = t["carrier"]
    with ExitStack() as ctx:
        def sb(name, shape, dt=F32):
            return ctx.enter_context(nc.sbuf_tensor(name, shape, dt))

        part = sb("part", [P, 2, TABLES, QUARTERS, FEATURES + 1])
        x_cols, x_rows = sb("x_cols", [P, 2, CHUNK]), sb("x_rows", [P, 2] + spread[1:])
        total01, total23 = sb("total01", [P, QUARTERS, FEATURES + 1]), sb("total23", [P, QUARTERS, FEATURES + 1])
        total = sb("total_n", [P, 2, QUARTERS, FEATURES + 1])
        x_bias = sb("x_bias", [P, 2] + spread[1:])
        count = sb("count", [P, 3, QUARTERS])
        scale_d, some_d = sb("scale_d", [P, 2] + spread[1:]), sb("some_d", [P, 2] + spread[1:])
        mean_c, agg_c, mid_c, x1_c, h_c, hs_c = (sb(x, [P, CHUNK]) for x in ("mean_c", "agg_c", "mid_c", "x1_c", "h_c", "hs_c"))
        res, x1 = sb("res", spread), sb("x1", [P, 2] + spread[1:])
        g_rows = sb("g_rows", [P, 2] + spread[1:])
        stats, moments, dev, inv, shift = norm_tiles(sb)
        pa, pb, pt, pl, pc, pd = (ctx.enter_context(nc.psum_tensor(x, spread, F32)) for x in ("pa", "pb", "pt", "pl", "pc", "pd"))
        flat = lambda ps: ps[:, :, :].rearrange("p q n -> p (q n)")
        sem = lambda name: ctx.enter_context(nc.semaphore(name))
        part_in, x_in, x1_stored, g_stored = ([sem(f"{x}{b}") for b in range(2)] for x in ("part_in", "nx_in", "x1_stored", "g_stored"))
        (pair01, pair23, biased, summed, clipped, inverted, diagonals, meaned, mean_ready, agged, agg_ready,
         mixed, mid_ready, outed, res_ready, stat, stat_seen, mom, dev_ready, inv_ready, shift_ready, x1_ready, turned, x1c_ready,
         lined, h_ready, hs_ready, projected, g_ready, acc_ready) = (sem(x) for x in (
            "pair01 pair23 biased summed clipped inverted diagonals meaned mean_ready agged agg_ready mixed "
            "mid_ready outed res_ready stat stat_seen mom dev_ready inv_ready shift_ready x1_ready turned x1c_ready lined h_ready "
            "hs_ready projected g_ready acc_ready").split())
        block = ctx.enter_context(nc.Block())

        @block.sync
        def _(sp):
            def step(k, live):
                if live(0):
                    c, b, _ = live(0)
                    at = bass.ds(c * CHUNK, CHUNK)
                    sp.wait_ge(summed, c + 1)
                    sp.wait_ge(pair23, c + 1)
                    for j in range(TABLES):
                        sp.dma_start(part[:, b, j, :, :], sums[j][at, :].rearrange("(q p) n -> p q n", p=P)).then_inc(part_in[b], 16)
                    sp.wait_ge(mid_ready, c + 1)
                    sp.wait_ge(biased, c + 1)
                    sp.sem_inc(carrier, 1)
                    sp.dma_start(x_cols[:, b, :], ins["xT"][:, at]).then_inc(x_in[b], 16)
                    sp.dma_start(x_rows[:, b, :, :], ins["x"][at, :].rearrange("(q p) n -> p q n", p=P)).then_inc(x_in[b], 16)
                if live(3):
                    c, b, _ = live(3)
                    sp.wait_ge(g_ready, c + 2)
                    sp.sem_inc(carrier, 1)
                    sp.dma_start(g_table[bass.ds(c * CHUNK, CHUNK), :].rearrange("(q p) n -> p q n", p=P),
                                 g_rows[:, b, :, :]).then_inc(g_stored[b], 16)

            pipeline(sp, NCHUNK, 4, step)
            for b in range(2):
                sp.wait_ge(g_stored[b], NCHUNK // 2 * 16 + 16)

        @block.gpsimd
        def _(pool):
            def step(k, live):
                if live(0):
                    c, b, used = live(0)
                    pool.wait_ge(part_in[b], used * 16 * TABLES + 16 * TABLES)
                    pool.wait_ge(summed, c + 2)
                    nc.gpsimd.tensor_tensor(total23[:, :, :], part[:, b, 2, :, :], part[:, b, 3, :, :], ALU.add).then_inc(pair23, 1)
                    pool.wait_ge(x_in[b], used * 32 + 32)
                    pool.wait_ge(res_ready, c + 1)
                    nc.gpsimd.tensor_tensor(x_bias[:, b, :, :], x_rows[:, b, :, :], t["b2b_r"][:, :].unsqueeze(1).to_broadcast(spread),
                                            ALU.add).then_inc(biased, 1)

            pool.sem_inc(pair23, 2)
            pool.sem_inc(biased, 2)
            pipeline(pool, NCHUNK, 4, step)

        @block.vector
        def _(dve):
            def step(k, live):
                if live(2):
                    c, b, _ = live(2)
                    dve.wait_ge(res_ready, c + 3)
                    norm_moments(nc, dve, c, res, stats, moments, stat, stat_seen, mom)
                if live(0):
                    c, b, used = live(0)
                    dve.wait_ge(part_in[b], used * 16 * TABLES + 16 * TABLES)
                    nc.vector.tensor_tensor(total01[:, :, :], part[:, b, 0, :, :], part[:, b, 1, :, :], ALU.add).then_inc(pair01, 1)
                    dve.wait_ge(pair01, c + 1)
                    dve.wait_ge(pair23, c + 3)
                    dve.wait_ge(agg_ready, c + 1)
                    nc.vector.tensor_tensor(total[:, b, :, :], total01[:, :, :], total23[:, :, :], ALU.add).then_inc(summed, 1)
                    dve.wait_ge(summed, c + 3)
                    nc.vector.tensor_scalar(count[:, 0, :], total[:, b, :, FEATURES], 1.0, None, ALU.max).then_inc(clipped, 1)
                    nc.vector.tensor_scalar(count[:, 2, :], total[:, b, :, FEATURES], 1.0, None, ALU.min).then_inc(clipped, 1)
                    dve.wait_ge(clipped, c * 2 + 2)
                    nc.vector.reciprocal(count[:, 1, :], count[:, 0, :]).then_inc(inverted, 1)
                    dve.wait_ge(inverted, c + 1)
                    for tile, j in ((scale_d, 1), (some_d, 2)):
                        nc.vector.tensor_tensor(tile[:, b, :, :], ident[:, :].unsqueeze(1).to_broadcast(spread),
                                                count[:, j, :].unsqueeze(2).to_broadcast(spread), ALU.mult).then_inc(diagonals, 1)
                if live(3):
                    c, b, _ = live(3)
                    dve.wait_ge(h_ready, c + 1)
                    nc.vector.tensor_tensor(hs_c[:, :], h_c[:, :], dinv[:, bass.ds(c * CHUNK, CHUNK)], ALU.mult).then_inc(hs_ready, 1)
                if live(2):
                    c, b, used = live(2)
                    dve.wait_ge(dev_ready, c + 1)
                    nc.vector.reciprocal(inv[:, :], dev[:, :]).then_inc(inv_ready, 1)
                    dve.wait_ge(inv_ready, c + 1)
                    dve.wait_ge(x1_stored[b], used * 16 + 16)
                    dve.wait_ge(x1c_ready, c + 1)
                    for q in range(QUARTERS):
                        nc.vector.tensor_scalar(x1[:, b, q, :], res[:, q, :], moments[:, q, 0:1], inv[:, q:q + 1],
                                                ALU.subtract, ALU.mult).then_inc(x1_ready, 1)
                if live(3):
                    c, b, _ = live(3)
                    dve.wait_ge(projected, c + 1)
                    nc.vector.tensor_scalar(acc[:, bass.ds(c * CHUNK, CHUNK)], flat(pd), 0.0, None, ALU.add).then_inc(acc_ready, 1)
                if live(1):
                    c, b, _ = live(1)
                    dve.wait_ge(outed, c + 1)
                    dve.wait_ge(biased, c + 3)
                    dve.wait_ge(x1_ready, c * QUARTERS + 1)
                    nc.vector.tensor_tensor(res[:, :, :], pb[:, :, :], x_bias[:, b, :, :], ALU.add).then_inc(res_ready, 1)

            dve.sem_inc(summed, 2)
            dve.sem_inc(res_ready, 2)
            dve.sem_inc(acc_ready, 1)
            dve.sem_inc(x1_ready, 1)
            pipeline(dve, NCHUNK, 4, step)

        @block.tensor
        def _(pe):
            def step(k, live):
                if live(1):
                    c, b, _ = live(1)
                    pe.wait_ge(diagonals, c * 2 + 2)
                    for q in range(QUARTERS):
                        last = nc.tensor.matmul(pa[:, q, :], total[:, b, q, 0:FEATURES], scale_d[:, b, q, :], start=True, stop=True)
                    last.then_inc(meaned, 1)
                if live(3):
                    c, _, _ = live(3)
                    pe.wait_ge(x1c_ready, c + 3)
                    nc.tensor.matmul(flat(pl), t["lin0"][:, :], x1_c[:, :], start=True, stop=True).then_inc(lined, 1)
                if live(1):
                    c, b, _ = live(1)
                    pe.wait_ge(mean_ready, c + 1)
                    pe.wait_ge(res_ready, c + 2)
                    for q in range(QUARTERS):
                        nc.tensor.matmul(pb[:, q, :], t["w1b"][:, :], mean_c[:, q * P:(q + 1) * P], start=True, stop=False)
                        last = nc.tensor.matmul(pb[:, q, :], t["b1b_r"][:, :], some_d[:, b, q, :], start=False, stop=True)
                    last.then_inc(agged, 1)
                if live(3):
                    c, _, _ = live(3)
                    pe.wait_ge(hs_ready, c + 1)
                    pe.wait_ge(g_ready, c + 1)
                    pe.wait_ge(acc_ready, c + 1)
                    project_chunk(nc, t["conv"][:, 0, :], hs_c[:, :], pc, flat(pd)).then_inc(projected, 1)
                if live(1):
                    c, b, used = live(1)
                    pe.wait_ge(agg_ready, c + 3)
                    pe.wait_ge(x_in[b], used * 32 + 32)
                    nc.tensor.matmul(flat(pa), t["w2x"][:, :], x_cols[:, b, :], start=True, stop=False)
                    nc.tensor.matmul(flat(pa), t["w2g"][:, :], agg_c[:, :], start=False, stop=True).then_inc(mixed, 1)
                if live(2):
                    c, b, _ = live(2)
                    pe.wait_ge(x1_ready, c * QUARTERS + QUARTERS + 1)
                    pe.wait_ge(x1c_ready, c + 2)
                    for q in range(QUARTERS):
                        last = nc.tensor.transpose(pt[:, q, :], x1[:, b, q, :], ident[:, :])
                    last.then_inc(turned, 1)
                if live(1):
                    c, _, _ = live(1)
                    pe.wait_ge(mid_ready, c + 3)
                    for q in range(QUARTERS):
                        last = nc.tensor.matmul(pb[:, q, :], mid_c[:, q * P:(q + 1) * P], t["w2b"][:, :], start=True, stop=True)
                    last.then_inc(outed, 1)

            pipeline(pe, NCHUNK, 4, step)

        @block.scalar
        def _(act):
            def step(k, live):
                if live(1):
                    c, _, _ = live(1)
                    act.wait_ge(meaned, c + 1)
                    nc.scalar.activation(mean_c[:, :], flat(pa), ACT.Copy).then_inc(mean_ready, 1)
                if live(2):
                    c, _, _ = live(2)
                    act.wait_ge(mom, c * QUARTERS + QUARTERS)
                    nc.scalar.activation(dev[:, :], moments[:, :, 1], ACT.Sqrt, bias=t["eps"][:, 0:1]).then_inc(dev_ready, 1)
                if live(3):
                    c, _, _ = live(3)
                    act.wait_ge(lined, c + 1)
                    nc.scalar.activation(h_c[:, :], flat(pl), ACT.Relu, bias=lin0_b).then_inc(h_ready, 1)
                if live(1):
                    c, b, used = live(1)
                    act.wait_ge(agged, c + 1)
                    nc.scalar.activation(agg_c[:, :], flat(pb), ACT.Copy).then_inc(agg_ready, 1)
                    act.wait_ge(mixed, c + 1)
                    nc.scalar.activation(mid_c[:, :], flat(pa), ACT.Relu, bias=b2a).then_inc(mid_ready, 1)
                if live(3):
                    c, b, used = live(3)
                    act.wait_ge(projected, c + 1)
                    act.wait_ge(g_stored[b], used * 16 + 16)
                    nc.scalar.activation(g_rows[:, b, :, :], pc[:, :, :], ACT.Copy).then_inc(g_ready, 1)
                if live(2):
                    c, b, _ = live(2)
                    act.wait_ge(x1_ready, c * QUARTERS + QUARTERS + 1)
                    act.dma_start(x1_rows[bass.ds(c * CHUNK, CHUNK), :].rearrange("(q p) n -> p q n", p=P),
                                  x1[:, b, :, :]).then_inc(x1_stored[b], 16)
                    act.wait_ge(turned, c + 1)
                    nc.scalar.activation(x1_c[:, :], flat(pt), ACT.Copy).then_inc(x1c_ready, 1)

            act.sem_inc(mid_ready, 2)
            act.sem_inc(agg_ready, 2)
            act.sem_inc(x1c_ready, 2)
            act.sem_inc(g_ready, 1)
            for b in range(2):
                act.sem_inc(x1_stored[b], 16)
                act.sem_inc(g_stored[b], 16)
            pipeline(act, NCHUNK, 4, step)
            for b in range(2):
                act.wait_ge(x1_stored[b], NCHUNK // 2 * 16 + 16)


def norm_tiles(sb):
    return (sb("stats", [P, QUARTERS, 6]), sb("moments", [P, QUARTERS, 2]), sb("dev", [P, QUARTERS]), sb("inv", [P, QUARTERS]),
            sb("shift", [P, QUARTERS]))


def norm_moments(nc, dve, c, res, stats, moments, stat, stat_seen, mom):
    for q in range(QUARTERS):
        nc.vector.bn_stats(stats[:, q, :], res[:, q, :]).then_inc(stat, 1)
    dve.wait_ge(stat, c * QUARTERS + QUARTERS)
    dve.sem_inc(stat_seen, 1)
    for q in range(QUARTERS):
        nc.vector.bn_aggr(moments[:, q, :], stats[:, q, :]).then_inc(mom, 1)
    dve.wait_ge(mom, c * QUARTERS + QUARTERS)


def project_chunk(nc, weights, hs_c, ps_rows, ps_cols):
    for q in range(QUARTERS):
        nc.tensor.matmul(ps_rows[:, q, :], hs_c[:, q * P:(q + 1) * P], weights, start=True, stop=True)
    return nc.tensor.matmul(ps_cols, weights, hs_c, start=True, stop=True)


def convolve_semaphores(sem):
    one = "dst_free rows_used placed picked acc_added summed gathers_issued"
    return {**{x: sem(x) for x in one.split()}, "src_in": [sem(f"src_in{r}") for r in range(RING)],
            "dst_in": [sem(f"dst_in{b}") for b in range(2)], "rows_in": [sem(f"rows_in{r}") for r in range(RING)]}


def convolve(nc, t, ins, g_table, SUPERS, layer, sems):
    acc = t["acc"]
    NP = acc.shape[1]
    WINDOWS = NP // STEP
    carrier = t["carrier"]
    with ExitStack() as ctx:
        def sb(name, shape, dt=F32):
            return ctx.enter_context(nc.sbuf_tensor(f"{name}{layer}", shape, dt))

        src_c, dst_c = sb("gsrc", [P, RING, TILES], I32), sb("gdst", [P, 2, TILES], I32)
        place = sb("place", [P, 2, TILES])
        pick = sb("gpick", [P, 2, TILES, WINDOW])
        rows = sb("grows", [P, RING, TILES, FEATURES])
        ps = [ctx.enter_context(nc.psum_tensor(f"gps{layer}_{b}", [P, WINDOW], F32)) for b in range(2)]
        src_in, dst_in, rows_in = sems["src_in"], sems["dst_in"], sems["rows_in"]
        dst_free, rows_used, placed, picked, added, summed, issued = (
            sems[x] for x in "dst_free rows_used placed picked acc_added summed gathers_issued".split())
        done = layer * SUPERS
        block = ctx.enter_context(nc.Block())

        @block.sync
        def _(sp):
            with sp.Fori(0, SUPERS // RING) as i:
                for r in range(RING):
                    n = i * RING + r + done
                    at = bass.ds((i * RING + r) * TILES, TILES)
                    sp.wait_ge(rows_used, n + 1)
                    sp.dma_start(src_c[:, r, :], ins["src_cols"][:, at]).then_inc(src_in[r], 16)
                    sp.wait_ge(dst_free, n + 1)
                    sp.dma_start(dst_c[:, r % 2, :], ins["dst_cols"][:, at]).then_inc(dst_in[r % 2], 16)

        @block.gpsimd
        def _(pool):
            with pool.Fori(0, SUPERS // RING) as i:
                for r in range(RING):
                    pool.wait_ge(src_in[r], (i + done // RING + 1) * 16)
                    pool.sem_inc(issued, 1)
                    for q in range(TILES):
                        pool.indirect_dma_start(rows[:, r, q, :], None, g_table,
                                                bass.IndirectOffsetOnAxis(ap=src_c[:, r, q:q + 1], axis=0)).then_inc(rows_in[r], 16)

        @block.vector
        def _(dve):
            def pick_out(local, m, s, b, w):
                dve.wait_ge(summed, m + 1)
                start, span = (t["first"][:, bass.ds(local, 1)], WINDOW) if w is None else (t["starts"][:, bass.ds(w, 1)], STEP)
                nc.vector.tensor_tensor(place[:, s, :], dst_c[:, b, :], start.to_broadcast([P, TILES]), ALU.subtract).then_inc(placed, 1)
                dve.wait_ge(placed, m + 1)
                for q in range(TILES):
                    last = nc.vector.tensor_scalar(pick[:, s, q, 0:span], t["iota_w"][:, 0:span], place[:, s, q:q + 1], None, ALU.is_equal)
                last.then_inc(picked, 1)

            def add_sums(m, s, base, span):
                dve.wait_ge(summed, m + 3)
                dve.wait_ge(added, m + 2)
                nc.vector.tensor_tensor(acc[:, bass.ds(base, span)], acc[:, bass.ds(base, span)], ps[s][:, 0:span], ALU.add).then_inc(added, 1)

            def program(wide):
                with dve.Fori(0, SUPERS // RING) as i:
                    for r in range(RING):
                        local, b = i * RING + r, r % 2
                        n = local + done
                        dve.wait_ge(dst_in[b], (i * (RING // 2) + done // 2 + r // 2 + 1) * 16)
                        for m, s, w in visits(dve, wide, n, b, WINDOWS, carrier):
                            pick_out(local, m, s, b, w)
                            if wide:
                                add_sums(m, s, w * STEP, STEP)
                        dve.sem_inc(dst_free, 1)
                        if not wide:
                            add_sums(n, b, dve.value_load(t["first_i"][0:1, bass.ds(local, 1)], min_val=0, max_val=NP - WINDOW), WINDOW)

            if layer == 0:
                dve.sem_inc(dst_free, 2)
            each_way(dve, t, program)

        @block.tensor
        def _(pe):
            def program(wide):
                span = STEP if wide else WINDOW
                with pe.Fori(0, SUPERS // RING) as i:
                    for r in range(RING):
                        local, b = i * RING + r, r % 2
                        n = local + done
                        pe.wait_ge(rows_in[r], (i + done // RING + 1) * 16 * TILES)
                        for m, s, w in visits(pe, wide, n, b, WINDOWS, carrier):
                            pe.wait_ge(picked, m + 1)
                            pe.wait_ge(added, m + 1)
                            for q in range(TILES):
                                last = nc.tensor.matmul(ps[s][:, 0:span], rows[:, r, q, :], pick[:, s, q, 0:span], start=(q == 0), stop=(q == TILES - 1))
                            last.then_inc(summed, 1)
                        last_visit = (n + 1) * WINDOWS - 1 if wide else n
                        pe.wait_ge(summed, last_visit + 3)
                        pe.sem_inc(rows_used, 1)

            if layer == 0:
                pe.sem_inc(summed, 2)
                pe.sem_inc(rows_used, RING)
                pe.sem_inc(added, 2)
            each_way(pe, t, program)


def project_semaphores(sem):
    return {**{x: sem(x + "_p") for x in "scaled h_ready hs_ready projected g_ready acc_ready".split()},
            "g_stored": [sem(f"g_stored_p{b}") for b in range(2)]}


def project(nc, t, g_table, NCHUNK, layer, sems):
    acc, dinv = t["acc"], t["dinv"]
    spread = [P, QUARTERS, FEATURES]
    carrier = t["carrier"]
    with ExitStack() as ctx:
        def sb(name, shape, dt=F32):
            return ctx.enter_context(nc.sbuf_tensor(f"{name}_p{layer}", shape, dt))

        t_c, h_c, hs_c, g_rows = sb("t_c", [P, 2, CHUNK]), sb("h_c", [P, 2, CHUNK]), sb("hs_c", [P, 2, CHUNK]), sb("g_rows", [P, 2] + spread[1:])
        pr = [ctx.enter_context(nc.psum_tensor(f"pr{layer}_{b}", spread, F32)) for b in range(2)]
        pc = [ctx.enter_context(nc.psum_tensor(f"pc{layer}_{b}", [P, CHUNK], F32)) for b in range(2)]
        scaled, h_ready, hs_ready, projected, g_ready, acc_ready, g_stored = (
            sems[x] for x in "scaled h_ready hs_ready projected g_ready acc_ready g_stored".split())
        done = layer * NCHUNK
        block = ctx.enter_context(nc.Block())

        @block.vector
        def _(dve):
            def step(k, live):
                if live(0):
                    c, b, _ = live(0)
                    at = bass.ds(c * CHUNK, CHUNK)
                    dve.wait_ge(h_ready, c + done + 1)
                    nc.vector.tensor_tensor(t_c[:, b, :], acc[:, at], dinv[:, at], ALU.mult).then_inc(scaled, 1)
                if live(1):
                    c, b, _ = live(1)
                    dve.wait_ge(h_ready, c + done + 3)
                    dve.wait_ge(projected, c + done + 1)
                    nc.vector.tensor_tensor(hs_c[:, b, :], h_c[:, b, :], dinv[:, bass.ds(c * CHUNK, CHUNK)], ALU.mult).then_inc(hs_ready, 1)
                if live(2):
                    c, b, _ = live(2)
                    dve.wait_ge(projected, c + done + 3)
                    nc.vector.tensor_scalar(acc[:, bass.ds(c * CHUNK, CHUNK)], pc[b][:, :], 0.0, None, ALU.add).then_inc(acc_ready, 1)

            if layer == 0:
                dve.sem_inc(acc_ready, 2)
                dve.sem_inc(hs_ready, 2)
            pipeline(dve, NCHUNK, 2, step)

        @block.scalar
        def _(act):
            def step(k, live):
                if live(0):
                    c, b, _ = live(0)
                    act.wait_ge(scaled, c + done + 1)
                    act.wait_ge(hs_ready, c + done + 1)
                    nc.scalar.activation(h_c[:, b, :], t_c[:, b, :], ACT.Relu, bias=t["bn_b"][:, layer:layer + 1],
                                         scale=t["bn_s"][:, layer:layer + 1]).then_inc(h_ready, 1)
                if live(2):
                    c, b, used = live(2)
                    act.wait_ge(projected, c + done + 3)
                    act.wait_ge(g_stored[b], (used + done // 2) * 16 + 16)
                    nc.scalar.activation(g_rows[:, b, :, :], pr[b][:, :, :], ACT.Copy).then_inc(g_ready, 1)

            if layer == 0:
                act.sem_inc(h_ready, 2)
                act.sem_inc(g_ready, 2)
                for b in range(2):
                    act.sem_inc(g_stored[b], 16)
            pipeline(act, NCHUNK, 2, step)

        @block.tensor
        def _(pe):
            def step(k, live):
                if live(1):
                    c, b, _ = live(1)
                    pe.wait_ge(hs_ready, c + done + 3)
                    pe.wait_ge(acc_ready, c + done + 1)
                    pe.wait_ge(g_ready, c + done + 1)
                    project_chunk(nc, t["conv"][:, layer + 1, :], hs_c[:, b, :], pr[b], pc[b][:, :]).then_inc(projected, 1)

            if layer == 0:
                pe.sem_inc(projected, 2)
            pipeline(pe, NCHUNK, 2, step)

        @block.sync
        def _(sp):
            def step(k, live):
                if live(2):
                    c, b, _ = live(2)
                    sp.wait_ge(g_ready, c + done + 3)
                    sp.sem_inc(carrier, 1)
                    sp.dma_start(g_table[bass.ds(c * CHUNK, CHUNK), :].rearrange("(q p) n -> p q n", p=P), g_rows[:, b, :, :]).then_inc(g_stored[b], 16)

            pipeline(sp, NCHUNK, 2, step)
            for b in range(2):
                sp.wait_ge(g_stored[b], (done + NCHUNK) // 2 * 16 + 16)


def finish(nc, t, x1_rows, out, NCHUNK):
    acc, dinv = t["acc"], t["dinv"]
    spread = [P, QUARTERS, FEATURES]
    layer = LAYERS - 1
    carrier = t["carrier"]
    with ExitStack() as ctx:
        def sb(name, shape, dt=F32):
            return ctx.enter_context(nc.sbuf_tensor(f"{name}_f", shape, dt))

        t_c, h_c = sb("t_c", [P, 2, CHUNK]), sb("h_c", [P, 2, CHUNK])
        x1, x1_bias = sb("x1", [P, 2] + spread[1:]), sb("x1_bias", [P, 2] + spread[1:])
        res, y = sb("res", [P, 2] + spread[1:]), sb("y", [P, 2] + spread[1:])
        stats, moments, dev, inv, shift = norm_tiles(sb)
        ps = [ctx.enter_context(nc.psum_tensor(f"ps_f{b}", spread, F32)) for b in range(2)]
        sem = lambda name: ctx.enter_context(nc.semaphore(f"{name}_f"))
        x1_in = [sem(f"x1_in{b}") for b in range(2)]
        stored = [sem(f"stored{b}") for b in range(2)]
        scaled, h_ready, biased, lined, res_ready, stat, stat_seen, mom, dev_ready, inv_ready, shift_ready, y_ready = (
            sem(x) for x in "scaled h_ready biased lined res_ready stat stat_seen mom dev_ready inv_ready shift_ready y_ready".split())
        block = ctx.enter_context(nc.Block())

        @block.sync
        def _(sp):
            def step(k, live):
                if live(0):
                    c, b, _ = live(0)
                    sp.wait_ge(biased, c + 1)
                    sp.sem_inc(carrier, 1)
                    sp.dma_start(x1[:, b, :, :], x1_rows[bass.ds(c * CHUNK, CHUNK), :].rearrange("(q p) n -> p q n", p=P)).then_inc(x1_in[b], 16)
                if live(2):
                    c, b, _ = live(2)
                    sp.wait_ge(y_ready, c * QUARTERS + QUARTERS + 1)
                    sp.sem_inc(carrier, 1)
                    sp.dma_start(out[bass.ds(c * CHUNK, CHUNK), :].rearrange("(q p) n -> p q n", p=P), y[:, b, :, :]).then_inc(stored[b], 16)

            pipeline(sp, NCHUNK, 2, step)
            for b in range(2):
                sp.wait_ge(stored[b], NCHUNK // 2 * 16 + 16)

        @block.gpsimd
        def _(pool):
            def step(k, live):
                if live(0):
                    c, b, used = live(0)
                    at = bass.ds(c * CHUNK, CHUNK)
                    pool.wait_ge(h_ready, c + 1)
                    nc.gpsimd.tensor_tensor(t_c[:, b, :], acc[:, at], dinv[:, at], ALU.mult).then_inc(scaled, 1)
                    pool.wait_ge(x1_in[b], used * 16 + 16)
                    pool.wait_ge(res_ready, c + 1)
                    nc.gpsimd.tensor_tensor(x1_bias[:, b, :, :], x1[:, b, :, :], t["lin1b_r"][:, :].unsqueeze(1).to_broadcast(spread),
                                            ALU.add).then_inc(biased, 1)

            pool.sem_inc(biased, 2)
            pipeline(pool, NCHUNK, 2, step)

        @block.vector
        def _(dve):
            def step(k, live):
                if live(2):
                    c, b, _ = live(2)
                    dve.wait_ge(dev_ready, c + 1)
                    dve.wait_ge(y_ready, c * QUARTERS + 1)
                    nc.vector.reciprocal(inv[:, :], dev[:, :]).then_inc(inv_ready, 1)
                    dve.wait_ge(inv_ready, c + 1)
                    nc.vector.scalar_tensor_tensor(out=shift[:, :], in0=moments[:, :, 0], scalar=-1.0, in1=inv[:, :],
                                                   op0=ALU.mult, op1=ALU.mult).then_inc(shift_ready, 1)
                if live(1):
                    c, b, _ = live(1)
                    dve.wait_ge(lined, c + 1)
                    dve.wait_ge(biased, c + 3)
                    dve.wait_ge(y_ready, c * QUARTERS - QUARTERS + 1) if not isinstance(c, int) or c > 1 else None
                    nc.vector.tensor_tensor(res[:, b, :, :], ps[b][:, :, :], x1_bias[:, b, :, :], ALU.add).then_inc(res_ready, 1)
                    dve.wait_ge(res_ready, c + 3)
                    if not isinstance(c, int) or c > 0:
                        dve.wait_ge(shift_ready, c)
                    norm_moments(nc, dve, c, res[:, b, :, :], stats, moments, stat, stat_seen, mom)

            dve.sem_inc(res_ready, 2)
            pipeline(dve, NCHUNK, 2, step)

        @block.tensor
        def _(pe):
            def step(k, live):
                if live(0):
                    c, b, _ = live(0)
                    pe.wait_ge(h_ready, c + 3)
                    pe.wait_ge(res_ready, c + 1)
                    for q in range(QUARTERS):
                        last = nc.tensor.matmul(ps[b][:, q, :], h_c[:, b, q * P:(q + 1) * P], t["lin1"][:, :], start=True, stop=True)
                    last.then_inc(lined, 1)

            pipeline(pe, NCHUNK, 2, step)

        @block.scalar
        def _(act):
            def step(k, live):
                if live(0):
                    c, b, _ = live(0)
                    act.wait_ge(scaled, c + 1)
                    if not isinstance(c, int) or c > 1:
                        act.wait_ge(lined, c - 1)
                    nc.scalar.activation(h_c[:, b, :], t_c[:, b, :], ACT.Relu, bias=t["bn_b"][:, layer:layer + 1],
                                         scale=t["bn_s"][:, layer:layer + 1]).then_inc(h_ready, 1)
                if live(1):
                    c, _, _ = live(1)
                    act.wait_ge(mom, c * QUARTERS + QUARTERS)
                    nc.scalar.activation(dev[:, :], moments[:, :, 1], ACT.Sqrt, bias=t["eps"][:, 0:1]).then_inc(dev_ready, 1)
                if live(2):
                    c, b, used = live(2)
                    act.wait_ge(shift_ready, c + 1)
                    act.wait_ge(stored[b], used * 16 + 16)
                    for q in range(QUARTERS):
                        nc.scalar.activation(y[:, b, q, :], res[:, b, q, :], ACT.Identity, bias=shift[:, q:q + 1],
                                             scale=inv[:, q:q + 1]).then_inc(y_ready, 1)

            act.sem_inc(h_ready, 2)
            act.sem_inc(y_ready, 1)
            for b in range(2):
                act.sem_inc(stored[b], 16)
            pipeline(act, NCHUNK, 2, step)


_L0, _L1 = "L0_gnn_", "L1_gnn_"


def kernel(**inputs):
    import concourse.bacc as bacc
    from concourse.bass_utils import run_bass_kernel_spmd

    a = {k: np.asarray(v) for k, v in inputs.items()}
    nodes, edges = a["x"].shape[0], a["src"].shape[0]
    NP, SUPERS = sizes(nodes, edges)
    EP = SUPERS * EDGES

    def padded(v, rows, fill=0):
        return np.concatenate([v, np.full((rows - v.shape[0],) + v.shape[1:], fill, v.dtype)])

    x, src, dst = padded(a["x"], NP), padded(a["src"], EP, nodes), padded(a["dst"], EP, nodes)
    per_layer = [a[_L1 + k] for k in ("conv_b", "bn_gamma", "bn_beta", "bn_mean", "bn_var")]
    arrays = {
        "x": x, "xT": np.ascontiguousarray(x.T), "attrT": np.ascontiguousarray(padded(a["edge_attr_64"], EP).T),
        "src_flat": src.reshape(1, EP), "dst_flat": dst.reshape(1, EP),
        "src_cols": np.ascontiguousarray(src.reshape(-1, P).T), "dst_cols": np.ascontiguousarray(dst.reshape(-1, P).T),
        "first": np.ascontiguousarray(dst.reshape(SUPERS, EDGES)[:, 0]).reshape(1, SUPERS),
        "cols": np.ascontiguousarray(np.concatenate([a[_L0 + "b2a"][None], a[_L1 + "lin0_b"][None], *per_layer]).T),
        "lin0_w": a[_L1 + "lin0_w"], "lin1_w": a[_L1 + "lin1_w"], "lin1_b": a[_L1 + "lin1_b"], "conv_w": a[_L1 + "conv_w"],
        **{k: a[_L0 + k] for k in ("W1a", "b1a", "W1b", "b1b", "W2a", "W2b", "b2b")},
    }
    arrays = {f"in_{k}": v for k, v in arrays.items()}
    nc = bacc.Bacc("TRN2", target_bir_lowering=False, num_devices=1)
    ins = {k[3:]: nc.dram_tensor(k, v.shape, mybir.dt.from_np(v.dtype), kind="ExternalInput").ap() for k, v in arrays.items()}
    out = nc.dram_tensor("out", (NP, FEATURES), F32, kind="ExternalOutput").ap()
    build(nc, nodes, edges, ins, out)
    r = run_bass_kernel_spmd(nc, [arrays], core_ids=[0])
    return r.results[0]["out"][:nodes]
```

```python
from contextlib import ExitStack

import numpy as np

import concourse.bass as bass
from concourse import mybir

ALU = mybir.AluOpType
ACT = mybir.ActivationFunctionType
AXX = mybir.AxisListType.X
F32 = mybir.dt.float32
I32 = mybir.dt.int32
I16 = mybir.dt.int16

P = 128
FEATURES = 128
EDGE_FEATURES = 64
TILES = 8
EDGES = TILES * P
HALF = TILES // 2
CHUNK = 512
QUARTERS = CHUNK // P
LEAD = P - EDGE_FEATURES
WINDOW = LEAD + P
STEP = P
TABLES = 4
EPS = 1e-5
LAYERS = 3
GROUPS = [range(q, min(q + 3, TILES)) for q in range(0, TILES, 3)]
ZEROS = 1536
EARLY = 4
FEW = 3
RING = 4


def sizes(nodes, edges):
    chunks = -(-(nodes + 1 + WINDOW) // CHUNK)
    supers = -(-edges // EDGES)
    return (chunks + chunks % 2) * CHUNK, supers + -supers % RING


def build(nc, nodes, edges, ins, out):
    NP, SUPERS = sizes(nodes, edges)
    NCHUNK = NP // CHUNK
    ROWW = FEATURES + 1
    TROWS = NP + P
    p_table = nc.dram_tensor("p_table", [NP, FEATURES], F32, kind="Internal").ap()
    g_tables = [nc.dram_tensor(f"g_table{k}", [NP, FEATURES], F32, kind="Internal").ap() for k in range(2)]
    assert NP < 1 << 15
    index16 = nc.dram_tensor("index16", [SUPERS, 2, EDGES], I16, kind="Internal").ap()
    x1_rows = nc.dram_tensor("x1_rows", [NP, FEATURES], F32, kind="Internal").ap()
    dinv_row = nc.dram_tensor("dinv_row", [1, NP], F32, kind="Internal").ap()
    sums = [nc.dram_tensor(f"sums{k}", [TROWS, ROWW], F32, kind="Internal").ap() for k in range(TABLES)]

    whole = ExitStack()
    with whole:
        def sb(name, shape, dt=F32):
            return whole.enter_context(nc.sbuf_tensor(name, shape, dt))

        sem = lambda name: whole.enter_context(nc.semaphore(name))
        carrier = sem("carrier")

        acc = sb("acc", [P, NP])
        dinv = sb("dinv", [P, NP])
        ident = sb("ident", [P, P])
        ones = sb("ones", [P, P])
        triangle = sb("triangle", [P, P])
        iota_w = sb("iota_w", [P, WINDOW])
        part_node = sb("part_node", [P, 3])
        spare = sb("spare", [P, 1])
        eps = sb("eps", [P, 1])
        w1x = sb("w1x", [P, FEATURES])
        w1b = sb("w1b", [P, FEATURES])
        w2x = sb("w2x", [P, FEATURES])
        w2g = sb("w2g", [P, FEATURES])
        w2b = sb("w2b", [P, FEATURES])
        lin0 = sb("lin0", [P, FEATURES])
        lin1 = sb("lin1", [P, FEATURES])
        conv = sb("conv", [P, LAYERS, FEATURES])
        w1g = sb("w1g", [P, FEATURES])
        b1g_r = sb("b1g_r", [P, FEATURES])
        b1a_r = sb("b1a_r", [P, FEATURES])
        b1b_r = sb("b1b_r", [P, FEATURES])
        b2b_r = sb("b2b_r", [P, FEATURES])
        lin1b_r = sb("lin1b_r", [P, FEATURES])
        cols = sb("cols", [P, 2 + 5 * LAYERS])
        bn_s = sb("bn_s", [P, LAYERS])
        bn_b = sb("bn_b", [P, LAYERS])
        bn_t = sb("bn_t", [P, LAYERS])
        bn_d = sb("bn_d", [P, LAYERS])
        first_i = sb("first_i", [1, SUPERS], I32)
        first = sb("first", [P, SUPERS], I32)
        starts = sb("starts", [P, NP // STEP])
        wide = sb("wide", [P, 1], I32)
        ends_at = sb("ends_at", [P, SUPERS // 2], I32)
        chunk_at = sb("chunk_at", [P, SUPERS // 2], I32)
        late = sb("late", [P, NCHUNK], I32)

        setup(nc, locals(), ins, p_table, index16, sums, NP, NCHUNK, TROWS)
        message_pass(nc, locals(), ins, p_table, index16, sums, SUPERS)
        degree_roots(nc, dinv, dinv_row)
        update_nodes(nc, locals(), ins, sums, dinv_row, x1_rows, g_tables[0], NCHUNK)
        convolve_sems, project_sems = convolve_semaphores(sem), project_semaphores(sem)
        for layer in range(LAYERS):
            convolve(nc, locals(), ins, g_tables[layer % 2], g_tables[(layer + 1) % 2], x1_rows, out, SUPERS, NCHUNK, layer,
                     convolve_sems, project_sems)


def setup(nc, t, ins, p_table, index16, sums, NP, NCHUNK, TROWS):
    dinv, ident, ones, triangle = t["dinv"], t["ident"], t["ones"], t["triangle"]
    w1x, b1a_r = t["w1x"], t["b1a_r"]
    rows = [(t["b1b_r"], "b1b"), (t["b2b_r"], "b2b"), (t["lin1b_r"], "lin1_b")]
    squares = [(t["w1b"], ins["W1b"]),
               (t["w2x"], ins["W2a"][0:FEATURES, :]), (t["w2g"], ins["W2a"][FEATURES:, :]),
               (t["w2b"], ins["W2b"]), (t["lin0"], ins["lin0_w"]), (t["lin1"], ins["lin1_w"])]
    REST = 16 * (len(squares) + len(rows) + 3)
    SUPERS = index16.shape[0]
    rounds = [(n, min(P, SUPERS - n)) for n in range(0, SUPERS, P)]
    flat = TROWS * (FEATURES + 1) // P
    pieces = [(table, at, min(ZEROS, flat - at)) for table in sums for at in range(0, flat, ZEROS)]
    with ExitStack() as ctx:
        def sb(name, shape, dt=F32):
            return ctx.enter_context(nc.sbuf_tensor(name, shape, dt))

        xc, pr = sb("xc", [P, 2, CHUNK]), sb("pr", [P, 2, QUARTERS, FEATURES])
        whole_index, short_index = sb("whole_index", [P, 2, EDGES], I32), sb("short_index", [P, 2, EDGES], I16)
        dst_c, place = sb("dst_all", [P, SUPERS, TILES], I32), sb("place_all", [P, SUPERS, TILES])
        ends = sb("ends", [P, 4])
        beyond, most = sb("beyond", [P, 1]), sb("most", [P, 1])
        PAIRS = SUPERS // 2
        chunk_no, chunk_end = sb("chunk_no", [P, NCHUNK]), sb("chunk_end", [P, NCHUNK])
        passed = sb("passed", [P, PAIRS - 1, NCHUNK])
        full = sb("full", [P, PAIRS + 1])
        more, drop = sb("more", [P, PAIRS]), sb("drop", [P, SUPERS - 1])
        worst, good, early = sb("worst", [P, 2]), sb("good", [P, 2]), sb("early", [P, 1])
        ps = [ctx.enter_context(nc.psum_tensor(f"ps{b}", [P, QUARTERS, FEATURES], F32)) for b in range(2)]
        sem = lambda name: ctx.enter_context(nc.semaphore(name))
        weights_in, rest_in = sem("weights_in"), sem("rest_in")
        x_in = [sem(f"x_in{b}") for b in range(2)]
        stored = [sem(f"p_stored{b}") for b in range(2)]
        index_in, shortened, index_stored = sem("whole_index_in"), sem("shortened"), sem("index_stored")
        dst_in, steps, reduced = sem("dst_all_in"), sem("wide_steps"), sem("wide_reduced")
        zeroed, cleared = sem("zeroed"), sem("cleared")
        made, multiplied, biased = sem("made"), sem("multiplied"), sem("biased")
        bn, turned, copied, joined = sem("bn"), sem("w_turned"), sem("w_copied"), sem("w_joined")
        turned_w = sb("turned_w", [P, 2, FEATURES])
        ps_w = ctx.enter_context(nc.psum_tensor("ps_w", [P, 2, FEATURES], F32))
        block = ctx.enter_context(nc.Block())

        @block.sync
        def _(sp):
            sp.dma_start(w1x[:, :], ins["W1a"][0:FEATURES, :]).then_inc(weights_in, 16)
            sp.dma_start(b1a_r[:, :], ins["b1a"].rearrange("(a n) -> a n", a=1).to_broadcast([P, FEATURES])).then_inc(weights_in, 16)
            for b in range(2):
                sp.sem_inc(stored[b], 16)
            with sp.Fori(0, NCHUNK // 2) as i:
                for b in range(2):
                    c = i * 2 + b
                    sp.wait_ge(multiplied, c + 1)
                    sp.dma_start(xc[:, b, :], ins["xT"][:, bass.ds(c * CHUNK, CHUNK)]).then_inc(x_in[b], 16)

        @block.gpsimd
        def _(pool):
            nc.gpsimd.memset(ident[:, :], 0.0).then_inc(made, 1)
            nc.gpsimd.memset(triangle[:, :], 1.0).then_inc(made, 1)
            nc.gpsimd.memset(ones[:, :], 1.0)
            nc.gpsimd.memset(t["eps"][:, :], EPS)
            pool.wait_ge(made, 2)
            nc.gpsimd.affine_select(out=ident[:, :], in_=ident[:, :], compare_op=ALU.not_equal, fill=1.0, base=0,
                                    pattern=[[-1, P]], channel_multiplier=1).then_inc(made, 1)
            nc.gpsimd.affine_select(out=triangle[:, :], in_=triangle[:, :], compare_op=ALU.is_ge, fill=0.0, base=0,
                                    pattern=[[-1, P]], channel_multiplier=1).then_inc(made, 1)
            nc.gpsimd.iota(t["iota_w"][:, :], pattern=[[1, WINDOW]], base=0, channel_multiplier=0,
                           allow_small_or_imprecise_dtypes=True).then_inc(made, 1)
            for j, offset in enumerate((-EDGE_FEATURES, LEAD, 0)):
                nc.gpsimd.iota(t["part_node"][:, j:j + 1], pattern=[[0, 1]], base=offset, channel_multiplier=1,
                               allow_small_or_imprecise_dtypes=True).then_inc(made, 1)
            nc.gpsimd.iota(t["starts"][:, :], pattern=[[STEP, NP // STEP]], base=0, channel_multiplier=0,
                           allow_small_or_imprecise_dtypes=True).then_inc(made, 1)
            nc.gpsimd.iota(t["spare"][:, :], pattern=[[0, 1]], base=NP, channel_multiplier=1,
                           allow_small_or_imprecise_dtypes=True).then_inc(made, 1)
            nc.gpsimd.iota(chunk_no[:, :], pattern=[[1, NCHUNK]], base=0, channel_multiplier=0,
                           allow_small_or_imprecise_dtypes=True).then_inc(made, 1)
            nc.gpsimd.iota(chunk_end[:, :], pattern=[[CHUNK, NCHUNK]], base=CHUNK, channel_multiplier=0,
                           allow_small_or_imprecise_dtypes=True).then_inc(made, 1)
            pool.wait_ge(cleared, 1)
            for j, (table, at, width) in enumerate(pieces):
                if j > EARLY:
                    pool.wait_ge(multiplied, 2 + (j - EARLY) * NCHUNK // (len(pieces) - EARLY))
                pool.dma_start(table.rearrange("(p a) c -> p (a c)", p=P)[:, at:at + width], dinv[:, 0:width]).then_inc(zeroed, 16)
            pool.wait_ge(steps, 6)
            nc.gpsimd.partition_all_reduce(most[:, :], beyond[:, :], P, bass.bass_isa.ReduceOp.max).then_inc(reduced, 1)
            pool.wait_ge(zeroed, 16 * len(pieces))

        @block.tensor
        def _(pe):
            pe.sem_inc(multiplied, 2)
            pe.wait_ge(weights_in, 32)
            with pe.Fori(0, NCHUNK // 2) as i:
                for b in range(2):
                    c = i * 2 + b
                    pe.wait_ge(x_in[b], (i + 1) * 16)
                    pe.wait_ge(biased, c + 1)
                    for q in range(QUARTERS):
                        last = nc.tensor.matmul(ps[b][:, q, :], xc[:, b, q * P:(q + 1) * P], w1x[:, :], start=True, stop=True)
                    last.then_inc(multiplied, 1)
            pe.wait_ge(bn, 1)
            nc.tensor.transpose(ps_w[:, 0, :], t["w1b"][:, :], ident[:, :])
            nc.tensor.transpose(ps_w[:, 1, :], t["b1b_r"][:, :], ident[:, :]).then_inc(turned, 1)
            pe.wait_ge(copied, 1)
            for j in range(2):
                last = nc.tensor.matmul(ps_w[:, j, :], turned_w[:, j, :], t["w2g"][:, :], start=True, stop=True)
            last.then_inc(joined, 1)

        @block.vector
        def _(dve):
            nc.vector.memset(dinv[:, 0:ZEROS], 0.0).then_inc(cleared, 1)
            dve.sem_inc(biased, 2)
            dve.wait_ge(dst_in, 32)
            nc.vector.tensor_tensor(place[:, :, :], dst_c[:, :, :], t["first"][:, :].unsqueeze(2).to_broadcast([P, SUPERS, TILES]),
                                    ALU.subtract).then_inc(steps, 1)
            dve.wait_ge(steps, 1)
            places = place[:, :, :].rearrange("p n t -> p (n t)")
            nc.vector.tensor_reduce(ends[:, 0:1], places, AXX, ALU.min).then_inc(steps, 1)
            nc.vector.tensor_reduce(ends[:, 1:2], places, AXX, ALU.max).then_inc(steps, 1)
            dve.wait_ge(steps, 3)
            nc.vector.tensor_scalar(ends[:, 2:3], ends[:, 0:1], -1.0, None, ALU.mult).then_inc(steps, 1)
            nc.vector.tensor_scalar(ends[:, 3:4], ends[:, 1:2], float(WINDOW - 1), None, ALU.subtract).then_inc(steps, 1)
            dve.wait_ge(steps, 5)
            nc.vector.tensor_tensor(beyond[:, :], ends[:, 2:3], ends[:, 3:4], ALU.max).then_inc(steps, 1)
            dve.wait_ge(made, 12)
            pair_first = t["first"][:, :].rearrange("p (n two) -> p n two", two=2)[:, 1:, 0]
            nc.vector.tensor_tensor(passed[:, :, :], pair_first.unsqueeze(2).to_broadcast([P, PAIRS - 1, NCHUNK]),
                                    chunk_end[:, :].unsqueeze(1).to_broadcast([P, PAIRS - 1, NCHUNK]), ALU.is_ge).then_inc(steps, 1)
            nc.vector.memset(full[:, 0:1], 0.0)
            nc.vector.tensor_tensor(drop[:, :], t["first"][:, 0:SUPERS - 1], t["first"][:, 1:], ALU.subtract).then_inc(steps, 1)
            dve.wait_ge(steps, 8)
            nc.vector.tensor_reduce(full[:, 1:PAIRS], passed[:, :, :], AXX, ALU.add).then_inc(steps, 1)
            nc.vector.tensor_reduce(worst[:, 0:1], drop[:, :], AXX, ALU.max).then_inc(steps, 1)
            dve.wait_ge(steps, 10)
            nc.vector.tensor_scalar(full[:, PAIRS:], full[:, PAIRS - 1:PAIRS], 0.0, None, ALU.add).then_inc(steps, 1)
            dve.wait_ge(steps, 11)
            nc.vector.tensor_tensor(more[:, :], full[:, 1:], full[:, 0:PAIRS], ALU.subtract).then_inc(steps, 1)
            nc.vector.tensor_scalar(t["chunk_at"][:, :], full[:, 0:PAIRS], 0.0, None, ALU.add)
            dve.wait_ge(steps, 12)
            nc.vector.tensor_reduce(worst[:, 1:2], more[:, :], AXX, ALU.max).then_inc(steps, 1)
            for j, (_, count) in enumerate(rounds):
                dve.wait_ge(index_in, 32 * j + 32)
                if j > 0:
                    dve.wait_ge(index_stored, 16 * j)
                nc.vector.tensor_scalar(short_index[0:count, :, :], whole_index[0:count, :, :], 0.0, None, ALU.add).then_inc(shortened, 1)
            nc.vector.memset(dinv[:, ZEROS:], 0.0)
            conv_b, gamma, beta, mean, var = (t["cols"][:, 2 + LAYERS * j:2 + LAYERS * (j + 1)] for j in range(5))
            dve.wait_ge(bn, 1)
            nc.vector.reciprocal(t["bn_d"][:, :], t["bn_t"][:, :]).then_inc(bn, 1)
            dve.wait_ge(bn, 2)
            nc.vector.tensor_tensor(t["bn_s"][:, :], t["bn_d"][:, :], gamma, ALU.mult).then_inc(bn, 1)
            nc.vector.tensor_tensor(t["bn_t"][:, :], conv_b, mean, ALU.subtract).then_inc(bn, 1)
            dve.wait_ge(bn, 4)
            nc.vector.tensor_tensor(t["bn_d"][:, :], t["bn_t"][:, :], t["bn_s"][:, :], ALU.mult).then_inc(bn, 1)
            dve.wait_ge(bn, 5)
            nc.vector.tensor_tensor(t["bn_b"][:, :], t["bn_d"][:, :], beta, ALU.add)
            dve.wait_ge(weights_in, 32)
            with dve.Fori(0, NCHUNK // 2) as i:
                for b in range(2):
                    c = i * 2 + b
                    dve.wait_ge(multiplied, c + 3)
                    dve.wait_ge(stored[b], (i + 1) * 16)
                    nc.vector.tensor_tensor(pr[:, b, :, :], ps[b][:, :, :],
                                            b1a_r[:, :].unsqueeze(1).to_broadcast([P, QUARTERS, FEATURES]),
                                            ALU.add).then_inc(biased, 1)
            dve.wait_ge(reduced, 1)
            nc.vector.tensor_scalar(t["wide"][:, :], most[:, :], 0.0, None, ALU.is_gt)
            dve.wait_ge(steps, 13)
            nc.vector.tensor_scalar(good[:, 0:1], most[:, :], 0.0, None, ALU.is_le).then_inc(steps, 1)
            nc.vector.tensor_scalar(good[:, 1:2], worst[:, 1:2], 1.0, None, ALU.is_le).then_inc(steps, 1)
            dve.wait_ge(steps, 15)
            nc.vector.scalar_tensor_tensor(out=early[:, :], in0=worst[:, 0:1], scalar=0.0, in1=good[:, 0:1],
                                           op0=ALU.is_le, op1=ALU.mult).then_inc(steps, 1)
            dve.wait_ge(steps, 16)
            nc.vector.tensor_tensor(early[:, :], early[:, :], good[:, 1:2], ALU.mult).then_inc(steps, 1)
            dve.wait_ge(steps, 17)
            nc.vector.tensor_scalar(t["ends_at"][:, :], more[:, :], early[:, 0:1], None, ALU.mult)
            nc.vector.tensor_tensor(worst[:, 0:1], full[:, PAIRS:], early[:, :], ALU.mult).then_inc(steps, 1)
            dve.wait_ge(steps, 18)
            nc.vector.tensor_scalar(t["late"][:, :], chunk_no[:, :], worst[:, 0:1], None, ALU.is_ge)

        @block.scalar
        def _(act):
            act.dma_start(dst_c[:, :, :].rearrange("p n t -> p (n t)"), ins["dst_cols"]).then_inc(dst_in, 16)
            act.dma_start(t["first"][:, :], ins["first"].to_broadcast([P, SUPERS])).then_inc(dst_in, 16)
            act.dma_start(t["cols"][:, :], ins["cols"]).then_inc(rest_in, 16)
            for j, (n, count) in enumerate(rounds):
                if j > 0:
                    act.wait_ge(shortened, j)
                for part, name in enumerate(("src_flat", "dst_flat")):
                    act.dma_start(whole_index[0:count, part, :], ins[name].rearrange("a (n e) -> (a n) e", e=EDGES)[n:n + count, :]).then_inc(index_in, 16)
                act.wait_ge(shortened, j + 1)
                act.dma_start(index16[n:n + count, :, :], short_index[0:count, :, :]).then_inc(index_stored, 16)
            for tile, source in squares:
                act.dma_start(tile[:, :], source).then_inc(rest_in, 16)
            for tile, name in rows:
                act.dma_start(tile[:, :], ins[name].rearrange("(a n) -> a n", a=1).to_broadcast([P, FEATURES])).then_inc(rest_in, 16)
            act.dma_start(t["conv"][:, :, :], ins["conv_w"].rearrange("l k n -> k l n")).then_inc(rest_in, 16)
            act.dma_start(t["first_i"][:, :], ins["first"]).then_inc(rest_in, 16)
            act.wait_ge(rest_in, REST)
            act.wait_ge(made, 12)
            nc.scalar.activation(t["bn_t"][:, :], t["cols"][:, 2 + 4 * LAYERS:2 + 5 * LAYERS], ACT.Sqrt,
                                 bias=t["eps"][:, 0:1]).then_inc(bn, 1)
            with act.Fori(0, NCHUNK // 2) as i:
                for b in range(2):
                    c = i * 2 + b
                    act.wait_ge(biased, c + 3)
                    act.dma_start(p_table[bass.ds(c * CHUNK, CHUNK), :].rearrange("(q p) n -> p q n", p=P),
                                  pr[:, b, :, :]).then_inc(stored[b], 16)
            act.wait_ge(turned, 1)
            nc.scalar.activation(turned_w[:, :, :], ps_w[:, :, :], ACT.Copy).then_inc(copied, 1)
            act.wait_ge(joined, 1)
            nc.scalar.activation(t["w1g"][:, :], ps_w[:, 0, :], ACT.Copy)
            nc.scalar.activation(t["b1g_r"][:, :], ps_w[:, 1, :], ACT.Copy)
            for b in range(2):
                act.wait_ge(stored[b], 16 * (NCHUNK // 2 + 1))
            act.wait_ge(index_stored, 16 * len(rounds))


def each_way(eng, t, program):
    flag = eng.value_load(t["wide"][0:1, 0:1], min_val=0, max_val=1)
    with eng.If(flag):
        program(True)
    with eng.Else():
        program(False)


def visits(eng, wide, n, slot, windows, carrier):
    if not wide:
        yield n, slot, None
        return
    eng.sem_inc(carrier, 1)
    with eng.Fori(0, windows // 2) as v:
        for s in range(2):
            yield n * windows + v * 2 + s, s, v * 2 + s


def message_pass(nc, t, ins, p_table, index16, sums, SUPERS):
    dinv, ident, ones = t["dinv"], t["ident"], t["ones"]
    NP = dinv.shape[1]
    WINDOWS = NP // STEP
    carrier = t["carrier"]
    with ExitStack() as ctx:
        def sb(name, shape, dt=F32):
            return ctx.enter_context(nc.sbuf_tensor(name, shape, dt))

        index_b = sb("index_b", [P, 2, 2, EDGES], I16)
        src_c = sb("src_c", [P, 2, TILES], I32)
        mixed = sb("mixed", [P, 2, EDGES])
        mixed_w = sb("mixed_w", [P, 2, FEATURES])
        pick = sb("pick", [P, 2, EDGES])
        window = sb("window", [P, 2, FEATURES])
        nodes_w = sb("nodes_w", [P, 2, 2])
        degree_c = sb("degree_c", [P, 2, 2])
        degree_lead = sb("degree_lead", [P, 2, LEAD])
        degree_main = sb("degree_main", [P, 2, P])
        lead = slice(EDGE_FEATURES, P)
        same = sb("same", [P, 2, TILES, P])
        rank = sb("rank", [P, TILES])
        source = sb("source", [P, TILES])
        offset = sb("offset", [P, TILES])
        moved = sb("moved", [P, TILES])
        rows = sb("rows", [P, 2, TILES, FEATURES + 1])
        total = sb("total", [P, 2, TILES, FEATURES + 1])
        target = sb("target", [P, 2, TILES], I32)
        ps_rows = [ctx.enter_context(nc.psum_tensor(f"ps_rows{h}", [P, HALF, FEATURES], F32)) for h in range(2)]
        ps_total = [ctx.enter_context(nc.psum_tensor(f"ps_total{g}", [P, len(group), FEATURES + 1], F32)) for g, group in enumerate(GROUPS)]
        ps_degree = ctx.enter_context(nc.psum_tensor("ps_degree", [P, WINDOW], F32))
        sem = lambda name: ctx.enter_context(nc.semaphore(name))
        index_in = [sem(f"index_in{b}") for b in range(2)]
        attr_in = [sem(f"attr_in{b}") for b in range(2)]
        window_in = [sem(f"window_in{b}") for b in range(2)]
        index_free, attr_free, visited, weights_in = (sem(x) for x in ("index_free", "attr_free", "visited", "edge_weights_in"))
        nodes_ready, picks_ready, degree_ready = sem("nodes_ready"), sem("picks_ready"), sem("degree_ready")
        degree_summed, degree_added = sem("degree_summed"), sem("degree_added")
        same_ready, marked_ready, steps = sem("same_ready"), sem("marked_ready"), sem("steps")
        target_ready = sem("target_ready")
        rows_ready, total_done, total_ready = (sem(x) for x in ("rows_ready", "total_done", "total_ready"))
        total_free, issued, ones_ready = sem("total_free"), sem("issued"), sem("ones_ready")
        added = [sem(f"added{k}") for k in range(TABLES)]
        CREDIT = 4
        block = ctx.enter_context(nc.Block())

        @block.sync
        def _(sp):
            def program(wide):
                with sp.Fori(0, SUPERS // 2) as i:
                    for b in range(2):
                        n = i * 2 + b
                        sp.wait_ge(index_free, n + 1)
                        sp.dma_start(index_b[:, b, :, :], index16[bass.ds(n, 1), :, :].to_broadcast([P, 2, EDGES])).then_inc(index_in[b], 16)
                        sp.dma_start(src_c[:, b, :], ins["src_cols"][:, bass.ds(n * TILES, TILES)]).then_inc(index_in[b], 16)
                        sp.wait_ge(attr_free, n + 1)
                        sp.dma_start(mixed[0:EDGE_FEATURES, b, :], ins["attrT"][:, bass.ds(n * EDGES, EDGES)]).then_inc(attr_in[b], 16)
                        for m, s, w in visits(sp, wide, n, b, WINDOWS, carrier):
                            base = w * STEP if wide else sp.value_load(t["first_i"][0:1, bass.ds(n, 1)], min_val=0, max_val=NP - WINDOW)
                            sp.wait_ge(visited, m * 2 + 2)
                            if not wide:
                                sp.dma_start(mixed_w[lead, s, :], p_table[bass.ds(base, LEAD), :]).then_inc(window_in[s], 16)
                            sp.dma_start(window[:, s, :], p_table[bass.ds(base if wide else base + LEAD, P), :]).then_inc(window_in[s], 16)

            for b in range(2):
                sp.dma_start(mixed_w[0:EDGE_FEATURES, b, :], ins["W1a"][FEATURES:, :]).then_inc(weights_in, 16)
            each_way(sp, t, program)

        @block.vector
        def _(dve):
            def pick_out(wide, n, m, s, b, w):
                if wide:
                    nc.vector.tensor_scalar(nodes_w[:, s, 1:2], t["part_node"][:, 2:3], t["starts"][:, bass.ds(w, 1)], None, ALU.add).then_inc(nodes_ready, 1)
                else:
                    nc.vector.tensor_scalar(nodes_w[:, s, :], t["part_node"][:, 0:2], t["first"][:, bass.ds(n, 1)], None, ALU.add).then_inc(nodes_ready, 1)
                dve.wait_ge(nodes_ready, m + 1)
                dve.wait_ge(visited, m * 2 + 2)
                if not wide:
                    nc.vector.tensor_scalar(mixed[lead, s, :], index_b[lead, b, 1, :], nodes_w[lead, s, 0:1], 0.0, ALU.is_equal, ALU.add,
                                            accum_out=degree_c[lead, s, 0:1]).then_inc(picks_ready, 1)
                nc.vector.tensor_scalar(pick[:, s, :], index_b[:, b, 1, :], nodes_w[:, s, 1:2], 0.0, ALU.is_equal, ALU.add,
                                        accum_out=degree_c[:, s, 1:2]).then_inc(picks_ready, 1)

            def spread_degrees(wide, m, s):
                dve.wait_ge(picks_ready, m + 1 if wide else m * 2 + 2)
                if not wide:
                    nc.vector.tensor_scalar(degree_lead[lead, s, :], ident[lead, lead], degree_c[lead, s, 0:1], None, ALU.mult).then_inc(degree_ready, 1)
                nc.vector.tensor_scalar(degree_main[:, s, :], ident[:, :], degree_c[:, s, 1:2], None, ALU.mult).then_inc(degree_ready, 1)

            def compare_sources(n, b):
                nc.vector.tensor_scalar(source[:, :], src_c[:, b, :], 0.0, None, ALU.add).then_inc(steps, 1)
                nc.vector.tensor_scalar(offset[:, :], src_c[:, b, :], -1.0, t["spare"][:, 0:1], ALU.mult, ALU.add).then_inc(steps, 1)
                dve.wait_ge(steps, n * 3 + 2)
                for q in range(TILES):
                    last = nc.vector.scalar_tensor_tensor(out=same[:, b, q, :], in0=index_b[:, b, 0, q * P:(q + 1) * P], scalar=source[:, q:q + 1],
                                                          in1=t["triangle"][:, :], op0=ALU.is_equal, op1=ALU.mult, accum_out=rank[:, q:q + 1])
                last.then_inc(same_ready, 1)

            def find_targets(n, b):
                dve.wait_ge(same_ready, n + 1)
                nc.vector.scalar_tensor_tensor(out=moved[:, :], in0=rank[:, :], scalar=1.0, in1=offset[:, :],
                                               op0=ALU.is_gt, op1=ALU.mult).then_inc(steps, 1)
                dve.wait_ge(steps, n * 3 + 3)
                dve.wait_ge(total_free, n + 1)
                nc.vector.tensor_tensor(target[:, b, :], moved[:, :], source[:, :], ALU.add).then_inc(target_ready, 1)

            def add_degrees(wide, m, base):
                dve.wait_ge(degree_summed, m + 1)
                dve.wait_ge(degree_added, m + 1)
                at, new = (bass.ds(base, STEP), ps_degree[:, LEAD:]) if wide else (bass.ds(base, WINDOW), ps_degree[:, :])
                nc.vector.tensor_tensor(dinv[:, at], dinv[:, at], new, ALU.add).then_inc(degree_added, 1)

            def program(wide):
                with dve.Fori(0, SUPERS // 2) as i:
                    for b in range(2):
                        n = i * 2 + b
                        dve.wait_ge(index_in[b], (i + 1) * 32)
                        if not wide:
                            pick_out(wide, n, n, b, b, None)
                            spread_degrees(wide, n, b)
                        else:
                            dve.wait_ge(attr_free, n + 1)
                        compare_sources(n, b)
                        find_targets(n, b)
                        for m, s, w in visits(dve, wide, n, b, WINDOWS, carrier):
                            if wide:
                                pick_out(wide, n, m, s, b, w)
                                spread_degrees(wide, m, s)
                                add_degrees(wide, m, w * STEP)
                        dve.wait_ge(target_ready, n + 1)
                        dve.sem_inc(index_free, 1)
                        if not wide:
                            add_degrees(wide, n, dve.value_load(t["first_i"][0:1, bass.ds(n, 1)], min_val=0, max_val=NP - WINDOW))

            dve.sem_inc(index_free, 2)
            dve.sem_inc(degree_added, 1)
            each_way(dve, t, program)

        @block.tensor
        def _(pe):
            def edges_of(h, q):
                return slice((h * HALF + q) * P, (h * HALF + q + 1) * P)

            def from_both(h, b):
                for q in range(HALF):
                    e = edges_of(h, q)
                    nc.tensor.matmul(ps_rows[h][:, q, :], mixed[:, b, e], mixed_w[:, b, :], start=True, stop=False)
                    last = nc.tensor.matmul(ps_rows[h][:, q, :], pick[:, b, e], window[:, b, :], start=False, stop=True)
                last.then_inc(visited, 1)

            def from_attributes(h, b):
                for q in range(HALF):
                    nc.tensor.matmul(ps_rows[h][:, q, :], mixed[0:EDGE_FEATURES, b, edges_of(h, q)], mixed_w[0:EDGE_FEATURES, b, :],
                                     start=(q == 0), stop=False, skip_group_check=True)

            def from_window(h, s):
                for q in range(HALF):
                    last = nc.tensor.matmul(ps_rows[h][:, q, :], pick[:, s, edges_of(h, q)], window[:, s, :],
                                            start=False, stop=True, skip_group_check=True)
                last.then_inc(visited, 1)

            def sum_degrees(wide, m, s):
                pe.wait_ge(degree_ready, m + 1 if wide else m * 2 + 2)
                pe.wait_ge(degree_added, m + 1)
                if not wide:
                    nc.tensor.matmul(ps_degree[:, 0:LEAD], ones[lead, :], degree_lead[lead, s, :], start=True, stop=True)
                nc.tensor.matmul(ps_degree[:, LEAD:], ones[:, :], degree_main[:, s, :], start=True, stop=True).then_inc(degree_summed, 1)

            def program(wide):
                with pe.Fori(0, SUPERS // 2) as i:
                    for b in range(2):
                        n = i * 2 + b
                        pe.wait_ge(attr_in[b], (i + 1) * 16)
                        if wide:
                            for h in range(2):
                                pe.wait_ge(rows_ready, n * 2 + h + 1)
                                from_attributes(h, b)
                        for m, s, w in visits(pe, wide, n, b, WINDOWS, carrier):
                            pe.wait_ge(window_in[s], (n * (WINDOWS // 2) + (w - s) // 2) * 16 + 16 if wide else i * 32 + 32)
                            pe.wait_ge(picks_ready, m + 1 if wide else m * 2 + 2)
                            for h in range(2):
                                if wide:
                                    from_window(h, s)
                                else:
                                    pe.wait_ge(rows_ready, n * 2 + h + 1)
                                    from_both(h, b)
                                if h == 0:
                                    sum_degrees(wide, m, s)
                        pe.wait_ge(same_ready, n + 1)
                        for g, group in enumerate(GROUPS):
                            pe.wait_ge(rows_ready, n * 2 + group[-1] // HALF + 3)
                            pe.wait_ge(total_ready, n * len(GROUPS) + g + 1)
                            for q in group:
                                last = nc.tensor.matmul(ps_total[g][:, q - group[0], :], same[:, b, q, :], rows[:, b, q, :], start=True, stop=True)
                            last.then_inc(total_done, 1)
                        pe.wait_ge(total_done, (n + 1) * len(GROUPS))
                        pe.sem_inc(attr_free, 1)

            pe.sem_inc(attr_free, 2)
            pe.sem_inc(visited, CREDIT)
            pe.wait_ge(weights_in, 32)
            pe.wait_ge(ones_ready, 1)
            each_way(pe, t, program)

        @block.scalar
        def _(act):
            def program(wide):
                with act.Fori(0, SUPERS // 2) as i:
                    for b in range(2):
                        n = i * 2 + b
                        for h in range(2):
                            last = (n + 1) * WINDOWS - 1 if wide else n
                            act.wait_ge(visited, last * 2 + CREDIT + h + 1)
                            nc.scalar.activation(rows[:, b, h * HALF:(h + 1) * HALF, 0:FEATURES], ps_rows[h][:, :, :], ACT.Relu).then_inc(rows_ready, 1)
                        act.wait_ge(total_free, n + 1)
                        for g, group in enumerate(GROUPS):
                            act.wait_ge(total_done, n * len(GROUPS) + g + 1)
                            nc.scalar.activation(total[:, b, group[0]:group[-1] + 1, :], ps_total[g][:, :, :], ACT.Copy).then_inc(total_ready, 1)

            act.sem_inc(rows_ready, 2)
            act.sem_inc(total_ready, len(GROUPS))
            each_way(act, t, program)

        @block.gpsimd
        def _(pool):
            nc.gpsimd.memset(rows[:, :, :, FEATURES:], 1.0).then_inc(ones_ready, 1)
            pool.sem_inc(total_free, 1)
            for k in range(TABLES):
                pool.dma_start(sums[k][NP + P - 1:, 0:1], ones[0:1, 0:1]).then_inc(added[k], 16)
            with pool.Fori(0, SUPERS // 2) as i:
                for b in range(2):
                    n = i * 2 + b
                    pool.wait_ge(target_ready, n + 1)
                    for q in range(TILES):
                        k = q % TABLES
                        for g, group in enumerate(GROUPS):
                            if q == group[0]:
                                pool.wait_ge(total_ready, (n + 1) * len(GROUPS) + g + 1)
                        pool.wait_ge(added[k], (n * (TILES // TABLES) + q // TABLES) * 16 + 16)
                        pool.sem_inc(total_free if q == TABLES - 1 else issued, 1)
                        pool.indirect_dma_start(sums[k], bass.IndirectOffsetOnAxis(ap=target[:, b, q:q + 1], axis=0),
                                                total[:, b, q, :], None, compute_op=ALU.add).then_inc(added[k], 16)
            for k in range(TABLES):
                pool.wait_ge(added[k], SUPERS * (16 * TILES // TABLES) + 16)


def degree_roots(nc, degree, row):
    with ExitStack() as ctx:
        spread = ctx.enter_context(nc.sbuf_tensor("spread", [P, degree.shape[1] // P], F32))
        moved, rooted = ctx.enter_context(nc.semaphore("degrees_moved")), ctx.enter_context(nc.semaphore("rooted"))
        over_partitions = row.rearrange("a (p n) -> (a p) n", p=P)
        block = ctx.enter_context(nc.Block())

        @block.sync
        def _(sp):
            sp.dma_start(row, degree[0:1, :]).then_inc(moved, 16)
            sp.wait_ge(moved, 16)
            sp.dma_start(spread[:, :], over_partitions).then_inc(moved, 16)
            sp.wait_ge(rooted, 2)
            sp.dma_start(over_partitions, spread[:, :]).then_inc(moved, 16)
            sp.wait_ge(moved, 48)

        @block.scalar
        def _(act):
            act.wait_ge(moved, 32)
            nc.scalar.activation(spread[:, :], spread[:, :], ACT.Sqrt, bias=1.0).then_inc(rooted, 1)

        @block.vector
        def _(dve):
            dve.wait_ge(rooted, 1)
            nc.vector.reciprocal(spread[:, :], spread[:, :]).then_inc(rooted, 1)


def pipeline(eng, chunks, depth, step):
    def at(k, slot, first, end):
        def live(d):
            if (first and k < d) or (end and k - d >= chunks):
                return None
            return k - d, (slot - d) % 2, (k - d - (slot - d) % 2) // 2
        return live

    for k in range(depth):
        step(k, at(k, k % 2, True, False))
    if chunks > depth:
        with eng.Fori(0, (chunks - depth) // 2) as i:
            for slot in range(2):
                k = i * 2 + slot + depth
                step(k, at(k, slot, False, False))
    for k in range(chunks, chunks + depth):
        step(k, at(k, k % 2, False, True))


def update_nodes(nc, t, ins, sums, dinv_row, x1_rows, g_table, NCHUNK):
    ident, dinv, acc = t["ident"], t["dinv"], t["acc"]
    b2a, lin0_b = t["cols"][:, 0:1], t["cols"][:, 1:2]
    spread = [P, QUARTERS, FEATURES]
    carrier = t["carrier"]
    with ExitStack() as ctx:
        def sb(name, shape, dt=F32):
            return ctx.enter_context(nc.sbuf_tensor(name, shape, dt))

        part = sb("part", [P, 2, TABLES, QUARTERS, FEATURES + 1])
        x_cols, x_rows = sb("x_cols", [P, 2, CHUNK]), sb("x_rows", [P, 2] + spread[1:])
        total01, total23 = sb("total01", [P, QUARTERS, FEATURES + 1]), sb("total23", [P, QUARTERS, FEATURES + 1])
        total = sb("total_n", [P, 2, QUARTERS, FEATURES + 1])
        x_bias = sb("x_bias", [P, 2] + spread[1:])
        count = sb("count", [P, 3, QUARTERS])
        scale_d, some_d = sb("scale_d", [P, 2] + spread[1:]), sb("some_d", [P, 2] + spread[1:])
        mean_c, mid_c, x1_c, h_c, hs_c = (sb(x, [P, CHUNK]) for x in ("mean_c", "mid_c", "x1_c", "h_c", "hs_c"))
        res, x1 = sb("res", spread), sb("x1", [P, 2] + spread[1:])
        g_rows = sb("g_rows", [P, 2] + spread[1:])
        stats, moments, dev, inv, shift = norm_tiles(sb)
        pa, pb, po, pt, pl, pc, pd = (ctx.enter_context(nc.psum_tensor(x, spread, F32)) for x in ("pa", "pb", "po", "pt", "pl", "pc", "pd"))
        flat = lambda ps: ps[:, :, :].rearrange("p q n -> p (q n)")
        sem = lambda name: ctx.enter_context(nc.semaphore(name))
        part_in, x_in, x1_stored, g_stored = ([sem(f"{x}{b}") for b in range(2)] for x in ("part_in", "nx_in", "x1_stored", "g_stored"))
        (pair01, pair23, biased, summed, clipped, inverted, diagonals, meaned, mean_ready,
         mixed, mid_ready, outed, res_ready, stat, stat_seen, mom, dev_ready, inv_ready, shift_ready, x1_ready, turned, x1c_ready,
         lined, h_ready, hs_ready, projected, g_ready, acc_ready) = (sem(x) for x in (
            "pair01 pair23 biased summed clipped inverted diagonals meaned mean_ready mixed "
            "mid_ready outed res_ready stat stat_seen mom dev_ready inv_ready shift_ready x1_ready turned x1c_ready lined h_ready "
            "hs_ready projected g_ready acc_ready").split())
        block = ctx.enter_context(nc.Block())

        @block.sync
        def _(sp):
            def step(k, live):
                if live(0):
                    c, b, _ = live(0)
                    at = bass.ds(c * CHUNK, CHUNK)
                    sp.wait_ge(summed, c + 1)
                    sp.wait_ge(pair23, c + 1)
                    for j in range(TABLES):
                        sp.dma_start(part[:, b, j, :, :], sums[j][at, :].rearrange("(q p) n -> p q n", p=P)).then_inc(part_in[b], 16)
                    sp.wait_ge(mid_ready, c + 1)
                    sp.wait_ge(biased, c + 1)
                    sp.sem_inc(carrier, 1)
                    sp.dma_start(dinv[:, at], dinv_row[:, at].to_broadcast([P, CHUNK])).then_inc(x_in[b], 16)
                    sp.dma_start(x_cols[:, b, :], ins["xT"][:, at]).then_inc(x_in[b], 16)
                    sp.dma_start(x_rows[:, b, :, :], ins["x"][at, :].rearrange("(q p) n -> p q n", p=P)).then_inc(x_in[b], 16)

            pipeline(sp, NCHUNK, 4, step)

        @block.gpsimd
        def _(pool):
            def step(k, live):
                if live(0):
                    c, b, used = live(0)
                    pool.wait_ge(part_in[b], used * 16 * TABLES + 16 * TABLES)
                    pool.wait_ge(summed, c + 2)
                    nc.gpsimd.tensor_tensor(total01[:, :, :], part[:, b, 0, :, :], part[:, b, 1, :, :], ALU.add).then_inc(pair01, 1)
                    nc.gpsimd.tensor_tensor(total23[:, :, :], part[:, b, 2, :, :], part[:, b, 3, :, :], ALU.add).then_inc(pair23, 1)
                    pool.wait_ge(x_in[b], used * 48 + 48)
                    pool.wait_ge(res_ready, c + 1)
                    nc.gpsimd.tensor_tensor(x_bias[:, b, :, :], x_rows[:, b, :, :], t["b2b_r"][:, :].unsqueeze(1).to_broadcast(spread),
                                            ALU.add).then_inc(biased, 1)

            pool.sem_inc(pair23, 2)
            pool.sem_inc(biased, 2)
            pipeline(pool, NCHUNK, 4, step)

        @block.vector
        def _(dve):
            def step(k, live):
                if live(2):
                    c, b, _ = live(2)
                    dve.wait_ge(res_ready, c + 3)
                    dve.wait_ge(shift_ready, c + 1)
                    norm_moments(nc, dve, c, res, stats, moments, stat, stat_seen, mom)
                if live(0):
                    c, b, _ = live(0)
                    dve.wait_ge(pair01, c + 1)
                    dve.wait_ge(pair23, c + 3)
                    dve.wait_ge(mid_ready, c + 1)
                    nc.vector.tensor_tensor(total[:, b, :, :], total01[:, :, :], total23[:, :, :], ALU.add).then_inc(summed, 1)
                if live(3):
                    c, b, _ = live(3)
                    dve.wait_ge(h_ready, c + 1)
                    nc.vector.tensor_tensor(hs_c[:, :], h_c[:, :], dinv[:, bass.ds(c * CHUNK, CHUNK)], ALU.mult).then_inc(hs_ready, 1)
                if live(2):
                    c, b, _ = live(2)
                    dve.wait_ge(dev_ready, c + 1)
                    dve.wait_ge(x1_ready, c * QUARTERS + 1)
                    nc.vector.reciprocal(inv[:, :], dev[:, :]).then_inc(inv_ready, 1)
                    dve.wait_ge(inv_ready, c + 1)
                    nc.vector.scalar_tensor_tensor(out=shift[:, :], in0=moments[:, :, 0], scalar=-1.0, in1=inv[:, :],
                                                   op0=ALU.mult, op1=ALU.mult).then_inc(shift_ready, 1)
                if live(0):
                    c, b, _ = live(0)
                    dve.wait_ge(summed, c + 3)
                    nc.vector.tensor_scalar(count[:, 0, :], total[:, b, :, FEATURES], 1.0, None, ALU.max).then_inc(clipped, 1)
                    nc.vector.tensor_scalar(count[:, 2, :], total[:, b, :, FEATURES], 1.0, None, ALU.min).then_inc(clipped, 1)
                    dve.wait_ge(clipped, c * 2 + 2)
                    nc.vector.reciprocal(count[:, 1, :], count[:, 0, :]).then_inc(inverted, 1)
                    dve.wait_ge(inverted, c + 1)
                    for tile, j in ((scale_d, 1), (some_d, 2)):
                        nc.vector.tensor_tensor(tile[:, b, :, :], ident[:, :].unsqueeze(1).to_broadcast(spread),
                                                count[:, j, :].unsqueeze(2).to_broadcast(spread), ALU.mult).then_inc(diagonals, 1)
                if live(1):
                    c, b, _ = live(1)
                    dve.wait_ge(outed, c + 1)
                    dve.wait_ge(biased, c + 3)
                    dve.wait_ge(x1_ready, c * QUARTERS + 1)
                    nc.vector.tensor_tensor(res[:, :, :], po[:, :, :], x_bias[:, b, :, :], ALU.add).then_inc(res_ready, 1)

            dve.sem_inc(summed, 2)
            dve.sem_inc(res_ready, 2)
            dve.sem_inc(acc_ready, 1)
            dve.sem_inc(x1_ready, 1)
            dve.sem_inc(shift_ready, 1)
            pipeline(dve, NCHUNK, 4, step)

        @block.tensor
        def _(pe):
            def step(k, live):
                if live(1):
                    c, b, _ = live(1)
                    pe.wait_ge(diagonals, c * 2 + 2)
                    for q in range(QUARTERS):
                        last = nc.tensor.matmul(pa[:, q, :], total[:, b, q, 0:FEATURES], scale_d[:, b, q, :], start=True, stop=True)
                    last.then_inc(meaned, 1)
                if live(3):
                    c, _, _ = live(3)
                    pe.wait_ge(x1c_ready, c + 3)
                    nc.tensor.matmul(flat(pl), t["lin0"][:, :], x1_c[:, :], start=True, stop=True).then_inc(lined, 1)
                if live(1):
                    c, b, used = live(1)
                    pe.wait_ge(x_in[b], used * 48 + 48)
                    nc.tensor.matmul(flat(pb), t["w2x"][:, :], x_cols[:, b, :], start=True, stop=False)
                    nc.tensor.matmul(flat(pb), t["b1g_r"][:, :], some_d[:, b, :, :].rearrange("p q n -> p (q n)"), start=False, stop=False)
                    pe.wait_ge(mean_ready, c + 1)
                    nc.tensor.matmul(flat(pb), t["w1g"][:, :], mean_c[:, :], start=False, stop=True).then_inc(mixed, 1)
                if live(3):
                    c, _, _ = live(3)
                    pe.wait_ge(hs_ready, c + 1)
                    pe.wait_ge(g_ready, c + 1)
                    pe.wait_ge(acc_ready, c + 1)
                    project_chunk(nc, t["conv"][:, 0, :], hs_c[:, :], pc, flat(pd)).then_inc(projected, 1)
                if live(2):
                    c, b, _ = live(2)
                    pe.wait_ge(x1_ready, c * QUARTERS + QUARTERS + 1)
                    pe.wait_ge(x1c_ready, c + 2)
                    for q in range(QUARTERS):
                        last = nc.tensor.transpose(pt[:, q, :], x1[:, b, q, :], ident[:, :])
                    last.then_inc(turned, 1)
                if live(1):
                    c, _, _ = live(1)
                    pe.wait_ge(mid_ready, c + 3)
                    pe.wait_ge(res_ready, c + 2)
                    for q in range(QUARTERS):
                        last = nc.tensor.matmul(po[:, q, :], mid_c[:, q * P:(q + 1) * P], t["w2b"][:, :], start=True, stop=True)
                    last.then_inc(outed, 1)

            pipeline(pe, NCHUNK, 4, step)

        @block.scalar
        def _(act):
            def step(k, live):
                if live(1):
                    c, _, _ = live(1)
                    act.wait_ge(meaned, c + 1)
                    nc.scalar.activation(mean_c[:, :], flat(pa), ACT.Copy).then_inc(mean_ready, 1)
                if live(2):
                    c, _, _ = live(2)
                    act.wait_ge(mom, c * QUARTERS + QUARTERS)
                    nc.scalar.activation(dev[:, :], moments[:, :, 1], ACT.Sqrt, bias=t["eps"][:, 0:1]).then_inc(dev_ready, 1)
                if live(3):
                    c, _, _ = live(3)
                    act.wait_ge(lined, c + 1)
                    nc.scalar.activation(h_c[:, :], flat(pl), ACT.Relu, bias=lin0_b).then_inc(h_ready, 1)
                if live(1):
                    c, b, used = live(1)
                    act.wait_ge(mixed, c + 1)
                    nc.scalar.activation(mid_c[:, :], flat(pb), ACT.Relu, bias=b2a).then_inc(mid_ready, 1)
                if live(2):
                    c, b, used = live(2)
                    act.wait_ge(shift_ready, c + 2)
                    act.wait_ge(x1_stored[b], used * 16 + 16)
                    act.wait_ge(x1c_ready, c + 1)
                    for q in range(QUARTERS):
                        nc.scalar.activation(x1[:, b, q, :], res[:, q, :], ACT.Identity, bias=shift[:, q:q + 1],
                                             scale=inv[:, q:q + 1]).then_inc(x1_ready, 1)
                if live(3):
                    c, b, used = live(3)
                    act.wait_ge(projected, c + 1)
                    nc.scalar.activation(acc[:, bass.ds(c * CHUNK, CHUNK)], flat(pd), ACT.Copy).then_inc(acc_ready, 1)
                    act.wait_ge(g_stored[b], used * 16 + 16)
                    nc.scalar.activation(g_rows[:, b, :, :], pc[:, :, :], ACT.Copy).then_inc(g_ready, 1)
                if live(2):
                    c, b, _ = live(2)
                    act.wait_ge(turned, c + 1)
                    nc.scalar.activation(x1_c[:, :], flat(pt), ACT.Copy).then_inc(x1c_ready, 1)
                    act.wait_ge(x1_ready, c * QUARTERS + QUARTERS + 1)
                    act.dma_start(x1_rows[bass.ds(c * CHUNK, CHUNK), :].rearrange("(q p) n -> p q n", p=P),
                                  x1[:, b, :, :]).then_inc(x1_stored[b], 16)
                if live(3):
                    c, b, _ = live(3)
                    act.wait_ge(g_ready, c + 2)
                    act.dma_start(g_table[bass.ds(c * CHUNK, CHUNK), :].rearrange("(q p) n -> p q n", p=P),
                                  g_rows[:, b, :, :]).then_inc(g_stored[b], 16)

            act.sem_inc(mid_ready, 2)
            act.sem_inc(x1c_ready, 2)
            act.sem_inc(g_ready, 1)
            for b in range(2):
                act.sem_inc(x1_stored[b], 16)
                act.sem_inc(g_stored[b], 16)
            pipeline(act, NCHUNK, 4, step)
            for b in range(2):
                act.wait_ge(x1_stored[b], NCHUNK // 2 * 16 + 16)
                act.wait_ge(g_stored[b], NCHUNK // 2 * 16 + 16)


def norm_tiles(sb):
    return (sb("stats", [P, QUARTERS, 6]), sb("moments", [P, QUARTERS, 2]), sb("dev", [P, QUARTERS]), sb("inv", [P, QUARTERS]),
            sb("shift", [P, QUARTERS]))


def norm_moments(nc, dve, c, res, stats, moments, stat, stat_seen, mom):
    for q in range(QUARTERS):
        nc.vector.bn_stats(stats[:, q, :], res[:, q, :]).then_inc(stat, 1)
    dve.wait_ge(stat, c * QUARTERS + QUARTERS)
    dve.sem_inc(stat_seen, 1)
    for q in range(QUARTERS):
        nc.vector.bn_aggr(moments[:, q, :], stats[:, q, :]).then_inc(mom, 1)
    dve.wait_ge(mom, c * QUARTERS + QUARTERS)


def project_chunk(nc, weights, hs_c, ps_rows, ps_cols):
    for q in range(QUARTERS):
        nc.tensor.matmul(ps_rows[:, q, :], hs_c[:, q * P:(q + 1) * P], weights, start=True, stop=True)
    return nc.tensor.matmul(ps_cols, weights, hs_c, start=True, stop=True)


def convolve_semaphores(sem):
    one = "dst_free rows_used placed picked acc_added summed gathers_issued"
    return {**{x: sem(x) for x in one.split()}, "src_in": [sem(f"src_in{r}") for r in range(RING)],
            "dst_in": [sem(f"dst_in{b}") for b in range(2)], "rows_in": [sem(f"rows_in{r}") for r in range(RING)]}


def convolve(nc, t, ins, g_table, g_next, x1_rows, out, SUPERS, NCHUNK, layer, sems, chunk_sems):
    acc = t["acc"]
    NP = acc.shape[1]
    WINDOWS = NP // STEP
    carrier = t["carrier"]
    with ExitStack() as ctx:
        def sb(name, shape, dt=F32):
            return ctx.enter_context(nc.sbuf_tensor(f"{name}{layer}", shape, dt))

        src_c, dst_c = sb("gsrc", [P, RING, TILES], I32), sb("gdst", [P, 2, TILES], I32)
        place = sb("place", [P, 2, TILES])
        pick = sb("gpick", [P, 2, TILES, WINDOW])
        rows = sb("grows", [P, RING, TILES, FEATURES])
        ps = [ctx.enter_context(nc.psum_tensor(f"gps{layer}_{b}", [P, WINDOW], F32)) for b in range(2)]
        src_in, dst_in, rows_in = sems["src_in"], sems["dst_in"], sems["rows_in"]
        dst_free, rows_used, placed, picked, added, summed, issued = (
            sems[x] for x in "dst_free rows_used placed picked acc_added summed gathers_issued".split())
        done = layer * SUPERS
        if layer + 1 < LAYERS:
            chunk_end = project_steps(nc, t, ctx, sb, g_next, layer, layer * NCHUNK, chunk_sems)
        else:
            chunk_end = finish_steps(nc, t, ctx, sb, x1_rows, out)
        block = ctx.enter_context(nc.Block())

        def in_turn(eng, wide, super_tile, end):
            with eng.Fori(0, SUPERS // RING) as i:
                for r in range(RING):
                    super_tile(i, r)
                    if r % 2 == 1 and not wide:
                        pair = i * (RING // 2) + r // 2
                        with eng.If(eng.value_load(t["ends_at"][0:1, bass.ds(pair, 1)], min_val=0, max_val=1)):
                            end(eng.value_load(t["chunk_at"][0:1, bass.ds(pair, 1)], min_val=0, max_val=NCHUNK - 1))
            def end_late(low, high):
                with eng.Fori(low, high) as c:
                    with eng.If(eng.value_load(t["late"][0:1, bass.ds(c, 1)], min_val=0, max_val=1)):
                        end(c)

            many = NCHUNK - FEW
            with eng.If(eng.value_load(t["late"][0:1, many - 1:many], min_val=0, max_val=1)):
                end_late(0, many)
            end_late(many, NCHUNK)

        @block.sync
        def _(sp):
            with sp.Fori(0, SUPERS // RING) as i:
                for r in range(RING):
                    n = i * RING + r + done
                    at = bass.ds((i * RING + r) * TILES, TILES)
                    sp.wait_ge(rows_used, n + 1)
                    sp.dma_start(src_c[:, r, :], ins["src_cols"][:, at]).then_inc(src_in[r], 16)
                    sp.wait_ge(dst_free, n + 1)
                    sp.dma_start(dst_c[:, r % 2, :], ins["dst_cols"][:, at]).then_inc(dst_in[r % 2], 16)

        @block.gpsimd
        def _(pool):
            with pool.Fori(0, SUPERS // RING) as i:
                for r in range(RING):
                    pool.wait_ge(src_in[r], (i + done // RING + 1) * 16)
                    pool.sem_inc(issued, 1)
                    for q in range(TILES):
                        pool.indirect_dma_start(rows[:, r, q, :], None, g_table,
                                                bass.IndirectOffsetOnAxis(ap=src_c[:, r, q:q + 1], axis=0)).then_inc(rows_in[r], 16)

        @block.vector
        def _(dve):
            def pick_out(local, m, s, b, w):
                dve.wait_ge(summed, m + 1)
                start, span = (t["first"][:, bass.ds(local, 1)], WINDOW) if w is None else (t["starts"][:, bass.ds(w, 1)], STEP)
                nc.vector.tensor_tensor(place[:, s, :], dst_c[:, b, :], start.to_broadcast([P, TILES]), ALU.subtract).then_inc(placed, 1)
                dve.wait_ge(placed, m + 1)
                for q in range(TILES):
                    last = nc.vector.tensor_scalar(pick[:, s, q, 0:span], t["iota_w"][:, 0:span], place[:, s, q:q + 1], None, ALU.is_equal)
                last.then_inc(picked, 1)

            def add_sums(m, s, base, span):
                dve.wait_ge(summed, m + 3)
                dve.wait_ge(added, m + 2)
                nc.vector.tensor_tensor(acc[:, bass.ds(base, span)], acc[:, bass.ds(base, span)], ps[s][:, 0:span], ALU.add).then_inc(added, 1)

            def program(wide):
                def start(i, r):
                    dve.wait_ge(dst_in[r % 2], (i * (RING // 2) + done // 2 + r // 2 + 1) * 16)
                    if not wide:
                        local = i * RING + r
                        pick_out(local, local + done, r % 2, r % 2, None)
                        dve.sem_inc(dst_free, 1)

                def super_tile(i, r):
                    local = i * RING + r
                    n = local + done
                    if wide:
                        start(i, r)
                        for m, s, w in visits(dve, wide, n, r % 2, WINDOWS, carrier):
                            pick_out(local, m, s, r % 2, w)
                            add_sums(m, s, w * STEP, STEP)
                        dve.sem_inc(dst_free, 1)
                    else:
                        for ahead in ((0, 1) if r == 0 else (r + 1,) if r + 1 < RING else ()):
                            start(i, ahead)
                        add_sums(n, r % 2, dve.value_load(t["first_i"][0:1, bass.ds(local, 1)], min_val=0, max_val=NP - WINDOW), WINDOW)
                    if wide or r % 2 == 1:
                        dve.wait_ge(added, (n + 1) * WINDOWS + 2 if wide else n + 3)
                        dve.sem_inc(carrier, 1)

                in_turn(dve, wide, super_tile, lambda c: chunk_end["vector"](dve, c))

            if layer == 0:
                dve.sem_inc(dst_free, 2)
            each_way(dve, t, program)

        @block.tensor
        def _(pe):
            def program(wide):
                span = STEP if wide else WINDOW

                def super_tile(i, r):
                    n, b = i * RING + r + done, r % 2
                    pe.wait_ge(rows_in[r], (i + done // RING + 1) * 16 * TILES)
                    for m, s, w in visits(pe, wide, n, b, WINDOWS, carrier):
                        pe.wait_ge(picked, m + 1)
                        pe.wait_ge(added, m + 1)
                        for q in range(TILES):
                            last = nc.tensor.matmul(ps[s][:, 0:span], rows[:, r, q, :], pick[:, s, q, 0:span], start=(q == 0), stop=(q == TILES - 1))
                        last.then_inc(summed, 1)
                    last_visit = (n + 1) * WINDOWS - 1 if wide else n
                    pe.wait_ge(summed, last_visit + 3)
                    pe.sem_inc(rows_used, 1)

                in_turn(pe, wide, super_tile, lambda c: chunk_end["tensor"](pe, c))

            if layer == 0:
                pe.sem_inc(summed, 2)
                pe.sem_inc(rows_used, RING)
                pe.sem_inc(added, 2)
            each_way(pe, t, program)

        @block.scalar
        def _(act):
            chunk_end["start"](act)
            with act.Fori(0, NCHUNK) as c:
                chunk_end["scalar"](act, c)
            chunk_end["stores"](act)


def project_semaphores(sem):
    return {x: sem(x + "_p") for x in "scaled h_ready hs_ready projected g_ready acc_ready g_stored".split()}


def project_steps(nc, t, ctx, sb, g_table, layer, done, sems):
    acc, dinv = t["acc"], t["dinv"]
    spread = [P, QUARTERS, FEATURES]
    t_c, h_c, hs_c, g_rows = sb("t_c", [P, CHUNK]), sb("h_c", [P, CHUNK]), sb("hs_c", [P, CHUNK]), sb("g_rows", spread)
    pr = ctx.enter_context(nc.psum_tensor(f"pr{layer}", spread, F32))
    pc = ctx.enter_context(nc.psum_tensor(f"pc{layer}", [P, CHUNK], F32))
    scaled, h_ready, hs_ready, projected, g_ready, acc_ready, g_stored = (
        sems[x] for x in "scaled h_ready hs_ready projected g_ready acc_ready g_stored".split())

    def vector(dve, c):
        at, n = bass.ds(c * CHUNK, CHUNK), c + done
        nc.vector.tensor_tensor(t_c[:, :], acc[:, at], dinv[:, at], ALU.mult).then_inc(scaled, 1)
        dve.wait_ge(h_ready, n + 1)
        nc.vector.tensor_tensor(hs_c[:, :], h_c[:, :], dinv[:, at], ALU.mult).then_inc(hs_ready, 1)
        dve.wait_ge(projected, n + 1)
        nc.vector.tensor_scalar(acc[:, at], pc[:, :], 0.0, None, ALU.add).then_inc(acc_ready, 1)

    def tensor(pe, c):
        n = c + done
        pe.wait_ge(hs_ready, n + 1)
        pe.wait_ge(acc_ready, n + 1)
        pe.wait_ge(g_ready, n + 1)
        project_chunk(nc, t["conv"][:, layer + 1, :], hs_c[:, :], pr, pc[:, :]).then_inc(projected, 1)

    def scalar(act, c):
        n = c + done
        act.wait_ge(scaled, n + 1)
        nc.scalar.activation(h_c[:, :], t_c[:, :], ACT.Relu, bias=t["bn_b"][:, layer:layer + 1],
                             scale=t["bn_s"][:, layer:layer + 1]).then_inc(h_ready, 1)
        act.wait_ge(projected, n + 1)
        act.wait_ge(g_stored, n * 16 + 16)
        nc.scalar.activation(g_rows[:, :, :], pr[:, :, :], ACT.Copy).then_inc(g_ready, 1)
        act.wait_ge(g_ready, n + 2)
        act.dma_start(g_table[bass.ds(c * CHUNK, CHUNK), :].rearrange("(q p) n -> p q n", p=P), g_rows[:, :, :]).then_inc(g_stored, 16)

    def start(act):
        if layer == 0:
            act.sem_inc(g_stored, 16)
            act.sem_inc(g_ready, 1)
            act.sem_inc(acc_ready, 1)

    def stores(act):
        act.wait_ge(g_stored, (done + acc.shape[1] // CHUNK + 1) * 16)

    return {"vector": vector, "tensor": tensor, "scalar": scalar, "stores": stores, "start": start}


def finish_steps(nc, t, ctx, sb, x1_rows, out):
    acc, dinv = t["acc"], t["dinv"]
    spread = [P, QUARTERS, FEATURES]
    layer = LAYERS - 1
    t_c, h_c = sb("t_c", [P, CHUNK]), sb("h_c", [P, CHUNK])
    x1, x1_bias, res, y = sb("x1", spread), sb("x1_bias", spread), sb("res", spread), sb("y", spread)
    stats, moments, dev, inv, shift = norm_tiles(sb)
    ps = ctx.enter_context(nc.psum_tensor("ps_f", spread, F32))
    x1_in, stored, scaled, h_ready, biased, lined, res_ready, stat, stat_seen, mom, dev_ready, inv_ready, shift_ready, y_ready = (
        ctx.enter_context(nc.semaphore(f"{x}_f")) for x in
        "x1_in stored scaled h_ready biased lined res_ready stat stat_seen mom dev_ready inv_ready shift_ready y_ready".split())

    def vector(dve, c):
        at = bass.ds(c * CHUNK, CHUNK)
        nc.vector.tensor_tensor(t_c[:, :], acc[:, at], dinv[:, at], ALU.mult).then_inc(scaled, 1)
        dve.wait_ge(x1_in, c * 16 + 16)
        nc.vector.tensor_tensor(x1_bias[:, :, :], x1[:, :, :], t["lin1b_r"][:, :].unsqueeze(1).to_broadcast(spread), ALU.add).then_inc(biased, 1)
        dve.wait_ge(biased, c + 1)
        dve.wait_ge(lined, c + 1)
        dve.wait_ge(y_ready, c * QUARTERS + 1)
        nc.vector.tensor_tensor(res[:, :, :], ps[:, :, :], x1_bias[:, :, :], ALU.add).then_inc(res_ready, 1)
        dve.wait_ge(res_ready, c + 1)
        norm_moments(nc, dve, c, res, stats, moments, stat, stat_seen, mom)
        dve.wait_ge(dev_ready, c + 1)
        nc.vector.reciprocal(inv[:, :], dev[:, :]).then_inc(inv_ready, 1)
        dve.wait_ge(inv_ready, c + 1)
        nc.vector.scalar_tensor_tensor(out=shift[:, :], in0=moments[:, :, 0], scalar=-1.0, in1=inv[:, :],
                                       op0=ALU.mult, op1=ALU.mult).then_inc(shift_ready, 1)
        dve.wait_ge(shift_ready, c + 1)
        dve.sem_inc(stat_seen, 1)

    def tensor(pe, c):
        pe.wait_ge(h_ready, c + 1)
        for q in range(QUARTERS):
            last = nc.tensor.matmul(ps[:, q, :], h_c[:, q * P:(q + 1) * P], t["lin1"][:, :], start=True, stop=True)
        last.then_inc(lined, 1)

    def scalar(act, c):
        act.dma_start(x1[:, :, :], x1_rows[bass.ds(c * CHUNK, CHUNK), :].rearrange("(q p) n -> p q n", p=P)).then_inc(x1_in, 16)
        act.wait_ge(scaled, c + 1)
        nc.scalar.activation(h_c[:, :], t_c[:, :], ACT.Relu, bias=t["bn_b"][:, layer:layer + 1],
                             scale=t["bn_s"][:, layer:layer + 1]).then_inc(h_ready, 1)
        act.wait_ge(mom, c * QUARTERS + QUARTERS)
        nc.scalar.activation(dev[:, :], moments[:, :, 1], ACT.Sqrt, bias=t["eps"][:, 0:1]).then_inc(dev_ready, 1)
        act.wait_ge(shift_ready, c + 1)
        act.wait_ge(stored, c * 16 + 16)
        for q in range(QUARTERS):
            nc.scalar.activation(y[:, q, :], res[:, q, :], ACT.Identity, bias=shift[:, q:q + 1],
                                 scale=inv[:, q:q + 1]).then_inc(y_ready, 1)
        act.wait_ge(y_ready, c * QUARTERS + QUARTERS + 1)
        act.dma_start(out[bass.ds(c * CHUNK, CHUNK), :].rearrange("(q p) n -> p q n", p=P), y[:, :, :]).then_inc(stored, 16)

    def start(act):
        act.sem_inc(stored, 16)
        act.sem_inc(y_ready, 1)

    def stores(act):
        act.wait_ge(stored, acc.shape[1] // CHUNK * 16 + 16)

    return {"vector": vector, "tensor": tensor, "scalar": scalar, "stores": stores, "start": start}


_L0, _L1 = "L0_gnn_", "L1_gnn_"


def kernel(**inputs):
    import concourse.bacc as bacc
    from concourse.bass_utils import run_bass_kernel_spmd

    a = {k: np.asarray(v) for k, v in inputs.items()}
    nodes, edges = a["x"].shape[0], a["src"].shape[0]
    NP, SUPERS = sizes(nodes, edges)
    EP = SUPERS * EDGES

    def padded(v, rows, fill=0):
        return np.concatenate([v, np.full((rows - v.shape[0],) + v.shape[1:], fill, v.dtype)])

    x, src, dst = padded(a["x"], NP), padded(a["src"], EP, nodes), padded(a["dst"], EP, nodes)
    per_layer = [a[_L1 + k] for k in ("conv_b", "bn_gamma", "bn_beta", "bn_mean", "bn_var")]
    arrays = {
        "x": x, "xT": np.ascontiguousarray(x.T), "attrT": np.ascontiguousarray(padded(a["edge_attr_64"], EP).T),
        "src_flat": src.reshape(1, EP), "dst_flat": dst.reshape(1, EP),
        "src_cols": np.ascontiguousarray(src.reshape(-1, P).T), "dst_cols": np.ascontiguousarray(dst.reshape(-1, P).T),
        "first": np.ascontiguousarray(dst.reshape(SUPERS, EDGES)[:, 0]).reshape(1, SUPERS),
        "cols": np.ascontiguousarray(np.concatenate([a[_L0 + "b2a"][None], a[_L1 + "lin0_b"][None], *per_layer]).T),
        "lin0_w": a[_L1 + "lin0_w"], "lin1_w": a[_L1 + "lin1_w"], "lin1_b": a[_L1 + "lin1_b"], "conv_w": a[_L1 + "conv_w"],
        **{k: a[_L0 + k] for k in ("W1a", "b1a", "W1b", "b1b", "W2a", "W2b", "b2b")},
    }
    arrays = {f"in_{k}": v for k, v in arrays.items()}
    nc = bacc.Bacc("TRN2", target_bir_lowering=False, num_devices=1)
    ins = {k[3:]: nc.dram_tensor(k, v.shape, mybir.dt.from_np(v.dtype), kind="ExternalInput").ap() for k, v in arrays.items()}
    out = nc.dram_tensor("out", (NP, FEATURES), F32, kind="ExternalOutput").ap()
    build(nc, nodes, edges, ins, out)
    r = run_bass_kernel_spmd(nc, [arrays], core_ids=[0])
    return r.results[0]["out"][:nodes]
```
